# Optimizing a Trainium2 kernel written in Bass

```python
import numpy as np
import jax
import jax.numpy as jnp

def _softmax(x, axis=-1):
    return jax.nn.softmax(x, axis=axis)

def _gelu(x):
    return jax.nn.gelu(x, approximate=True)

def _silu(x):
    return jax.nn.silu(x)

def _sigmoid(x):
    return jax.nn.sigmoid(x)

def _layernorm(x, axis=-1, eps=1e-05):
    m = jnp.mean(x, axis=axis, keepdims=True)
    v = jnp.var(x, axis=axis, keepdims=True)
    return (x - m) / jnp.sqrt(v + eps)

def _scatter_add(tgt, idx, src, axis=0):
    return tgt.at[idx].add(src)

def _segment_sum(src, seg, n):
    return jax.ops.segment_sum(src, seg, n)
kernel_name = 'mk_gnn_preln_d2_gnn_r8_d794e8'

def setup_inputs(seed: int=0):
    np.random.seed(seed)
    _w = jnp.asarray

    def _rec_inputs():
        import jax
        import jax.numpy as jnp
        _gk = jax.random.key(seed)
        x = -0.000202 + 1 * jax.random.normal(jax.random.fold_in(_gk, 1), (6250, 128), jnp.float32)
        _s = jax.random.randint(jax.random.fold_in(_gk, 2), (100000,), 0, 6250, jnp.int32)
        _d = jax.random.randint(jax.random.fold_in(_gk, 3), (100000,), 0, 6250, jnp.int32)
        _loop = jnp.arange(6250, dtype=jnp.int32)
        src = jnp.concatenate([_s, _d, _loop])
        dst = jnp.concatenate([_d, _s, _loop])
        _o = jnp.argsort(dst, stable=True)
        src = src[_o]
        dst = dst[_o]
        edge_attr_64 = 0.000189758 + 1.00013 * jax.random.normal(jax.random.fold_in(_gk, 11), (206250, 64), jnp.float32)
        return (x, src, dst, edge_attr_64)
    x, src, dst, edge_attr_64 = _rec_inputs()

    def _L0_gnn_setup():
        import jax, jax.numpy as jnp
        import numpy as np
        N, E, IN_DIM, OUT_DIM, EDGE_DIM, HEADS = (6250, 100000, 128, 128, 64, 4)
        C = OUT_DIM // HEADS
        NEG_SLOPE = 0.2
        EPS = 1e-05

        def _gatv2_graphnorm(x, edge_index, edge_attr, Wl, bl, Wr, br, We, att, bias_out, gn_weight, gn_bias, gn_mean_scale):
            src, dst = (edge_index[0], edge_index[1])
            n = x.shape[0]
            deg = jax.ops.segment_sum(jnp.ones((edge_attr.shape[0],), x.dtype), dst, num_segments=n)
            loop_attr = jax.ops.segment_sum(edge_attr, dst, num_segments=n) / jnp.maximum(deg, 1.0)[:, None]
            loop = jnp.arange(n, dtype=src.dtype)
            src_a = jnp.concatenate([src, loop])
            dst_a = jnp.concatenate([dst, loop])
            eattr = jnp.concatenate([edge_attr, loop_attr], axis=0)
            xl = (x @ Wl + bl).reshape(n, HEADS, C)
            xr = (x @ Wr + br).reshape(n, HEADS, C)
            ee = (eattr @ We).reshape(-1, HEADS, C)
            msg = xl[src_a] + xr[dst_a] + ee
            score = jnp.einsum('ehc,hc->eh', jax.nn.leaky_relu(msg, NEG_SLOPE), att)
            smax = jax.ops.segment_max(score, dst_a, num_segments=n)
            ex = jnp.exp(score - smax[dst_a])
            denom = jax.ops.segment_sum(ex, dst_a, num_segments=n)
            alpha = ex / (denom[dst_a] + 1e-16)
            out = jax.ops.segment_sum(alpha[:, :, None] * xl[src_a], dst_a, num_segments=n)
            out = out.reshape(n, HEADS * C) + bias_out
            mean = out.mean(axis=0)
            o = out - mean * gn_mean_scale
            var = (o * o).mean(axis=0)
            out = gn_weight * o / jnp.sqrt(var + EPS) + gn_bias
            return jax.nn.relu(out)
        key = jax.random.key(seed)
        ks = jax.random.split(key, 12)
        x = jax.random.normal(ks[0], (N, IN_DIM), dtype=jnp.float32)
        edge_index = jax.random.randint(ks[1], (2, E), 0, N, dtype=jnp.int64)
        edge_attr = jax.random.normal(ks[2], (E, EDGE_DIM), dtype=jnp.float32)
        s = 0.05
        Wl = jax.random.normal(ks[3], (IN_DIM, HEADS * C), dtype=jnp.float32) * s
        bl = jnp.zeros((HEADS * C,), dtype=jnp.float32)
        Wr = jax.random.normal(ks[4], (IN_DIM, HEADS * C), dtype=jnp.float32) * s
        br = jnp.zeros((HEADS * C,), dtype=jnp.float32)
        We = jax.random.normal(ks[5], (EDGE_DIM, HEADS * C), dtype=jnp.float32) * s
        att = jax.random.normal(ks[6], (HEADS, C), dtype=jnp.float32) * s
        bias_out = jnp.zeros((HEADS * C,), dtype=jnp.float32)
        gn_weight = jnp.ones((OUT_DIM,), dtype=jnp.float32)
        gn_bias = jnp.zeros((OUT_DIM,), dtype=jnp.float32)
        gn_mean_scale = jnp.ones((OUT_DIM,), dtype=jnp.float32)
        return dict(x=x, edge_index=edge_index, edge_attr=edge_attr, Wl=Wl, bl=bl, Wr=Wr, br=br, We=We, att=att, bias_out=bias_out, gn_weight=gn_weight, gn_bias=gn_bias, gn_mean_scale=gn_mean_scale)
    _L0_gnn_all = _L0_gnn_setup()
    _L0_gnn_in = {k: v for k, v in _L0_gnn_all.items() if k in ('Wl', 'bl', 'Wr', 'br', 'We', 'att', 'bias_out', 'gn_weight', 'gn_bias', 'gn_mean_scale')}
    del _L0_gnn_all

    def _L1_gnn_setup():
        import jax, jax.numpy as jnp
        import numpy as np
        HEADS, OUT_C = (8, 16)
        NEG_SLOPE = 0.2
        key = jax.random.key(seed)
        ks = jax.random.split(key, 6)
        N, E, IN = (12500, 200000, 128)
        x = jax.random.normal(ks[0], (N, IN), jnp.float32)
        edge_index = jax.random.randint(ks[1], (2, E), 0, N, dtype=jnp.int32)
        W = jax.random.normal(ks[2], (IN, HEADS * OUT_C), jnp.float32) / np.float32(np.sqrt(IN))
        att_src = jax.random.normal(ks[3], (HEADS, OUT_C), jnp.float32) * 0.1
        att_dst = jax.random.normal(ks[4], (HEADS, OUT_C), jnp.float32) * 0.1
        bias = jax.random.normal(ks[5], (HEADS * OUT_C,), jnp.float32) * 0.01
        return {'x': x, 'edge_index': edge_index, 'W': W, 'att_src': att_src, 'att_dst': att_dst, 'bias': bias}
    _L1_gnn_all = _L1_gnn_setup()
    _L1_gnn_in = {k: v for k, v in _L1_gnn_all.items() if k in ('W', 'att_src', 'att_dst', 'bias')}
    del _L1_gnn_all
    return {'x': x, 'src': src, 'dst': dst, 'edge_attr_64': edge_attr_64, 'L0_gnn_Wl': _L0_gnn_in['Wl'], 'L0_gnn_bl': _L0_gnn_in['bl'], 'L0_gnn_Wr': _L0_gnn_in['Wr'], 'L0_gnn_br': _L0_gnn_in['br'], 'L0_gnn_We': _L0_gnn_in['We'], 'L0_gnn_att': _L0_gnn_in['att'], 'L0_gnn_bias_out': _L0_gnn_in['bias_out'], 'L0_gnn_gn_weight': _L0_gnn_in['gn_weight'], 'L0_gnn_gn_bias': _L0_gnn_in['gn_bias'], 'L0_gnn_gn_mean_scale': _L0_gnn_in['gn_mean_scale'], 'L1_gnn_W': _L1_gnn_in['W'], 'L1_gnn_att_src': _L1_gnn_in['att_src'], 'L1_gnn_att_dst': _L1_gnn_in['att_dst'], 'L1_gnn_bias': _L1_gnn_in['bias']}

def reference(x, src, dst, edge_attr_64, L0_gnn_Wl, L0_gnn_bl, L0_gnn_Wr, L0_gnn_br, L0_gnn_We, L0_gnn_att, L0_gnn_bias_out, L0_gnn_gn_weight, L0_gnn_gn_bias, L0_gnn_gn_mean_scale, L1_gnn_W, L1_gnn_att_src, L1_gnn_att_dst, L1_gnn_bias):
    import jax
    import jax.numpy as jnp

    def _L0_gnn_ref(x, edge_index, edge_attr, Wl, bl, Wr, br, We, att, bias_out, gn_weight, gn_bias, gn_mean_scale):
        import jax, jax.numpy as jnp
        import numpy as np
        N, E, IN_DIM, OUT_DIM, EDGE_DIM, HEADS = (6250, 100000, 128, 128, 64, 4)
        C = OUT_DIM // HEADS
        NEG_SLOPE = 0.2
        EPS = 1e-05

        def _gatv2_graphnorm(x, edge_index, edge_attr, Wl, bl, Wr, br, We, att, bias_out, gn_weight, gn_bias, gn_mean_scale):
            src, dst = (edge_index[0], edge_index[1])
            n = x.shape[0]
            deg = jax.ops.segment_sum(jnp.ones((edge_attr.shape[0],), x.dtype), dst, num_segments=n)
            loop_attr = jax.ops.segment_sum(edge_attr, dst, num_segments=n) / jnp.maximum(deg, 1.0)[:, None]
            loop = jnp.arange(n, dtype=src.dtype)
            src_a = jnp.concatenate([src, loop])
            dst_a = jnp.concatenate([dst, loop])
            eattr = jnp.concatenate([edge_attr, loop_attr], axis=0)
            xl = (x @ Wl + bl).reshape(n, HEADS, C)
            xr = (x @ Wr + br).reshape(n, HEADS, C)
            ee = (eattr @ We).reshape(-1, HEADS, C)
            msg = xl[src_a] + xr[dst_a] + ee
            score = jnp.einsum('ehc,hc->eh', jax.nn.leaky_relu(msg, NEG_SLOPE), att)
            smax = jax.ops.segment_max(score, dst_a, num_segments=n)
            ex = jnp.exp(score - smax[dst_a])
            denom = jax.ops.segment_sum(ex, dst_a, num_segments=n)
            alpha = ex / (denom[dst_a] + 1e-16)
            out = jax.ops.segment_sum(alpha[:, :, None] * xl[src_a], dst_a, num_segments=n)
            out = out.reshape(n, HEADS * C) + bias_out
            mean = out.mean(axis=0)
            o = out - mean * gn_mean_scale
            var = (o * o).mean(axis=0)
            out = gn_weight * o / jnp.sqrt(var + EPS) + gn_bias
            return jax.nn.relu(out)
        return _gatv2_graphnorm(x, edge_index, edge_attr, Wl, bl, Wr, br, We, att, bias_out, gn_weight, gn_bias, gn_mean_scale)

    def _L1_gnn_ref(x, edge_index, W, att_src, att_dst, bias):
        import jax, jax.numpy as jnp
        import numpy as np
        HEADS, OUT_C = (8, 16)
        NEG_SLOPE = 0.2
        N = x.shape[0]
        xw = (x @ W).reshape(N, HEADS, OUT_C)
        loops = jnp.arange(N, dtype=edge_index.dtype)
        src = jnp.concatenate([edge_index[0], loops])
        dst = jnp.concatenate([edge_index[1], loops])
        a_s = jnp.einsum('nhc,hc->nh', xw, att_src)
        a_d = jnp.einsum('nhc,hc->nh', xw, att_dst)
        e = a_s[src] + a_d[dst]
        e = jnp.where(e > 0, e, NEG_SLOPE * e)
        emax = jax.ops.segment_max(e, dst, num_segments=N)
        p = jnp.exp(e - emax[dst])
        denom = jax.ops.segment_sum(p, dst, num_segments=N)
        alpha = p / (denom[dst] + 1e-16)
        out = jax.ops.segment_sum(xw[src] * alpha[:, :, None], dst, num_segments=N)
        out = out.reshape(N, HEADS * OUT_C) + bias
        return jax.nn.relu(out)
    edge_index = jnp.stack([src, dst])
    h = jnp.maximum(_layernorm(x, axis=-1), 0.0)
    x = x + _L0_gnn_ref(h, edge_index, edge_attr_64, L0_gnn_Wl, L0_gnn_bl, L0_gnn_Wr, L0_gnn_br, L0_gnn_We, L0_gnn_att, L0_gnn_bias_out, L0_gnn_gn_weight, L0_gnn_gn_bias, L0_gnn_gn_mean_scale)
    h = jnp.maximum(_layernorm(x, axis=-1), 0.0)
    x = x + _L1_gnn_ref(h, edge_index, L1_gnn_W, L1_gnn_att_src, L1_gnn_att_dst, L1_gnn_bias)
    return x

_drawn_inputs = setup_inputs


def setup_inputs(seed=0):
    import zlib

    import numpy as np

    out = dict(_drawn_inputs(seed))
    spreads = {'L0_gnn_bl': (0.0, 0.1),
     'L0_gnn_br': (0.0, 0.8),
     'L0_gnn_bias_out': (0.0, 0.1),
     'L0_gnn_gn_weight': (1.0, 0.2),
     'L0_gnn_gn_bias': (0.0, 0.1),
     'L0_gnn_gn_mean_scale': (1.0, 0.2)}
    factors = {'L0_gnn_Wr': 3.274, 'L1_gnn_att_src': 3.029, 'L1_gnn_att_dst': 8.0, 'L1_gnn_bias': 8.0}
    for name, (base, spread) in spreads.items():
        noise = np.random.default_rng([zlib.crc32(name.encode()), seed]).standard_normal(out[name].shape)
        drawn = base * np.exp(spread * noise) if base else spread * noise
        out[name] = jnp.asarray(drawn.astype(out[name].dtype))
    for name, factor in factors.items():
        out[name] = (out[name] * factor).astype(out[name].dtype)
    return out
```

```python
from contextlib import ExitStack

import concourse.bass as bass
from concourse import mybir

F32 = mybir.dt.float32
I32 = mybir.dt.int32
ALU = mybir.AluOpType
ACT = mybir.ActivationFunctionType
AX = mybir.AxisListType.X
DVE, PE, SPE = mybir.EngineType.DVE, mybir.EngineType.PE, mybir.EngineType.SP

P = 128
NODES = 6250
EDGES = 206250
D = 128
DE = 64
WINDOWS = -(-NODES // P)
NP = WINDOWS * P
LASTW = NODES - (WINDOWS - 1) * P
TILES = -(-EDGES // P)
TP = TILES + 1
G = 15
GS = 3
NG = G // GS
RING = 3
STEPS = -(-(TILES + WINDOWS - 1) // (G * RING)) * G * RING
BATCHES = STEPS // G
ROUNDS = BATCHES // RING
KC = -(-(STEPS + 1) // P)
KP = KC * P
NOWHERE = 1 << 14
BIG = 1e30
HEADS = 8
SLOPE = 0.2
EPS = 1e-5
CH = 7
CHUNKS = WINDOWS // CH
assert CHUNKS * CH == WINDOWS


class Names:
    pass


def bc(ap, *shape):
    return ap.to_broadcast(list(shape))


def settle(eng):
    eng.nop(nofuse=True)


class Kit:

    def __init__(self, nc, ctx):
        self.nc, self.ctx, self.used = nc, ctx, {}

    def own(self, name):
        self.used[name] = self.used.get(name, 0) + 1
        return name if self.used[name] == 1 else f"{name}_{self.used[name]}"

    def sb(self, name, shape, dt=F32, ctx=None):
        return (ctx or self.ctx).enter_context(self.nc.sbuf_tensor(self.own(name), shape, dt))

    def ps(self, name, shape, dt=F32, ctx=None):
        return (ctx or self.ctx).enter_context(self.nc.psum_tensor(self.own(name), shape, dt))

    def sem(self, name, ctx=None):
        return self.ctx.enter_context(self.nc.semaphore(self.own(name)))

    def dram(self, name, shape, dt=F32):
        return self.nc.dram_tensor(name, shape, dt).ap()


def constants(nc, kit, t):
    made = kit.sem("c_made")
    sel = kit.sem("c_sel")
    with nc.Block() as block:
        @block.gpsimd
        def _(pool):
            pool.memset(t.ident[:, :], 0.0).then_inc(made, 1)
            pool.memset(t.ones[:, :], 1.0).then_inc(made, 1)
            pool.iota(t.iota_i[:, :], [[1, P]], base=0, channel_multiplier=0).then_inc(made, 1)
            pool.wait_ge(made, 3)
            pool.affine_select(out=t.ident[:, :], in_=t.ident[:, :], compare_op=ALU.not_equal, fill=1.0,
                               base=0, pattern=[[-1, P]], channel_multiplier=1).then_inc(sel, 1)
            pool.tensor_copy(t.iota[:, :], t.iota_i[:, :]).then_inc(sel, 1)
            pool.wait_ge(sel, 2)


def step_tables(nc, kit, io, t):
    with ExitStack() as ctx:
        def sb(name, shape, dt=F32):
            return kit.sb(name, shape, dt, ctx)

        lasts_i = sb("lasts_i", [P, TILES], I32)
        lastw = sb("lastw", [P, TILES], I32)
        tile_no = sb("tile_no", [P, TILES], I32)
        ends_at = sb("ends_at", [P, TILES])
        before = sb("before", [P, TILES])
        step_no_i = sb("step_no_i", [P, KC], I32)
        step_no = sb("step_no", [P, KC])
        tile_f = sb("tile_f", [P, KC])
        tile_i = sb("tile_i", [P, KC], I32)
        win_f = sb("win_f", [P, KC])
        win_i = sb("win_i", [P, KC], I32)
        srcr = sb("srcr", [P, KC, P], I32)
        dstr = sb("dstr", [P, KC, P], I32)
        srcf = sb("srcf", [P, KC, P])
        dstf = sb("dstf", [P, KC, P])
        rel = sb("rel", [P, KC, P])
        inw = sb("inw", [P, KC, P])
        key = sb("key", [P, KC, P])
        prev = sb("prev", [P, KC, P])
        reset = sb("reset", [P, KC, P])
        after = sb("after", [P, KC, P])
        last = sb("last", [P, KC, P])
        tail = sb("tail", [1, P])
        sums = sb("sums", [P, 2, KC])
        turned = [kit.ps(f"turned{i}", [P, 512], F32, ctx) for i in range(2)]
        loaded, counted = kit.sem("t_loaded"), kit.sem("t_counted")
        numbered, vec = kit.sem("t_numbered"), kit.sem("t_vec")
        rows_src, rows_dst = kit.sem("t_rows_src"), kit.sem("t_rows_dst")
        keys_out, keys_in = kit.sem("t_keys_out"), kit.sem("t_keys_in")
        resets_out, resets_in = kit.sem("t_resets_out"), kit.sem("t_resets_in")
        rows_out, spread_out = kit.sem("t_rows_out"), kit.sem("t_spread_out")
        tabs_out, tabs_in = kit.sem("t_tabs_out"), kit.sem("t_tabs_in")
        turned_ready, turned_used = kit.sem("t_turned_ready"), kit.sem("t_turned_used")
        FOUND, KEYED, RESET, SUMMED, FLAGGED = KC + 9, KC + 19, KC + 21, KC + 23, KC + 24
        block = ctx.enter_context(nc.Block())

        @block.gpsimd
        def _(pool):
            pool.iota(tile_no[:, :], [[1, TILES]], base=0, channel_multiplier=0).then_inc(numbered, 1)
            pool.iota(step_no_i[:, :], [[P, KC]], base=0, channel_multiplier=1).then_inc(numbered, 1)
            pool.wait_ge(vec, FOUND)
            for c in range(KC):
                pool.indirect_dma_start(srcr[:, c, :], None, io.src_rows,
                                        bass.IndirectOffsetOnAxis(tile_i[:, c:c + 1], 0)).then_inc(rows_src, 16)
                pool.indirect_dma_start(dstr[:, c, :], None, io.dst_rows,
                                        bass.IndirectOffsetOnAxis(tile_i[:, c:c + 1], 0)).then_inc(rows_dst, 16)

        @block.sync
        def _(sp):
            sp.dma_start(lasts_i[:, :], bc(io.dst_lasts, P, TILES)).then_inc(loaded, 16)
            with nc.allow_non_contiguous_dma(reason="small tables"):
                sp.wait_ge(vec, FOUND)
                sp.dma_start(io.tab_i[0, :].rearrange("(c p) -> p c", p=P), tile_i[:, :]).then_inc(tabs_out, 16)
                sp.dma_start(io.tab_i[1, :].rearrange("(c p) -> p c", p=P), win_i[:, :]).then_inc(tabs_out, 16)
                sp.wait_ge(vec, KEYED)
                sp.dma_start(io.keys[1:1 + KP * P].rearrange("(c p e) -> p c e", p=P, e=P), key[:, :, :]).then_inc(keys_out, 16)
                sp.dma_start(io.keys[0:1].rearrange("(a b) -> a b", a=1), tail[0:1, 0:1]).then_inc(keys_out, 16)
                sp.wait_ge(keys_out, 32)
                sp.dma_start(prev[:, :, :], io.keys[0:KP * P].rearrange("(c p e) -> p c e", p=P, e=P)).then_inc(keys_in, 16)
                sp.wait_ge(vec, RESET)
                sp.dma_start(io.resets[0:KP * P].rearrange("(c p e) -> p c e", p=P, e=P), reset[:, :, :]).then_inc(resets_out, 16)
                sp.dma_start(io.resets[KP * P:KP * P + P].rearrange("(a b) -> a b", a=1), tail[0:1, :]).then_inc(resets_out, 16)
                sp.wait_ge(resets_out, 32)
                sp.dma_start(after[:, :, :], io.resets[1:1 + KP * P].rearrange("(c p e) -> p c e", p=P, e=P)).then_inc(resets_in, 16)
                sp.wait_ge(resets_in, 16)
                rows = io.resets_r.rearrange("(c p) e -> p c e", p=P)
                sp.dma_start(rows[:, :, 0:P], reset[:, :, :]).then_inc(rows_out, 16)
                sp.dma_start(rows[:, :, P:P + 1], after[:, :, P - 1:P]).then_inc(rows_out, 16)
                sp.wait_ge(vec, SUMMED)
                sp.dma_start(io.tab_f[0, :].rearrange("(c p) -> p c", p=P), sums[:, 0, :]).then_inc(tabs_out, 16)
                sp.dma_start(io.tab_f[1, :].rearrange("(c p) -> p c", p=P), sums[:, 1, :]).then_inc(tabs_out, 16)
            sp.wait_ge(tabs_out, 64)
            sp.dma_start(t.tiles[0:1, :], io.tab_i[0:1, :]).then_inc(tabs_in, 16)
            sp.dma_start(t.wins[0:1, :], io.tab_i[1:2, :]).then_inc(tabs_in, 16)
            sp.dma_start(t.rsum_f[0:1, :], io.tab_f[0:1, :]).then_inc(tabs_in, 16)
            sp.dma_start(t.rsum_b[0:1, :], io.tab_f[1:2, :]).then_inc(tabs_in, 16)
            sp.wait_ge(tabs_in, 64)
            sp.wait_ge(rows_out, 32)
            for h in range(HEADS):
                sp.dma_start(io.resets_h[:, h, :, :], io.resets_r[0:STEPS, :].rearrange("(b g) e -> b g e", g=G)).then_inc(spread_out, 16)
            sp.wait_ge(spread_out, 16 * HEADS)

        @block.vector
        def _(dve):
            n = [0]

            def step(ins, wait=True):
                n[0] += 1
                ins.then_inc(vec, 1)
                if wait:
                    dve.wait_ge(vec, n[0])

            dve.wait_ge(loaded, 16)
            dve.wait_ge(numbered, 2)
            step(dve.tensor_scalar(lastw[:, :], lasts_i[:, :], 7, None, ALU.arith_shift_right), False)
            step(dve.tensor_copy(step_no[:, :], step_no_i[:, :]))
            step(dve.tensor_scalar(ends_at[:, :], lastw[:, :], float(WINDOWS - 1), 0.0, ALU.min, ALU.max))
            step(dve.tensor_tensor(ends_at[:, :], ends_at[:, :], tile_no[:, :], ALU.add))
            for c in range(KC):
                step(dve.tensor_scalar(before[:, :], ends_at[:, :], step_no[:, c:c + 1], 0.0, ALU.is_lt, ALU.add,
                                       accum_out=tile_f[:, c:c + 1]))
            step(dve.tensor_tensor(win_f[:, :], step_no[:, :], tile_f[:, :], ALU.subtract))
            step(dve.tensor_scalar(win_f[:, :], win_f[:, :], float(WINDOWS - 1), 0.0, ALU.min, ALU.max))
            step(dve.tensor_copy(tile_i[:, :], tile_f[:, :]), False)
            step(dve.tensor_copy(win_i[:, :], win_f[:, :]), False)
            step(dve.memset(tail[:, :], -BIG))
            assert n[0] == FOUND
            dve.wait_ge(rows_src, 16 * KC)
            step(dve.tensor_copy(srcf[:, :, :], srcr[:, :, :]), False)
            dve.wait_ge(rows_dst, 16 * KC)
            step(dve.tensor_copy(dstf[:, :, :], dstr[:, :, :]))
            step(dve.scalar_tensor_tensor(rel[:, :, :], bc(win_f[:, :].unsqueeze(2), P, KC, P), -float(P), dstf[:, :, :],
                                          ALU.mult, ALU.add))
            step(dve.tensor_scalar(inw[:, :, :], rel[:, :, :], 0.0, None, ALU.is_ge), False)
            step(dve.tensor_scalar(prev[:, :, :], rel[:, :, :], float(P), None, ALU.is_lt))
            step(dve.tensor_tensor(inw[:, :, :], inw[:, :, :], prev[:, :, :], ALU.mult))
            one_more = bc(step_no[:, :].unsqueeze(2), P, KC, P)
            step(dve.scalar_tensor_tensor(key[:, :, :], one_more, 1.0, dstf[:, :, :], ALU.add, ALU.add))
            step(dve.tensor_tensor(key[:, :, :], key[:, :, :], inw[:, :, :], ALU.mult))
            step(dve.scalar_tensor_tensor(reset[:, :, :], one_more, 1.0, key[:, :, :], ALU.add, ALU.subtract))
            n_key = n[0]
            step(dve.tensor_scalar(key[:, :, :], reset[:, :, :], -1.0, None, ALU.mult))
            dve.wait_ge(keys_in, 16)
            step(dve.tensor_tensor(reset[:, :, :], key[:, :, :], prev[:, :, :], ALU.not_equal))
            step(dve.tensor_scalar(reset[:, :, :], reset[:, :, :], -BIG, None, ALU.mult))
            dve.wait_ge(resets_in, 16)
            step(dve.tensor_reduce(sums[:, 0, :], reset[:, :, :], AX, ALU.add), False)
            step(dve.tensor_reduce(sums[:, 1, :], after[:, :, :], AX, ALU.add))
            step(dve.tensor_scalar(last[:, :, :], after[:, :, :], 0.0, None, ALU.is_lt))
            assert (n_key + 1, n_key + 3, n_key + 5, n_key + 6) == (KEYED, RESET, SUMMED, FLAGGED), (n_key, KC)
            for i in range(3 * KC):
                c, what = divmod(i, 3)
                dve.wait_ge(turned_ready, i + 1)
                out = (t.src_k, t.rel_k, t.last_k)[what]
                ins = dve.tensor_copy(out[:, c * P:(c + 1) * P], turned[i % 2][:, 0:P])
                ins.then_inc(turned_used, 1)
            dve.wait_ge(turned_used, 3 * KC)

        @block.tensor
        def _(pe):
            pe.wait_ge(vec, FLAGGED)
            for i in range(3 * KC):
                c, what = divmod(i, 3)
                if i >= 2:
                    pe.wait_ge(turned_used, i - 1)
                pe.transpose(turned[i % 2][:, 0:P], (srcf, rel, last)[what][:, c, :], t.ident[:, :]).then_inc(turned_ready, 1)
def load_weights(nc, kit, io, t, lay):
    H, C, R = lay.H, lay.C, lay.R
    with ExitStack() as ctx:
        def sb(name, shape):
            return kit.sb(f"{lay.n}_{name}", shape, F32, ctx)

        mats = lay.mats
        prod = sb("prod", [P, D])
        raw = sb("raw", [P, D])
        att = sb("att", [P, len(mats), D])
        loaded, vec = kit.sem(f"{lay.n}w_loaded"), kit.sem(f"{lay.n}w_vec")
        loads = sum(3 if b is not None else 2 for _, b, _, _, _, _ in mats)
        block = ctx.enter_context(nc.Block())

        @block.sync
        def _(sp):
            for i, (w, b, rows, a, to, keep) in enumerate(mats):
                dst = to[0:rows, :, 0:C] if keep else raw[0:rows, :].rearrange("p (h c) -> p h c", h=H)
                with nc.allow_non_contiguous_dma(reason="weights, once"):
                    sp.dma_start(dst, w.rearrange("k (h c) -> k h c", h=H)).then_inc(loaded, 16)
                    sp.dma_start(att[:, i, :], bc(a, P, D)).then_inc(loaded, 16)
                    if b is not None:
                        sp.dma_start(lay.bias[0:1, i, :, 0:C], b.rearrange("o (h c) -> o h c", h=H)).then_inc(loaded, 16)

        @block.vector
        def _(dve):
            n = [0]

            def step(ins):
                n[0] += 1
                ins.then_inc(vec, 1)
                dve.wait_ge(vec, n[0])

            dve.wait_ge(loaded, 16 * loads)
            for i, (w, b, rows, a, to, keep) in enumerate(mats):
                src = to[0:rows, :, 0:C] if keep else raw[0:rows, :].rearrange("p (h c) -> p h c", h=H)
                col = to[0:rows, :, C] if keep else to[0:rows, :, 0]
                last = bc(col.unsqueeze(2), rows, H, 1)
                for src, rows, last in [(src, rows, last)] + (
                        [(lay.bias[0:1, i, :, 0:C], 1, lay.bias[0:1, i, :, C:C + 1])] if b is not None else []):
                    pr = prod[0:rows, :].rearrange("p (h c) -> p h c", h=H)
                    step(dve.tensor_tensor(pr, src, att[0:rows, i, :].rearrange("p (h c) -> p h c", h=H), ALU.mult))
                    step(dve.tensor_reduce(last, pr, AX, ALU.add))
                    if lay.lin != 1.0:
                        step(dve.tensor_scalar(last, last, lay.lin, None, ALU.mult))
            if lay.edge:
                step(dve.tensor_scalar(t.att08[:, :], att[:, 0, :], 1.0 - SLOPE, None, ALU.mult))


def project(nc, kit, io, t, lay):
    RW, DW = lay.RW, lay.DW
    BW = RW + DW
    n = lay.n + "p_"
    with ExitStack() as ctx:
        def sb(name, shape):
            return kit.sb(n + name, shape, F32, ctx)

        def sem(name):
            return kit.sem(n + name, ctx)

        x = sb("x", [P, CH, D])
        xc = sb("xc", [P, CH, D])
        sq = sb("sq", [P, CH, D])
        xn = sb("xn", [P, CH, D])
        hT = sb("hT", [P, CH * P])
        mean = sb("mean", [P, CH])
        var = sb("var", [P, CH])
        std = sb("std", [P, CH])
        stage = sb("stage", [P, CH, RW])
        turned = [kit.ps(n + f"turned{i}", [P, 512], F32, ctx) for i in range(2)]
        out = [kit.ps(n + f"out{i}", [P, 512], F32, ctx) for i in range(2)]
        x_in, stored = sem("x_in"), sem("stored")
        vec, squared, rooted = sem("vec"), sem("squared"), sem("rooted")
        h_turned, h_ready = sem("h_turned"), sem("h_ready")
        made = [sem("made_even"), sem("made_odd")]
        taken = [sem("taken_even"), sem("taken_odd")]
        MADE = [(CH + 1) // 2, CH // 2]
        CENTERED, SPREAD, SCALED, NV = 3, 5, 7, 7
        block = ctx.enter_context(nc.Block())

        @block.sync
        def _(sp):
            def chunk(r, first=False):
                if not first:
                    sp.wait_ge(vec, (r - 1) * NV + CENTERED)
                    settle(sp)
                sp.dma_start(x[:, :, :], lay.x_in[bass.ds(r * CH * P, CH * P), :].rearrange("(w p) d -> p w d", p=P)).then_inc(x_in, 16)
                for e in range(2):
                    sp.wait_ge(taken[e], (r + 1) * MADE[e])
                    settle(sp)
                sp.dma_start(lay.table[bass.ds(r * CH * P, CH * P), :].rearrange("(w p) d -> p w d", p=P), stage[:, :, :]).then_inc(stored, 16)

            chunk(0, True)
            with sp.Fori(1, CHUNKS) as r:
                chunk(r)
            sp.wait_ge(stored, 16 * CHUNKS)

        def take(eng, copy, parity, r, first):
            if not first:
                eng.wait_ge(stored, 16 * r)
            for i, w in enumerate(range(parity, CH, 2)):
                eng.wait_ge(made[parity], r * MADE[parity] + i + 1)
                copy(stage[:, w, :], out[parity][:, 0:RW])
                copy(lay.dst_table[:, bass.ds((r * CH + w) * DW, DW)], out[parity][:, RW:BW]).then_inc(taken[parity], 1)

        @block.vector
        def _(dve):
            def chunk(r, first=False):
                k = [0]

                def step(ins, wait=True):
                    k[0] += 1
                    ins.then_inc(vec, 1)
                    if wait:
                        dve.wait_ge(vec, r * NV + k[0])

                def wide(a):
                    return bc(a[:, :].unsqueeze(2), P, CH, D)

                dve.wait_ge(x_in, 16 * (r + 1))
                step(dve.tensor_reduce(mean[:, :], x[:, :, :], AX, ALU.add))
                step(dve.tensor_scalar(mean[:, :], mean[:, :], 1.0 / D, None, ALU.mult))
                step(dve.tensor_tensor(xc[:, :, :], x[:, :, :], wide(mean), ALU.subtract), False)
                dve.wait_ge(squared, r + 1)
                step(dve.tensor_reduce(var[:, :], sq[:, :, :], AX, ALU.add))
                step(dve.tensor_scalar(var[:, :], var[:, :], 1.0 / D, EPS, ALU.mult, ALU.add), False)
                dve.wait_ge(rooted, r + 1)
                step(dve.reciprocal(std[:, :], std[:, :]))
                step(dve.tensor_tensor(xn[:, :, :], xc[:, :, :], wide(std), ALU.mult), False)
                take(dve, dve.tensor_copy, 1, r, first)

            chunk(0, True)
            with dve.Fori(1, CHUNKS) as r:
                chunk(r)

        @block.scalar
        def _(act):
            def chunk(r, first=False):
                act.wait_ge(vec, r * NV + CENTERED)
                act.activation(sq[:, :, :], xc[:, :, :], ACT.Square).then_inc(squared, 1)
                act.wait_ge(vec, r * NV + SPREAD)
                act.activation(std[:, :], var[:, :], ACT.Sqrt).then_inc(rooted, 1)
                for half in range(2):
                    act.wait_ge(h_turned, 2 * r + half + 1)
                    w = CH // 2 + 1 if half == 0 else CH // 2
                    at = half * (CH // 2 + 1)
                    act.activation(hT[:, at * P:(at + w) * P], turned[half][:, 0:w * P], ACT.Relu).then_inc(h_ready, 1)
                take(act, lambda o, i: act.activation(o, i, ACT.Copy), 0, r, first)

            chunk(0, True)
            with act.Fori(1, CHUNKS) as r:
                chunk(r)

        @block.tensor
        def _(pe):
            def chunk(r, first=False):
                pe.wait_ge(vec, r * NV + SCALED)
                for w in range(CH):
                    half, at = divmod(w, CH // 2 + 1)
                    ins = pe.transpose(turned[half][:, at * P:(at + 1) * P], xn[:, w, :], t.ident[:, :])
                    if w in (CH // 2, CH - 1):
                        ins.then_inc(h_turned, 1)
                for w in range(CH):
                    half, e = w // (CH // 2 + 1), w % 2
                    if w in (0, CH // 2 + 1):
                        pe.wait_ge(h_ready, 2 * r + half + 1)
                    if w >= 2:
                        pe.wait_ge(taken[e], r * MADE[e] + w // 2)
                    elif not first:
                        pe.wait_ge(taken[e], r * MADE[e])
                    lhs = hT[:, w * P:(w + 1) * P]
                    if lay.bias is not None:
                        pe.matmul(out[e][:, 0:BW], t.ones[0:1, :], lay.bias[0:1, :, :, :].rearrange("p a h c -> p (a h c)"),
                                  start=True, stop=False)
                    pe.matmul(out[e][:, 0:BW], lhs, lay.wcat[:, 0:BW], start=lay.bias is None, stop=True).then_inc(made[e], 1)

            chunk(0, True)
            with pe.Fori(1, CHUNKS) as r:
                chunk(r)
class Batch:

    def __init__(self, no, slot, turn):
        self.no, self.slot, self.turn = no, slot, turn
        self.reuses = not isinstance(no, int) or no >= RING
        self.some_before = not isinstance(no, int) or no > 0

    def before(self):
        if self.slot:
            return Batch(self.no - 1, self.slot - 1, self.turn)
        return Batch(self.no - 1, RING - 1, self.turn - 1)


def gap_to(i):
    return {0: 1, 1: 3}.get(i, 2)


def edges(nc, kit, io, t, lay):
    H, C, R, RW, DW, VW = lay.H, lay.C, lay.R, lay.RW, lay.DW, lay.VW
    HG = H * G
    edge = lay.edge
    assert G % 2 == 1 and NG % 2 == 1 and HG <= P and GS * RW <= 512
    with ExitStack() as ctx:
        def sb(name, shape, dt=F32):
            return kit.sb(f"{lay.n}_{name}", shape, dt, ctx)

        def ps(name):
            return kit.ps(f"{lay.n}_{name}", [P, 512], F32, ctx)

        def sem(name):
            return kit.sem(f"{lay.n}_{name}", ctx)

        idx = [sb(f"idx{i}", [P, G], I32) for i in range(RING)]
        rel = [sb(f"rel{i}", [P, G]) for i in range(RING)]
        rows = [sb(f"rows{i}", [P, G, RW]) for i in range(RING)]
        hot = [sb(f"hot{i}", [P, G, P]) for i in range(RING)]
        val = [sb(f"val{i}", [P, G, VW]) for i in range(RING)]
        res = [sb(f"res{i}", [P, P + 1]) for i in range(RING)]
        hot0 = [sb(f"hot0_{i}", [P, 1]) for i in range(RING)]
        score = [sb(f"score{i}", [P, H, G]) for i in range(RING)]
        hotT = [sb(f"hotT{i}", [P, GS * P]) for i in range(2)]
        if edge:
            attrT = [sb(f"attrT{i}", [DE, G * P]) for i in range(RING)]
            mes = [sb(f"mes{i}", [P, GS * H, R]) for i in range(2)]
            pos = [sb(f"pos{i}", [P, GS * H, C]) for i in range(2)]
            wgt = sb("wgt", [P, GS * H, C])
            red = sb("red", [P, GS * H])
        raw = sb("raw", [P, G, H])
        fwd, bwd, top = sb("fwd", [P, P]), sb("bwd", [P, P]), sb("top", [P, P])
        chain_r = sb("chain_r", [1, 2, H, G + 1])
        chain_m = sb("chain_m", [1, 2, H, G + 1])
        chain = sb("chain", [1, 2, H, G + 1])
        before = sb("before", [1, 2, H, G])
        init = sb("init", [P, 2])
        gap = sb("gap", [1, 2, H])
        same = sb("same", [1, 1])
        fac_in, fac = sb("fac_in", [P, H]), sb("fac", [P, H])
        dif = sb("dif", [P, G, H])
        msg = [ps("msg0"), ps("msg1")]
        hotT_ps = ps("hotT_ps")
        agg = [ps("agg0"), ps("agg1")]
        mx = ps("mx")
        prob = ps("prob")
        att_ps = ps("att_ps")
        ENDS, INITS, GAPS = P, 3 * P, 3 * P + 8

        gathered = [sem(f"gathered{i}") for i in range(RING)]
        attrs_in = [sem(f"attrs_in{i}") for i in range(RING)]
        resets_in = [sem(f"resets_in{i}") for i in range(RING)]
        prepared, staged = sem("prepared"), sem("staged")
        hot_made, hot_turned, hotT_made = sem("hot_made"), sem("hot_turned"), sem("hotT_made")
        msg_made, msg_added = sem("msg_made"), sem("msg_added")
        relu_made, weighted, reduced, scored = sem("relu_made"), sem("weighted"), sem("reduced"), sem("scored")
        turned, scanned, ends_made = sem("turned"), sem("scanned"), sem("ends_made")
        chain_vec, chained, inits_made = sem("chain_vec"), sem("chained"), sem("inits_made")
        inits_taken, rescanned, top_made, top_turned = sem("inits_taken"), sem("rescanned"), sem("top_made"), sem("top_turned")
        dif_made, tops_kept, prob_made, prob_kept = sem("dif_made"), sem("tops_kept"), sem("prob_made"), sem("prob_kept")
        fac_made, rescaled = sem("fac_made"), sem("rescaled")
        val_made, agg_made, added = sem("val_made"), sem("agg_made"), sem("added")
        PREPARED = 4 + (RING if edge else 0)
        ATTR = RW + H
        block = ctx.enter_context(nc.Block())

        def run(eng, batch):
            for u in range(RING):
                b = Batch(u, u, 0)
                batch(b, b.before() if u else None)
            with eng.Fori(1, ROUNDS) as r:
                for u in range(RING):
                    b = Batch(r * RING + u, u, r)
                    batch(b, b.before())

        LAST = Batch(BATCHES - 1, (BATCHES - 1) % RING, ROUNDS - 1)

        @block.gpsimd
        def _(pool):
            pool.memset(t.acc[:, :], 0.0).then_inc(prepared, 1)
            pool.memset(chain_r[:, :, :, :], -1e3 * BIG).then_inc(prepared, 1)
            pool.memset(chain_m[:, :, :, :], -BIG).then_inc(prepared, 1)
            pool.memset(chain[:, :, :, :], -BIG).then_inc(prepared, 1)
            if edge:
                for u in range(RING):
                    pool.memset(val[u][:, :, ATTR + DE:ATTR + DE + 1], 1.0).then_inc(prepared, 1)

            def gather(b, c):
                pool.wait_ge(staged, b.no + 1)
                if b.reuses:
                    pool.wait_ge(val_made, (b.no - RING + 1) * NG)
                settle(pool)
                for j in range(G):
                    pool.indirect_dma_start(rows[b.slot][:, j, :], None, lay.table,
                                            bass.IndirectOffsetOnAxis(idx[b.slot][:, j:j + 1], 0)).then_inc(gathered[b.slot], 16)

            run(pool, gather)

        @block.sync
        def _(sp):
            def load(b, c):
                if b.reuses:
                    sp.wait_ge(top_made, b.no - RING + 1)
                sp.dma_start(res[b.slot][0:HG, :],
                             io.resets_h[bass.ds(b.no, 1), 0:H, :, :].rearrange("b h g e -> (b h g) e")).then_inc(resets_in[b.slot], 16)
                if edge:
                    tiles = nc.values_load_multi_w_load_instructions(
                        t.tiles[0:1, bass.ds(b.no * G, G)], engines=(SPE,), min_val=0, max_val=TILES,
                        skip_runtime_bounds_check_because="counts of tiles")[1]
                    if b.reuses:
                        sp.wait_ge(msg_made, (b.no - RING + 1) * NG)
                        settle(sp)
                        sp.wait_ge(agg_made, (b.no - RING + 1) * G)
                        settle(sp)
                    for j in range(G):
                        sp.dma_start(attrT[b.slot][:, j * P:(j + 1) * P], io.attrT[:, bass.ds(tiles[j] * P, P)]).then_inc(attrs_in[b.slot], 16)
                        sp.dma_start(val[b.slot][:, j, ATTR:ATTR + DE], io.attr[bass.ds(tiles[j] * P, P), :]).then_inc(attrs_in[b.slot], 16)

            run(sp, load)

        @block.scalar
        def _(act):
            def stage(b):
                if b.reuses:
                    act.wait_ge(gathered[b.slot], b.turn * G * 16)
                    act.wait_ge(hot_made, (b.no - RING + 1) * NG)
                act.activation(idx[b.slot][:, :], t.src_k[:, bass.ds(b.no * G, G)], ACT.Copy)
                act.activation(rel[b.slot][:, :], t.rel_k[:, bass.ds(b.no * G, G)], ACT.Copy).then_inc(staged, 1)

            def group(b, q):
                g = b.no * NG + q
                act.wait_ge(hot_turned, g + 1)
                if b.some_before or q >= 2:
                    act.wait_ge(msg_made, g + 1 - gap_to(q))
                if q == 0:
                    if b.reuses:
                        act.wait_ge(fac_made, b.no - RING + 1)
                    act.activation(hot0[b.slot][:, :], hotT_ps[:, 0:1], ACT.Copy)
                act.activation(hotT[q % 2][:, :], hotT_ps[:, 0:GS * P], ACT.Copy).then_inc(hotT_made, 1)
                if edge:
                    act.wait_ge(msg_added, g + 1)
                    if b.some_before or q >= 2:
                        act.wait_ge(weighted, g + 1 - gap_to(q))
                    act.activation(pos[q % 2][:, :, :], mes[q % 2][:, :, 0:C], ACT.Relu).then_inc(relu_made, 1)

            def probabilities(c):
                act.wait_ge(dif_made, c.no + 1)
                if c.some_before:
                    act.wait_ge(val_made, c.no * NG)
                act.activation(prob[:, 0:HG], dif[:, :, :].rearrange("p g h -> p (g h)"), ACT.Exp).then_inc(prob_made, 1)
                if c.reuses:
                    act.wait_ge(agg_made, (c.no - RING + 1) * G)
                act.activation(val[c.slot][:, :, 0:RW].rearrange("p g (h r) -> p g h r", r=R)[:, :, :, C], dif[:, :, :],
                               ACT.Exp).then_inc(prob_kept, 1)

            def factor(c):
                act.wait_ge(inits_taken, c.no + 1)
                if c.some_before:
                    act.wait_ge(rescaled, c.no)
                act.activation(fac[:, :], fac_in[:, :], ACT.Exp, scale=hot0[c.slot][:, 0:1]).then_inc(fac_made, 1)

            def batch(b, c):
                stage(Batch(b.no + 2, (b.slot + 2) % RING, b.turn + (b.slot + 2) // RING))
                for q in range(NG):
                    group(b, q)
                    if q == 3 and c:
                        factor(c)
                    if q == 4 and c:
                        probabilities(c)

            stage(Batch(0, 0, 0))
            stage(Batch(1, 1, 0))
            run(act, batch)
            factor(LAST)
            probabilities(LAST)

        @block.tensor
        def _(pe):
            def turn_hot(b, q):
                g = b.no * NG + q
                pe.wait_ge(hot_made, g + 1)
                if b.some_before or q:
                    pe.wait_ge(hotT_made, g)
                for j in range(GS):
                    ins = pe.transpose(hotT_ps[:, j * P:(j + 1) * P], hot[b.slot][:, q * GS + j, :], t.ident[:, :])
                ins.then_inc(hot_turned, 1)

            def messages(b, q, wins):
                g = b.no * NG + q
                pe.wait_ge(hotT_made, g + 1)
                if edge:
                    if q == 0:
                        pe.wait_ge(attrs_in[b.slot], (b.turn + 1) * 2 * G * 16)
                    if b.some_before or q >= 2:
                        pe.wait_ge(msg_added, g + 1 - gap_to(q))
                elif q == 0 and b.some_before:
                    pe.wait_ge(msg_added, b.no)
                for j in range(GS):
                    s = q * GS + j
                    dst = lay.dst_table[:, bass.ds(wins[s] * DW, DW)]
                    if edge:
                        out = msg[q % 2][:, j * RW:(j + 1) * RW]
                        pe.matmul(out, attrT[b.slot][:, s * P:(s + 1) * P], t.we[:, :, :].rearrange("k h r -> k (h r)"),
                                  start=True, stop=False)
                        ins = pe.matmul(out, hotT[q % 2][:, j * P:(j + 1) * P], dst, start=False, stop=True)
                    else:
                        ins = pe.matmul(msg[0][:, s * H:(s + 1) * H], hotT[q % 2][:, j * P:(j + 1) * P], dst, start=True, stop=True)
                ins.then_inc(msg_made, 1)

            def turn_scores(c):
                pe.wait_ge(scored, (c.no + 1) * (NG if edge else 1))
                if c.some_before:
                    pe.wait_ge(tops_kept, c.no)
                settle(pe)
                pe.transpose(mx[0:HG, 0:P], score[c.slot][:, :, :].rearrange("p h g -> p (h g)"), t.ident[:, :]).then_inc(turned, 1)

            def turn_ends(c):
                pe.wait_ge(scanned, 2 * (c.no + 1))
                settle(pe)
                pe.transpose(mx[0:1, ENDS:ENDS + HG], fwd[0:HG, P - 1:P], t.ident[0:HG, 0:HG])
                pe.transpose(mx[0:1, ENDS + P:ENDS + P + HG], bwd[0:HG, 0:1], t.ident[0:HG, 0:HG]).then_inc(ends_made, 1)

            def turn_inits(c):
                pe.wait_ge(chained, c.no + 1)
                pe.matmul(mx[0:HG, INITS:INITS + 1], before[0:1, 0, :, :].rearrange("p h g -> p (h g)"), t.ones[0:1, 0:1], start=True, stop=True)
                pe.matmul(mx[0:HG, INITS + 1:INITS + 2], before[0:1, 1, :, :].rearrange("p h g -> p (h g)"), t.ones[0:1, 0:1], start=True, stop=True)
                pe.matmul(mx[:, GAPS:GAPS + H], t.ones[0:1, :], gap[0:1, 1, :], start=True, stop=True).then_inc(inits_made, 1)

            def turn_tops(c):
                pe.wait_ge(top_made, c.no + 1)
                settle(pe)
                pe.transpose(mx[:, 0:HG], top[0:HG, :], t.ident[0:HG, 0:HG]).then_inc(top_turned, 1)

            def sums(c):
                for q in range(NG):
                    if q == 0:
                        pe.wait_ge(tops_kept, c.no + 1)
                        pe.wait_ge(prob_kept, c.no + 1)
                    pe.wait_ge(val_made, c.no * NG + q + 1)
                    for s in range(q * GS, (q + 1) * GS):
                        if c.some_before or s >= 2:
                            pe.wait_ge(added, c.no * G + s + 1 - gap_to(s))
                        pe.matmul(agg[s % 2][:, 0:VW], hot[c.slot][:, s, :], val[c.slot][:, s, :], start=True, stop=True).then_inc(agg_made, 1)

            def batch(b, c):
                wins = nc.values_load_multi_w_load_instructions(
                    t.wins[0:1, bass.ds(b.no * G, G)], engines=(PE,), min_val=0, max_val=WINDOWS - 1,
                    skip_runtime_bounds_check_because="clamped when made")[1]
                turn_hot(b, 0)
                for q in range(NG):
                    if q == 0 and c:
                        turn_scores(c)
                    messages(b, q, wins)
                    if q + 1 < NG:
                        turn_hot(b, q + 1)
                    if c and q < 4:
                        (lambda c: None, turn_ends, turn_inits, turn_tops)[q](c)
                if c:
                    sums(c)

            run(pe, batch)
            turn_scores(LAST)
            turn_ends(LAST)
            turn_inits(LAST)
            turn_tops(LAST)
            sums(LAST)

        @block.vector
        def _(dve):
            dve.wait_ge(prepared, PREPARED)
            if edge:
                dve.tensor_copy(att_ps[:, 0:D], t.att08[:, :]).then_inc(prepared, 1)
                dve.wait_ge(prepared, PREPARED + 1)

            def one_hot(b, q):
                if q == 0:
                    dve.wait_ge(staged, b.no + 1)
                if b.reuses:
                    dve.wait_ge(agg_made, (b.no - RING) * G + (q + 1) * GS)
                for s in range(q * GS, (q + 1) * GS):
                    ins = dve.tensor_scalar(hot[b.slot][:, s, :], t.iota[:, :], rel[b.slot][:, s:s + 1], None, ALU.is_equal)
                ins.then_inc(hot_made, 1)

            def add_rows(b, q):
                g = b.no * NG + q
                dve.wait_ge(msg_made, g + 1)
                if q == 0:
                    dve.wait_ge(gathered[b.slot], (b.turn + 1) * G * 16)
                if b.some_before or q >= 2:
                    dve.wait_ge(scored, g + 1 - gap_to(q))
                    dve.wait_ge(relu_made, g + 1 - gap_to(q))
                dve.tensor_tensor(mes[q % 2][:, :, :].rearrange("p a r -> p (a r)"), msg[q % 2][:, 0:GS * RW],
                                  rows[b.slot][:, q * GS:(q + 1) * GS, :].rearrange("p g r -> p (g r)"), ALU.add).then_inc(msg_added, 1)

            def weigh(b, q):
                g = b.no * NG + q
                dve.wait_ge(relu_made, g + 1)
                if b.some_before or q:
                    dve.wait_ge(reduced, g)
                dve.tensor_tensor(wgt[:, :, :].rearrange("p (g h) c -> p g (h c)", g=GS), pos[q % 2][:, :, :].rearrange("p (g h) c -> p g (h c)", g=GS),
                                  bc(att_ps[:, 0:D].unsqueeze(1), P, GS, D), ALU.mult).then_inc(weighted, 1)

            def reduce(b, q):
                g = b.no * NG + q
                dve.wait_ge(weighted, g + 1)
                if b.some_before or q:
                    dve.wait_ge(scored, g)
                dve.tensor_reduce(red[:, :], wgt[:, :, :], AX, ALU.add).then_inc(reduced, 1)

            def finish_scores(b, q):
                g = b.no * NG + q
                dve.wait_ge(reduced, g + 1)
                if b.reuses and q == 0:
                    dve.wait_ge(dif_made, b.no - RING + 1)
                dve.tensor_tensor(score[b.slot][:, :, q * GS:(q + 1) * GS].rearrange("p h g -> p g h"),
                                  red[:, :].rearrange("p (g h) -> p g h", h=H),
                                  mes[q % 2][:, :, C].rearrange("p (g h) -> p g h", h=H), ALU.add).then_inc(scored, 1)

            def scores_gat(b):
                dve.wait_ge(msg_made, (b.no + 1) * NG)
                dve.wait_ge(gathered[b.slot], (b.turn + 1) * G * 16)
                if b.some_before:
                    dve.wait_ge(scored, b.no)
                if b.reuses:
                    dve.wait_ge(dif_made, b.no - RING + 1)
                dve.tensor_tensor(raw[:, :, :], msg[0][:, 0:HG].rearrange("p (g h) -> p g h", h=H),
                                  rows[b.slot][:, :, :].rearrange("p g (h r) -> p g h r", r=R)[:, :, :, C], ALU.add).then_inc(msg_added, 1)
                dve.wait_ge(msg_added, b.no + 1)
                dve.scalar_tensor_tensor(score[b.slot][:, :, :].rearrange("p h g -> p g h"), raw[:, :, :], SLOPE, raw[:, :, :], ALU.mult, ALU.max).then_inc(scored, 1)

            def scan(c, out, which, initial, done):
                r = res[c.slot]
                s = mx[0:HG, 0:P]
                if which == 0:
                    dve.tensor_tensor_scan(out[0:HG, :], r[0:HG, 0:P], s, initial, ALU.add, ALU.max).then_inc(done, 1)
                else:
                    dve.tensor_tensor_scan(out[0:HG, ::-1], r[0:HG, P:0:-1], s[:, ::-1], initial, ALU.add, ALU.max).then_inc(done, 1)

            def scan_steps(c):
                dve.wait_ge(turned, c.no + 1)
                dve.wait_ge(resets_in[c.slot], (c.turn + 1) * 16)
                if c.some_before:
                    dve.wait_ge(top_made, c.no)
                scan(c, fwd, 0, -BIG, scanned)
                scan(c, bwd, 1, -BIG, scanned)

            def chain_steps(c):
                n = [0]

                def step(ins, wait=True):
                    n[0] += 1
                    ins.then_inc(chain_vec, 1)
                    if wait:
                        dve.wait_ge(chain_vec, c.no * 10 + n[0])

                if c.some_before:
                    dve.wait_ge(inits_made, c.no)
                step(dve.tensor_copy(chain_m[0:1, 0, :, 0], chain[0:1, 0, :, G]), False)
                step(dve.tensor_copy(chain_r[0:1, 0, :, 1:G + 1], bc(t.rsum_f[0:1, bass.ds(c.no * G, G)].unsqueeze(1), 1, H, G)), False)
                step(dve.tensor_copy(chain_r[0:1, 1, :, G:0:-1], bc(t.rsum_b[0:1, bass.ds(c.no * G, G)].unsqueeze(1), 1, H, G)), False)
                dve.wait_ge(ends_made, c.no + 1)
                ends = mx[0:1, ENDS:ENDS + 2 * P].rearrange("p (a b) -> p a b", a=2)[:, :, 0:HG].rearrange("p a (h g) -> p a h g", g=G)
                step(dve.tensor_copy(chain_m[0:1, 0, :, 1:G + 1], ends[:, 0]), False)
                step(dve.tensor_copy(chain_m[0:1, 1, :, G:0:-1], ends[:, 1]), False)
                dve.tensor_scalar(same[:, :], res[c.slot][0:1, 0:1], 0.0, None, ALU.is_equal).then_inc(chain_vec, 1)
                n[0] += 1
                dve.wait_ge(chain_vec, c.no * 10 + n[0])
                step(dve.tensor_tensor_scan(chain[:, :, :, :].rearrange("p a h g -> p (a h g)"), chain_r[:, :, :, :].rearrange("p a h g -> p (a h g)"),
                                            chain_m[:, :, :, :].rearrange("p a h g -> p (a h g)"), -BIG, ALU.add, ALU.max))
                step(dve.tensor_copy(before[0:1, 0, :, :], chain[0:1, 0, :, 0:G]), False)
                step(dve.tensor_copy(before[0:1, 1, :, :], chain[0:1, 1, :, G - 1::-1]), False)
                step(dve.tensor_tensor(gap[0:1, 0, :], chain_m[0:1, 0, :, 0], chain[0:1, 1, :, G], ALU.subtract))
                assert n[0] == 10
                dve.tensor_scalar(gap[0:1, 1, :], gap[0:1, 0, :], 0.0, same[:, 0:1], ALU.min, ALU.mult).then_inc(chained, 1)

            def rescan_steps(c):
                dve.wait_ge(inits_made, c.no + 1)
                if c.some_before:
                    dve.wait_ge(fac_made, c.no)
                dve.tensor_copy(init[0:HG, :], mx[0:HG, INITS:INITS + 2]).then_inc(rescanned, 1)
                dve.tensor_copy(fac_in[:, :], mx[:, GAPS:GAPS + H]).then_inc(inits_taken, 1)
                dve.wait_ge(rescanned, 3 * c.no + 1)
                scan(c, fwd, 0, init[0:HG, 0:1], rescanned)
                scan(c, bwd, 1, init[0:HG, 1:2], rescanned)
                dve.wait_ge(rescanned, 3 * (c.no + 1))
                if c.some_before:
                    dve.wait_ge(top_turned, c.no)
                dve.tensor_tensor(top[0:HG, :], fwd[0:HG, :], bwd[0:HG, :], ALU.max).then_inc(top_made, 1)

            def subtract_tops(c):
                dve.wait_ge(top_turned, c.no + 1)
                if c.some_before:
                    dve.wait_ge(prob_kept, c.no)
                tops = mx[:, 0:HG].rearrange("p (h g) -> p g h", g=G)
                dve.tensor_tensor(dif[:, :, :], score[c.slot][:, :, :].rearrange("p h g -> p g h"), tops, ALU.subtract).then_inc(dif_made, 1)
                if c.reuses:
                    dve.wait_ge(agg_made, (c.no - RING + 1) * G)
                dve.tensor_tensor(val[c.slot][:, :, RW:RW + H], tops, bc(t.last_k[:, bass.ds(c.no * G, G)].unsqueeze(2), P, G, H),
                                  ALU.mult).then_inc(tops_kept, 1)

            def acc_of(win, width):
                return t.acc[:, bass.ds(win * VW, width)]

            def rescale(c, wins):
                dve.wait_ge(fac_made, c.no + 1)
                if c.some_before:
                    dve.wait_ge(added, c.no * G)
                a = acc_of(wins[0], RW).rearrange("p (h r) -> p h r", r=R)
                dve.tensor_tensor(a, a, bc(fac[:, :].unsqueeze(2), P, H, R), ALU.mult).then_inc(rescaled, 1)

            def weigh_rows(c, q):
                g = c.no * NG + q
                if q == 0:
                    dve.wait_ge(prob_made, c.no + 1)
                part = slice(q * GS, (q + 1) * GS)
                p = prob[:, q * GS * H:(q + 1) * GS * H]
                dve.tensor_tensor(val[c.slot][:, part, 0:RW].rearrange("p g (h r) -> p g h r", r=R)[:, :, :, 0:C],
                                  rows[c.slot][:, part, :].rearrange("p g (h r) -> p g h r", r=R)[:, :, :, 0:C],
                                  bc(p.rearrange("p (g h) -> p g h", h=H).unsqueeze(3), P, GS, H, C), ALU.mult).then_inc(val_made, 1)

            def add_sums(c, q, wins):
                for s in range(q * GS, (q + 1) * GS):
                    dve.wait_ge(agg_made, c.no * G + s + 1)
                    if s == 0:
                        dve.wait_ge(rescaled, c.no + 1)
                    else:
                        dve.wait_ge(added, c.no * G + s)
                    a = acc_of(wins[s], VW)
                    dve.tensor_tensor(a, agg[s % 2][:, 0:VW], a, ALU.add).then_inc(added, 1)

            def finish(c):
                wins = nc.values_load_multi_w_load_instructions(
                    t.wins[0:1, bass.ds(c.no * G, G)], engines=(DVE,), min_val=0, max_val=WINDOWS - 1,
                    skip_runtime_bounds_check_because="clamped when made")[1]
                weigh_rows(c, 0)
                weigh_rows(c, 1)
                rescale(c, wins)
                for q in range(NG):
                    add_sums(c, q, wins)
                    if q + 2 < NG:
                        weigh_rows(c, q + 2)

            MAXIMA = (scan_steps, chain_steps, rescan_steps, subtract_tops)

            def batch(b, c):
                one_hot(b, 0)
                for q in range(NG):
                    if edge:
                        add_rows(b, q)
                    if q + 1 < NG:
                        one_hot(b, q + 1)
                    if edge:
                        weigh(b, q)
                    if c and q < 4:
                        MAXIMA[q](c)
                    if edge:
                        reduce(b, q)
                        finish_scores(b, q)
                if not edge:
                    scores_gat(b)
                if c:
                    finish(c)

            run(dve, batch)
            for part in MAXIMA:
                part(LAST)
            finish(LAST)
def merge(nc, kit, io, t, lay, out_of, last_step):
    H, C, R, RW, DW, VW = lay.H, lay.C, lay.R, lay.RW, lay.DW, lay.VW
    edge = lay.edge
    n = lay.n + "m_"
    ATTR = RW + H
    with ExitStack() as ctx:
        def sb(name, shape):
            return kit.sb(n + name, shape, F32, ctx)

        def sem(name):
            return kit.sem(n + name, ctx)

        own = sb("own", [P, CH, RW])
        num = sb("num", [P, CH, RW])
        loop = sb("loop", [P, CH, H, C])
        sl = sb("sl", [P, CH, H])
        seen = sb("seen", [P, CH, H])
        old = sb("old", [P, CH, H])
        new = sb("new", [P, CH, H])
        down = sb("down", [P, 2, CH, H])
        fac = sb("fac", [P, 2, CH, H])
        den = sb("den", [P, CH, H])
        res = sb("res", [P, CH, D])
        bias = sb("bias", [P, D])
        raw = sb("raw", [P, CH, H])
        if edge:
            count = sb("count", [P, CH, 1])
            mean = sb("mean", [P, CH, DE])
            meanT = sb("meanT", [DE, CH * P])
            mes = sb("mes", [P, CH, RW])
            pos = sb("pos", [P, CH * H, C])
            turned = [kit.ps(n + f"turned{i}", [P, 512], F32, ctx) for i in range(2)]
            ee = [kit.ps(n + f"ee{i}", [P, 512], F32, ctx) for i in range(3)]
        else:
            x = sb("x", [P, CH, D])
        loaded, own_in, vec, act_done = sem("loaded"), sem("own_in"), sem("vec"), sem("act_done")
        turned_ready, meanT_ready, ee_ready, stored = sem("turned_ready"), sem("meanT_ready"), sem("ee_ready"), sem("stored")
        MEAN, MES, SCORE = (3, 7, 10) if edge else (0, 0, 2)
        DOWN = SCORE + 5
        OWN_USED = DOWN + 2
        DONE = DOWN + 8 - (0 if edge else -1)
        NA = 3 if edge else 2
        block = ctx.enter_context(nc.Block())

        @block.sync
        def _(sp):
            sp.dma_start(bias[:, :], bc(lay.bias_out, P, D)).then_inc(loaded, 16)

            def chunk(r, first, last=False):
                if not first:
                    sp.wait_ge(vec, (r - 1) * DONE + OWN_USED)
                    settle(sp)
                rows = bass.ds(r * CH * P, CH * P)
                sp.dma_start(own[:, :, :], lay.table[rows, :].rearrange("(w p) d -> p w d", p=P)).then_inc(own_in, 16)
                if not edge:
                    if not first:
                        sp.wait_ge(vec, r * DONE)
                        settle(sp)
                    sp.dma_start(x[:, :, :], lay.x_in[rows, :].rearrange("(w p) d -> p w d", p=P)).then_inc(own_in, 16)
                    sp.wait_ge(vec, (r + 1) * DONE)
                    settle(sp)
                    if not last:
                        sp.dma_start(io.out[rows, :].rearrange("(w p) d -> p w d", p=P), res[:, :, :]).then_inc(stored, 16)
                    else:
                        at = r * CH * P
                        full = (CH - 1) * P
                        sp.dma_start(io.out[at:at + full, :].rearrange("(w p) d -> p w d", p=P), res[:, 0:CH - 1, :]).then_inc(stored, 16)
                        sp.dma_start(io.out[at + full:NODES, :], res[0:LASTW, CH - 1, :]).then_inc(stored, 16)

            chunk(0, True)
            with sp.Fori(1, CHUNKS - 1) as r:
                chunk(r, False)
            chunk(CHUNKS - 1, False, True)
            if not edge:
                sp.wait_ge(stored, 16 * (CHUNKS + 1))

        @block.scalar
        def _(act):
            def chunk(r):
                if edge:
                    for half in range(2):
                        act.wait_ge(turned_ready, 2 * r + half + 1)
                        at, w = half * 4, 4 - half
                        act.activation(meanT[:, at * P:(at + w) * P], turned[half][0:DE, 0:w * P], ACT.Copy).then_inc(meanT_ready, 1)
                    act.wait_ge(vec, r * DONE + MES)
                    act.activation(pos[:, :, :], mes[:, :, :].rearrange("p w (h r) -> p (w h) r", r=R)[:, :, 0:C], ACT.Relu).then_inc(act_done, 1)
                act.wait_ge(vec, r * DONE + DOWN)
                act.activation(fac[:, :, :, :], down[:, :, :, :], ACT.Exp).then_inc(act_done, 1)

            chunk(0)
            with act.Fori(1, CHUNKS) as r:
                chunk(r)

        @block.tensor
        def _(pe):
            def chunk(r):
                pe.wait_ge(vec, r * DONE + MEAN)
                settle(pe)
                for w in range(CH):
                    half, at = divmod(w, 4)
                    ins = pe.transpose(turned[half][0:DE, at * P:(at + 1) * P], mean[:, w, :], t.ident[:, :])
                    if w in (3, CH - 1):
                        ins.then_inc(turned_ready, 1)
                pe.wait_ge(meanT_ready, 2 * (r + 1))
                for w in range(CH):
                    ins = pe.matmul(ee[w // 3][:, (w % 3) * RW:(w % 3 + 1) * RW], meanT[:, w * P:(w + 1) * P],
                                    t.we[:, :, :].rearrange("k h r -> k (h r)"), start=True, stop=True)
                ins.then_inc(ee_ready, 1)

            if edge:
                chunk(0)
                with pe.Fori(1, CHUNKS) as r:
                    chunk(r)

        @block.vector
        def _(dve):
            dve.wait_ge(loaded, 16)

            def chunk(r):
                k = [0]

                def step(ins, wait=True):
                    k[0] += 1
                    ins.then_inc(vec, 1)
                    if wait:
                        dve.wait_ge(vec, r * DONE + k[0])

                a = t.acc[:, bass.ds(r * CH * VW, CH * VW)].rearrange("p (w v) -> p w v", v=VW)
                dst = lay.dst_table[:, bass.ds(r * CH * DW, CH * DW)].rearrange("p (w v) -> p w v", v=DW)
                sums = a[:, :, 0:RW].rearrange("p w (h r) -> p w h r", r=R)
                own4 = own[:, :, :].rearrange("p w (h r) -> p w h r", r=R)
                if edge:
                    step(dve.tensor_scalar(count[:, :, :], a[:, :, ATTR + DE:ATTR + DE + 1], 1.0, None, ALU.max))
                    step(dve.reciprocal(count[:, :, :], count[:, :, :]))
                    step(dve.tensor_tensor(mean[:, :, :], a[:, :, ATTR:ATTR + DE], bc(count[:, :, :], P, CH, DE), ALU.mult), False)
                    assert k[0] == MEAN
                    dve.wait_ge(own_in, 16 * (r + 1))
                    dve.wait_ge(ee_ready, r + 1)
                    for i in range(3):
                        w = slice(3 * i, min(3 * i + 3, CH))
                        c = (w.stop - w.start) * RW
                        step(dve.tensor_tensor(mes[:, w, :].rearrange("p w v -> p (w v)"), ee[i][:, 0:c],
                                               own[:, w, :].rearrange("p w v -> p (w v)"), ALU.add), i == 2)
                    step(dve.tensor_tensor(mes[:, :, :], mes[:, :, :], dst, ALU.add), False)
                    assert k[0] == MES
                    dve.wait_ge(act_done, r * 2 + 1)
                    step(dve.tensor_tensor(pos[:, :, :].rearrange("p (w h) c -> p w (h c)", h=H), pos[:, :, :].rearrange("p (w h) c -> p w (h c)", h=H),
                                           bc(t.att08[:, :].unsqueeze(1), P, CH, D), ALU.mult))
                    step(dve.tensor_reduce(raw[:, :, :].rearrange("p w h -> p (w h)"), pos[:, :, :], AX, ALU.add))
                    step(dve.tensor_tensor(sl[:, :, :], raw[:, :, :], mes[:, :, :].rearrange("p w (h r) -> p w h r", r=R)[:, :, :, C], ALU.add))
                else:
                    dve.wait_ge(own_in, 32 * (r + 1))
                    step(dve.tensor_tensor(raw[:, :, :], own4[:, :, :, C], dst, ALU.add))
                    step(dve.scalar_tensor_tensor(sl[:, :, :], raw[:, :, :], SLOPE, raw[:, :, :], ALU.mult, ALU.max))
                assert k[0] == SCORE
                step(dve.tensor_scalar(seen[:, :, :], sums[:, :, :, C], 0.5, BIG, ALU.is_gt, ALU.mult))
                step(dve.scalar_tensor_tensor(old[:, :, :], seen[:, :, :], -BIG, a[:, :, RW:RW + H], ALU.add, ALU.add))
                step(dve.tensor_tensor(new[:, :, :], old[:, :, :], sl[:, :, :], ALU.max))
                step(dve.tensor_tensor(down[:, 0], old[:, :, :], new[:, :, :], ALU.subtract), False)
                step(dve.tensor_tensor(down[:, 1], sl[:, :, :], new[:, :, :], ALU.subtract), False)
                assert k[0] == DOWN
                dve.wait_ge(act_done, (r + 1) * (2 if edge else 1))
                num4 = num[:, :, :].rearrange("p w (h r) -> p w h r", r=R)
                step(dve.tensor_tensor(num4, sums, bc(fac[:, 0].unsqueeze(3), P, CH, H, R), ALU.mult), False)
                step(dve.tensor_tensor(loop[:, :, :, :], own4[:, :, :, 0:C], bc(fac[:, 1].unsqueeze(3), P, CH, H, C), ALU.mult))
                assert k[0] == OWN_USED
                step(dve.tensor_tensor(num4[:, :, :, 0:C], num4[:, :, :, 0:C], loop[:, :, :, :], ALU.add), False)
                step(dve.tensor_tensor(den[:, :, :], num4[:, :, :, C], fac[:, 1], ALU.add))
                step(dve.tensor_scalar(den[:, :, :], den[:, :, :], 1e-16, None, ALU.add))
                step(dve.reciprocal(den[:, :, :], den[:, :, :]))
                wide = bc(bias[:, :].unsqueeze(1), P, CH, D)
                step(dve.tensor_tensor(loop[:, :, :, :], num4[:, :, :, 0:C], bc(den[:, :, :].unsqueeze(3), P, CH, H, C), ALU.mult))
                flat = loop[:, :, :, :].rearrange("p w h c -> p w (h c)")
                if edge:
                    step(dve.tensor_tensor(t.gn[:, bass.ds(r * CH * D, CH * D)].rearrange("p (w d) -> p w d", d=D), flat, wide, ALU.add))
                else:
                    step(dve.tensor_tensor(flat, flat, wide, ALU.add))
                    dve.wait_ge(stored, 16 * r) if not isinstance(r, int) else None
                    step(dve.scalar_tensor_tensor(res[:, :, :], flat, 0.0, x[:, :, :], ALU.max, ALU.add))
                assert k[0] == DONE, (k[0], DONE)

            chunk(0)
            with dve.Fori(1, CHUNKS) as r:
                chunk(r)


def graph_norm(nc, kit, io, t, lay):
    with ExitStack() as ctx:
        def sb(name, shape):
            return kit.sb("g_" + name, shape, F32, ctx)

        def sem(name):
            return kit.sem("g_" + name, ctx)

        x = sb("x", [P, WINDOWS, D])
        sq = sb("sq", [P, WINDOWS * D])
        par = sb("par", [P, 3, D])
        valid = sb("valid", [P, P])
        col = sb("col", [P, 2, D])
        std = sb("std", [P, D])
        bank = [kit.ps(f"g_bank{i}", [P, 512], F32, ctx) for i in range(4)]
        loaded, x_in, masked, vec = sem("loaded"), sem("x_in"), sem("masked"), sem("vec")
        summed, squared, rooted, stored = sem("summed"), sem("squared"), sem("rooted"), sem("stored")
        block = ctx.enter_context(nc.Block())
        CENTERED, VAR, OUT = 5, 9, 14

        @block.gpsimd
        def _(pool):
            pool.memset(valid[:, :], 0.0).then_inc(masked, 1)
            pool.wait_ge(masked, 1)
            pool.memset(valid[0:LASTW, :], 1.0).then_inc(masked, 1)

        @block.sync
        def _(sp):
            for i, a in enumerate((io.gn_weight, io.gn_bias, io.gn_mean_scale)):
                sp.dma_start(par[:, i, :], bc(a, P, D)).then_inc(loaded, 16)
            sp.dma_start(x[:, :, :], io.x.rearrange("(w p) d -> p w d", p=P)).then_inc(x_in, 16)
            sp.wait_ge(vec, OUT)
            sp.dma_start(io.x1.rearrange("(w p) d -> p w d", p=P), x[:, :, :]).then_inc(stored, 16)
            sp.wait_ge(stored, 16)

        @block.tensor
        def _(pe):
            for i, src in enumerate((t.gn, sq)):
                if i == 0:
                    pe.wait_ge(masked, 2)
                else:
                    pe.wait_ge(squared, 1)
                for w in range(0, WINDOWS - 1, 4):
                    pe.matmul(bank[2 * i][:, :], t.ones[:, :], src[:, w * D:(w + 4) * D], start=w == 0, stop=w == WINDOWS - 5)
                pe.matmul(bank[2 * i + 1][:, 0:D], valid[:, :], src[:, (WINDOWS - 1) * D:WINDOWS * D], start=True, stop=True).then_inc(summed, 1)

        @block.scalar
        def _(act):
            act.wait_ge(vec, CENTERED)
            act.activation(sq[:, :], t.gn[:, :], ACT.Square).then_inc(squared, 1)
            act.wait_ge(vec, VAR)
            act.activation(std[:, :], col[:, 1, :], ACT.Sqrt).then_inc(rooted, 1)

        @block.vector
        def _(dve):
            n = [0]

            def step(ins, wait=True):
                n[0] += 1
                ins.then_inc(vec, 1)
                if wait:
                    dve.wait_ge(vec, n[0])

            def mean_of(i):
                dve.wait_ge(summed, i + 1)
                step(dve.tensor_reduce(col[:, i, :], bank[2 * i][:, :].rearrange("p (w d) -> p d w", d=D), AX, ALU.add))
                step(dve.tensor_tensor(col[:, i, :], col[:, i, :], bank[2 * i + 1][:, 0:D], ALU.add))

            g3 = t.gn[:, :].rearrange("p (w d) -> p w d", d=D)

            def wide(a):
                return bc(a.unsqueeze(1), P, WINDOWS, D)

            dve.wait_ge(loaded, 48)
            mean_of(0)
            step(dve.tensor_scalar(col[:, 0, :], col[:, 0, :], 1.0 / NODES, None, ALU.mult))
            step(dve.tensor_tensor(col[:, 0, :], col[:, 0, :], par[:, 2, :], ALU.mult))
            step(dve.tensor_tensor(g3, g3, wide(col[:, 0, :]), ALU.subtract), False)
            assert n[0] == CENTERED
            dve.wait_ge(vec, CENTERED)
            mean_of(1)
            step(dve.tensor_scalar(col[:, 1, :], col[:, 1, :], 1.0 / NODES, None, ALU.mult))
            step(dve.tensor_scalar(col[:, 1, :], col[:, 1, :], EPS, None, ALU.add))
            assert n[0] == VAR
            dve.wait_ge(rooted, 1)
            step(dve.reciprocal(std[:, :], std[:, :]))
            step(dve.tensor_tensor(std[:, :], std[:, :], par[:, 0, :], ALU.mult))
            step(dve.tensor_tensor(g3, g3, wide(std[:, :]), ALU.mult))
            step(dve.tensor_tensor(g3, g3, wide(par[:, 1, :]), ALU.add))
            dve.wait_ge(x_in, 16)
            step(dve.scalar_tensor_tensor(x[:, :, :], g3, 0.0, x[:, :, :], ALU.max, ALU.add), False)
            assert n[0] == OUT


def layer(kit, n, H, table, x_in, edge, ctx):
    lay = Names()
    lay.n, lay.H, lay.C, lay.R = n, H, D // H, D // H + 1
    lay.RW = H * lay.R
    lay.DW = lay.RW if edge else H
    lay.VW = lay.RW + H + (DE + 1 if edge else 0)
    lay.table, lay.x_in, lay.edge = table, x_in, edge
    lay.lin = SLOPE if edge else 1.0
    return lay


def program(nc, io):
    with ExitStack() as ctx:
        kit, t = Kit(nc, ctx), Names()
        io.tab_i, io.tab_f = kit.dram("tab_i", (2, KP), I32), kit.dram("tab_f", (2, KP))
        io.keys, io.resets = kit.dram("keys", (1 + KP * P,)), kit.dram("resets", (KP * P + P,))
        io.resets_r, io.resets_h = kit.dram("resets_r", (KP, P + 1)), kit.dram("resets_h", (BATCHES, HEADS, G, P + 1))
        io.x1 = kit.dram("x1", (NP, D))
        l0 = layer(kit, "gatv2", 4, kit.dram("table0", (NP, 4 * 33)), io.x, True, ctx)
        l1 = layer(kit, "gat", 8, kit.dram("table1", (NP, 8 * 17)), io.x1, False, ctx)
        t.ident, t.ones = kit.sb("ident", [P, P]), kit.sb("ones", [P, P])
        t.iota_i, t.iota = kit.sb("iota_i", [P, P], I32), kit.sb("iota", [P, P])
        t.step_rows = kit.sb("step_rows", [97, KP], I32)
        t.tiles, t.wins = t.step_rows[0:1, :], t.step_rows[32:33, :]
        t.rsum_f, t.rsum_b = t.step_rows[64:65, :].bitcast(F32), t.step_rows[96:97, :].bitcast(F32)
        t.src_k, t.rel_k = kit.sb("src_k", [P, KP], mybir.dt.int16), kit.sb("rel_k", [P, KP], mybir.dt.bfloat16)
        t.last_k = kit.sb("last_k", [P, KP], mybir.dt.bfloat16)
        constants(nc, kit, t)
        step_tables(nc, kit, io, t)
        with ExitStack() as part:
            t.gn = None
            with ExitStack() as low:
                l0.dst_table = kit.sb("xr", [P, WINDOWS * l0.DW], F32, low)
                t.we, t.att08 = kit.sb("we", [DE, 4, 33], F32, low), kit.sb("att08", [P, D], F32, low)
                with ExitStack() as w:
                    both = kit.sb("w0", [P, 8, 33], F32, w)
                    l0.bias = kit.sb("b0", [1, 2, 4, 33], F32, w)
                    l0.wcat = both[:, :, :].rearrange("p h r -> p (h r)")
                    l0.mats = [(io.wl, io.bl, P, io.att, both[:, 0:4, :], True), (io.wr, io.br, P, io.att, both[:, 4:8, :], True),
                               (io.we, None, DE, io.att, t.we, True)]
                    load_weights(nc, kit, io, t, l0)
                    project(nc, kit, io, t, l0)
                t.acc = kit.sb("acc0", [P, WINDOWS * l0.VW], F32, low)
                edges(nc, kit, io, t, l0)
                t.gn = kit.sb("gn", [P, WINDOWS * D], F32, low)
                l0.bias_out = io.bias_out0
                merge(nc, kit, io, t, l0, None, None)
                graph_norm(nc, kit, io, t, l0)
        l1.dst_table = kit.sb("a_dst", [P, WINDOWS * l1.DW])
        with ExitStack() as w:
            cat = kit.sb("w1", [P, l1.RW + l1.DW], F32, w)
            l1.bias, l1.wcat = None, cat[:, :]
            to = cat[:, 0:l1.RW].rearrange("p (h r) -> p h r", r=l1.R)
            l1.mats = [(io.w1, None, P, io.att_src, to, True),
                       (io.w1, None, P, io.att_dst, cat[:, l1.RW:l1.RW + l1.DW].rearrange("p (h r) -> p h r", r=1), False)]
            load_weights(nc, kit, io, t, l1)
            project(nc, kit, io, t, l1)
        t.acc = kit.sb("acc1", [P, WINDOWS * l1.VW])
        edges(nc, kit, io, t, l1)
        l1.bias_out = io.bias1
        merge(nc, kit, io, t, l1, None, None)


def kernel(**inputs):
    import numpy as np
    import concourse.bacc as bacc
    from concourse.bass_utils import run_bass_kernel_spmd as run

    def arr(name):
        return np.asarray(inputs[name])

    x = np.zeros((NP, D), np.float32)
    x[:NODES] = arr("x")
    src, dst = np.zeros(TP * P, np.int32), np.full(TP * P, NOWHERE, np.int32)
    src[:EDGES], dst[:EDGES] = arr("src"), arr("dst")
    attr = np.zeros((TP * P, DE), np.float32)
    attr[:EDGES] = arr("edge_attr_64")
    dst = dst.reshape(TP, P)

    def row(name):
        return np.ascontiguousarray(arr(name).reshape(1, D))

    data = {
        "x": x, "src_rows": src.reshape(TP, P), "dst_rows": dst, "dst_lasts": np.ascontiguousarray(dst[:TILES, -1])[None],
        "attr": attr, "attrT": np.ascontiguousarray(attr.T),
        "wl": arr("L0_gnn_Wl"), "bl": row("L0_gnn_bl"), "wr": arr("L0_gnn_Wr"), "br": row("L0_gnn_br"), "we": arr("L0_gnn_We"),
        "att": row("L0_gnn_att"), "bias_out0": row("L0_gnn_bias_out"), "gn_weight": row("L0_gnn_gn_weight"),
        "gn_bias": row("L0_gnn_gn_bias"), "gn_mean_scale": row("L0_gnn_gn_mean_scale"),
        "w1": arr("L1_gnn_W"), "att_src": row("L1_gnn_att_src"), "att_dst": row("L1_gnn_att_dst"), "bias1": row("L1_gnn_bias"),
    }
    nc = bacc.Bacc("TRN2", target_bir_lowering=False, num_devices=1)

    def given(name):
        a = data[name]
        return nc.dram_tensor("in_" + name, a.shape, mybir.dt.from_np(a.dtype), kind="ExternalInput").ap()

    io = Names()
    io.x = given("x")
    io.src_rows = given("src_rows")
    io.dst_rows = given("dst_rows")
    io.dst_lasts = given("dst_lasts")
    io.attr = given("attr")
    io.attrT = given("attrT")
    io.wl = given("wl")
    io.bl = given("bl")
    io.wr = given("wr")
    io.br = given("br")
    io.we = given("we")
    io.att = given("att")
    io.bias_out0 = given("bias_out0")
    io.gn_weight = given("gn_weight")
    io.gn_bias = given("gn_bias")
    io.gn_mean_scale = given("gn_mean_scale")
    io.w1 = given("w1")
    io.att_src = given("att_src")
    io.att_dst = given("att_dst")
    io.bias1 = given("bias1")
    io.out = nc.dram_tensor("out", (NODES, D), F32, kind="ExternalOutput").ap()
    program(nc, io)
    r = run(nc, [{"in_" + name: a for name, a in data.items()}], core_ids=[0])
    return r.results[0]["out"]
```

```python
from contextlib import ExitStack

import concourse.bass as bass
from concourse import mybir

F32 = mybir.dt.float32
I32 = mybir.dt.int32
BF16 = mybir.dt.bfloat16
ALU = mybir.AluOpType
ACT = mybir.ActivationFunctionType
AX = mybir.AxisListType.X
DVE, PE, SPE = mybir.EngineType.DVE, mybir.EngineType.PE, mybir.EngineType.SP

P = 128
NODES = 6250
EDGES = 206250
D = 128
DE = 64
WINDOWS = -(-NODES // P)
NP = WINDOWS * P
LASTW = NODES - (WINDOWS - 1) * P
GS = 3
GE = GS * P
GROUPS = -(-EDGES // GE)
GP = GROUPS + 1
NG = 5
G = NG * GS
RING = 3
BATCHES = -(-(GROUPS + WINDOWS - 1) // NG)
TURNS = BATCHES // RING
KC = -(-(BATCHES + 2) * NG // P)
KP = KC * P
KT = KP * GS
NOWHERE = 1 << 14
BIG = 1e30
HEADS = 8
SLOPE = 0.2
EPS = 1e-5
CH = 7
CHUNKS = WINDOWS // CH
assert CHUNKS * CH == WINDOWS


class Names:
    pass


def bc(ap, *shape):
    return ap.to_broadcast(list(shape))


def settle(eng):
    eng.nop(nofuse=True)


class Kit:

    def __init__(self, nc, ctx):
        self.nc, self.ctx, self.used = nc, ctx, {}

    def own(self, name):
        self.used[name] = self.used.get(name, 0) + 1
        return name if self.used[name] == 1 else f"{name}_{self.used[name]}"

    def sb(self, name, shape, dt=F32, ctx=None):
        return (ctx or self.ctx).enter_context(self.nc.sbuf_tensor(self.own(name), shape, dt))

    def ps(self, name, shape, dt=F32, ctx=None):
        return (ctx or self.ctx).enter_context(self.nc.psum_tensor(self.own(name), shape, dt))

    def sem(self, name, ctx=None):
        return self.ctx.enter_context(self.nc.semaphore(self.own(name)))

    def dram(self, name, shape, dt=F32):
        return self.nc.dram_tensor(name, shape, dt).ap()


def constants(nc, kit, t):
    made = kit.sem("c_made")
    sel = kit.sem("c_sel")
    with nc.Block() as block:
        @block.gpsimd
        def _(pool):
            pool.memset(t.ident[:, :], 0.0).then_inc(made, 1)
            pool.memset(t.ones[:, :], 1.0).then_inc(made, 1)
            pool.iota(t.iota_i[:, :], [[1, P]], base=0, channel_multiplier=0).then_inc(made, 1)
            pool.wait_ge(made, 3)
            pool.affine_select(out=t.ident[:, :], in_=t.ident[:, :], compare_op=ALU.not_equal, fill=1.0,
                               base=0, pattern=[[-1, P]], channel_multiplier=1).then_inc(sel, 1)
            pool.tensor_copy(t.iota[:, :], t.iota_i[:, :]).then_inc(sel, 1)
            pool.wait_ge(sel, 2)


def step_tables(nc, kit, io, t):
    with ExitStack() as ctx:
        def sb(name, shape, dt=F32):
            return kit.sb(name, shape, dt, ctx)

        lasts_i = sb("lasts_i", [P, GROUPS], I32)
        lastw = sb("lastw", [P, GROUPS], I32)
        group_no = sb("group_no", [P, GROUPS], I32)
        ends_at = sb("ends_at", [P, GROUPS])
        before = sb("before", [P, GROUPS])
        step_no_i = sb("step_no_i", [P, KC], I32)
        step_no = sb("step_no", [P, KC])
        group_f = sb("group_f", [P, KC])
        group_i = sb("group_i", [P, KC], I32)
        win_f = sb("win_f", [P, KC])
        win_i = sb("win_i", [P, KC], I32)
        srcr = sb("srcr", [P, KC, GE], I32)
        dstr = sb("dstr", [P, KC, GE], I32)
        srcf = sb("srcf", [P, KC, GE])
        dstf = sb("dstf", [P, KC, GE])
        rel = sb("rel", [P, KC, GE])
        inw = sb("inw", [P, KC, GE])
        key = sb("key", [P, KC, GE])
        prev = sb("prev", [P, KC, GE])
        reset = sb("reset", [P, KC, GE])
        after = sb("after", [P, KC, GE])
        last = sb("last", [P, KC, GE])
        tail = sb("tail", [1, P])
        sums = sb("sums", [P, 2, KC * GS])
        turned = [kit.ps(f"turned{i}", [P, 512], F32, ctx) for i in range(2)]
        loaded, numbered, vec = kit.sem("t_loaded"), kit.sem("t_numbered"), kit.sem("t_vec")
        rows_src, rows_dst = kit.sem("t_rows_src"), kit.sem("t_rows_dst")
        keys_out, keys_in = kit.sem("t_keys_out"), kit.sem("t_keys_in")
        resets_out, resets_in = kit.sem("t_resets_out"), kit.sem("t_resets_in")
        rows_out, spread_out = kit.sem("t_rows_out"), kit.sem("t_spread_out")
        tabs_out, tabs_in = kit.sem("t_tabs_out"), kit.sem("t_tabs_in")
        turned_ready, turned_used = kit.sem("t_turned_ready"), kit.sem("t_turned_used")
        FOUND = KC + 9
        KEYED, RESET, SUMMED, FLAGGED = FOUND + 10, FOUND + 12, FOUND + 14, FOUND + 15
        block = ctx.enter_context(nc.Block())

        def by_tile(a):
            return a[:, :, :].rearrange("p c (j e) -> p (c j) e", e=P)

        @block.gpsimd
        def _(pool):
            pool.iota(group_no[:, :], [[1, GROUPS]], base=0, channel_multiplier=0).then_inc(numbered, 1)
            pool.iota(step_no_i[:, :], [[P, KC]], base=0, channel_multiplier=1).then_inc(numbered, 1)
            pool.wait_ge(vec, FOUND)
            for rows, table, done in ((dstr, io.dst_rows, rows_dst), (srcr, io.src_rows, rows_src)):
                for c in range(KC):
                    pool.indirect_dma_start(rows[:, c, :], None, table,
                                            bass.IndirectOffsetOnAxis(group_i[:, c:c + 1], 0)).then_inc(done, 16)

        @block.sync
        def _(sp):
            def steps_of(flat, at=0):
                return flat[at:at + KP * GE].rearrange("(c p e) -> p c e", p=P, e=GE)

            sp.dma_start(lasts_i[:, :], bc(io.dst_lasts, P, GROUPS)).then_inc(loaded, 16)
            with nc.allow_non_contiguous_dma(reason="small tables"):
                sp.wait_ge(vec, FOUND)
                sp.dma_start(io.tab_i[0, :].rearrange("(c p) -> p c", p=P), group_i[:, :]).then_inc(tabs_out, 16)
                sp.dma_start(io.tab_i[1, :].rearrange("(c p) -> p c", p=P), win_i[:, :]).then_inc(tabs_out, 16)
                sp.wait_ge(vec, KEYED)
                sp.dma_start(steps_of(io.keys, 1), key[:, :, :]).then_inc(keys_out, 16)
                sp.dma_start(io.keys[0:1].rearrange("(a b) -> a b", a=1), tail[0:1, 0:1]).then_inc(keys_out, 16)
                sp.wait_ge(keys_out, 32)
                sp.dma_start(prev[:, :, :], steps_of(io.keys)).then_inc(keys_in, 16)
                sp.wait_ge(vec, RESET)
                sp.dma_start(steps_of(io.resets), reset[:, :, :]).then_inc(resets_out, 16)
                sp.dma_start(io.resets[KP * GE:KP * GE + P].rearrange("(a b) -> a b", a=1), tail[0:1, :]).then_inc(resets_out, 16)
                sp.wait_ge(resets_out, 32)
                sp.dma_start(after[:, :, :], steps_of(io.resets, 1)).then_inc(resets_in, 16)
                sp.wait_ge(resets_in, 16)
                rows = io.resets_r.rearrange("(c p j) e -> p c j e", p=P, j=GS)
                for c in range(KC):
                    sp.dma_start(rows[:, c, :, 0:P], reset[:, c, :].rearrange("p (j e) -> p j e", e=P)).then_inc(rows_out, 16)
                    sp.dma_start(rows[:, c, :, P:P + 1], after[:, c, :].rearrange("p (j e) -> p j e", e=P)[:, :, P - 1:P]).then_inc(rows_out, 16)
                sp.wait_ge(vec, SUMMED)
                for i in range(2):
                    sp.dma_start(io.tab_f[i, :].rearrange("(c p j) -> p c j", p=P, j=GS),
                                 sums[:, i, :].rearrange("p (c j) -> p c j", j=GS)).then_inc(tabs_out, 16)
            sp.wait_ge(tabs_out, 64)
            for row, table in ((t.groups, io.tab_i[0:1, :]), (t.wins, io.tab_i[1:2, :]),
                               (t.rsum_f, io.tab_f[0:1, :]), (t.rsum_b, io.tab_f[1:2, :])):
                sp.dma_start(row, table).then_inc(tabs_in, 16)
            sp.wait_ge(rows_out, 32 * KC)
            for h in range(HEADS):
                sp.dma_start(io.resets_h[:, h, :, :], io.resets_r[0:BATCHES * G, :].rearrange("(b g) e -> b g e", g=G)).then_inc(spread_out, 16)
            sp.wait_ge(tabs_in, 64)
            sp.wait_ge(spread_out, 16 * HEADS)

        @block.vector
        def _(dve):
            n = [0]

            def step(ins, wait=True):
                n[0] += 1
                ins.then_inc(vec, 1)
                if wait:
                    dve.wait_ge(vec, n[0])

            dve.wait_ge(loaded, 16)
            dve.wait_ge(numbered, 2)
            step(dve.tensor_scalar(lastw[:, :], lasts_i[:, :], 7, None, ALU.arith_shift_right), False)
            step(dve.tensor_copy(step_no[:, :], step_no_i[:, :]))
            step(dve.tensor_scalar(ends_at[:, :], lastw[:, :], float(WINDOWS - 1), 0.0, ALU.min, ALU.max))
            step(dve.tensor_tensor(ends_at[:, :], ends_at[:, :], group_no[:, :], ALU.add))
            for c in range(KC):
                step(dve.tensor_scalar(before[:, :], ends_at[:, :], step_no[:, c:c + 1], 0.0, ALU.is_lt, ALU.add,
                                       accum_out=group_f[:, c:c + 1]))
            step(dve.tensor_tensor(win_f[:, :], step_no[:, :], group_f[:, :], ALU.subtract))
            step(dve.tensor_scalar(win_f[:, :], win_f[:, :], float(WINDOWS - 1), 0.0, ALU.min, ALU.max))
            step(dve.tensor_copy(group_i[:, :], group_f[:, :]), False)
            step(dve.tensor_copy(win_i[:, :], win_f[:, :]), False)
            step(dve.memset(tail[:, :], -BIG))
            assert n[0] == FOUND
            dve.wait_ge(rows_dst, 16 * KC)
            step(dve.tensor_copy(dstf[:, :, :], dstr[:, :, :]))
            step(dve.scalar_tensor_tensor(rel[:, :, :], bc(win_f[:, :].unsqueeze(2), P, KC, GE), -float(P), dstf[:, :, :],
                                          ALU.mult, ALU.add))
            step(dve.tensor_scalar(inw[:, :, :], rel[:, :, :], 0.0, None, ALU.is_ge), False)
            step(dve.tensor_scalar(prev[:, :, :], rel[:, :, :], float(P), None, ALU.is_lt))
            step(dve.tensor_tensor(inw[:, :, :], inw[:, :, :], prev[:, :, :], ALU.mult))
            one_more = bc(step_no[:, :].unsqueeze(2), P, KC, GE)
            step(dve.scalar_tensor_tensor(key[:, :, :], one_more, 1.0, dstf[:, :, :], ALU.add, ALU.add))
            step(dve.tensor_tensor(key[:, :, :], key[:, :, :], inw[:, :, :], ALU.mult))
            step(dve.scalar_tensor_tensor(reset[:, :, :], one_more, 1.0, key[:, :, :], ALU.add, ALU.subtract))
            step(dve.tensor_scalar(key[:, :, :], reset[:, :, :], -1.0, None, ALU.mult), False)
            dve.wait_ge(rows_src, 16 * KC)
            step(dve.tensor_copy(srcf[:, :, :], srcr[:, :, :]))
            assert n[0] == KEYED
            dve.wait_ge(keys_in, 16)
            step(dve.tensor_tensor(reset[:, :, :], key[:, :, :], prev[:, :, :], ALU.not_equal))
            step(dve.tensor_scalar(reset[:, :, :], reset[:, :, :], -BIG, None, ALU.mult))
            assert n[0] == RESET
            dve.wait_ge(resets_in, 16)
            step(dve.tensor_reduce(sums[:, 0, :], by_tile(reset), AX, ALU.add), False)
            step(dve.tensor_reduce(sums[:, 1, :], by_tile(after), AX, ALU.add))
            assert n[0] == SUMMED
            step(dve.tensor_scalar(last[:, :, :], after[:, :, :], 0.0, None, ALU.is_lt))
            assert n[0] == FLAGGED
            for i in range(3 * KC * GS):
                what, cj = divmod(i, KC * GS)
                c, j = divmod(cj, GS)
                dve.wait_ge(turned_ready, i + 1)
                out = (t.rel_k, t.src_k, t.last_k)[what][:, c * GE:(c + 1) * GE].rearrange("p (k j) -> p k j", j=GS)[:, :, j]
                dve.tensor_copy(out, turned[i % 2][:, 0:P]).then_inc(turned_used, 1)
            dve.wait_ge(turned_used, 3 * KC * GS)

        @block.tensor
        def _(pe):
            for i in range(3 * KC * GS):
                what, cj = divmod(i, KC * GS)
                c, j = divmod(cj, GS)
                if cj == 0:
                    pe.wait_ge(vec, (KEYED, KEYED, FLAGGED)[what])
                if i >= 2:
                    pe.wait_ge(turned_used, i - 1)
                pe.transpose(turned[i % 2][:, 0:P], (rel, srcf, last)[what][:, c, j * P:(j + 1) * P], t.ident[:, :]).then_inc(turned_ready, 1)
def load_weights(nc, kit, io, t, lay):
    H, C, R = lay.H, lay.C, lay.R
    with ExitStack() as ctx:
        def sb(name, shape):
            return kit.sb(f"{lay.n}_{name}", shape, F32, ctx)

        mats = lay.mats
        prod = sb("prod", [P, D])
        raw = sb("raw", [P, D])
        att = sb("att", [P, len(mats), D])
        loaded, vec = kit.sem(f"{lay.n}w_loaded"), kit.sem(f"{lay.n}w_vec")
        loads = sum(3 if b is not None else 2 for _, b, _, _, _, _ in mats)
        block = ctx.enter_context(nc.Block())

        @block.sync
        def _(sp):
            for i, (w, b, rows, a, to, keep) in enumerate(mats):
                dst = to[0:rows, :, 0:C] if keep else raw[0:rows, :].rearrange("p (h c) -> p h c", h=H)
                with nc.allow_non_contiguous_dma(reason="weights, once"):
                    sp.dma_start(dst, w.rearrange("k (h c) -> k h c", h=H)).then_inc(loaded, 16)
                    sp.dma_start(att[:, i, :], bc(a, P, D)).then_inc(loaded, 16)
                    if b is not None:
                        sp.dma_start(lay.bias[0:1, i, :, 0:C], b.rearrange("o (h c) -> o h c", h=H)).then_inc(loaded, 16)

        @block.vector
        def _(dve):
            n = [0]

            def step(ins):
                n[0] += 1
                ins.then_inc(vec, 1)
                dve.wait_ge(vec, n[0])

            dve.wait_ge(loaded, 16 * loads)
            for i, (w, b, rows, a, to, keep) in enumerate(mats):
                src = to[0:rows, :, 0:C] if keep else raw[0:rows, :].rearrange("p (h c) -> p h c", h=H)
                col = to[0:rows, :, C] if keep else to[0:rows, :, 0]
                last = bc(col.unsqueeze(2), rows, H, 1)
                for src, rows, last in [(src, rows, last)] + (
                        [(lay.bias[0:1, i, :, 0:C], 1, lay.bias[0:1, i, :, C:C + 1])] if b is not None else []):
                    pr = prod[0:rows, :].rearrange("p (h c) -> p h c", h=H)
                    step(dve.tensor_tensor(pr, src, att[0:rows, i, :].rearrange("p (h c) -> p h c", h=H), ALU.mult))
                    step(dve.tensor_reduce(last, pr, AX, ALU.add))
                    if lay.lin != 1.0:
                        step(dve.tensor_scalar(last, last, lay.lin, None, ALU.mult))
            if lay.edge:
                step(dve.memset(t.att08[:, :, C:C + 1], 1.0))
                step(dve.tensor_scalar(t.att08[:, :, 0:C], att[:, 0, :].rearrange("p (h c) -> p h c", h=H), 1.0 - SLOPE, None, ALU.mult))


def project(nc, kit, io, t, lay):
    RW, DW = lay.RW, lay.DW
    BW = RW + DW
    n = lay.n + "p_"
    with ExitStack() as ctx:
        def sb(name, shape):
            return kit.sb(n + name, shape, F32, ctx)

        def sem(name):
            return kit.sem(n + name, ctx)

        x = sb("x", [P, CH, D])
        xc = sb("xc", [P, CH, D])
        sq = sb("sq", [P, CH, D])
        xn = sb("xn", [P, CH, D])
        hT = sb("hT", [P, CH * P])
        mean = sb("mean", [P, CH])
        var = sb("var", [P, CH])
        std = sb("std", [P, CH])
        stage = sb("stage", [P, CH, RW])
        turned = [kit.ps(n + f"turned{i}", [P, 512], F32, ctx) for i in range(2)]
        out = [kit.ps(n + f"out{i}", [P, 512], F32, ctx) for i in range(2)]
        x_in, stored = sem("x_in"), sem("stored")
        vec, squared, rooted = sem("vec"), sem("squared"), sem("rooted")
        h_turned, h_ready = sem("h_turned"), sem("h_ready")
        made = [sem("made_even"), sem("made_odd")]
        taken = [sem("taken_even"), sem("taken_odd")]
        MADE = [(CH + 1) // 2, CH // 2]
        CENTERED, SPREAD, SCALED, NV = 3, 5, 7, 7
        block = ctx.enter_context(nc.Block())

        @block.sync
        def _(sp):
            def chunk(r, first=False):
                if not first:
                    sp.wait_ge(vec, (r - 1) * NV + CENTERED)
                    settle(sp)
                sp.dma_start(x[:, :, :], lay.x_in[bass.ds(r * CH * P, CH * P), :].rearrange("(w p) d -> p w d", p=P)).then_inc(x_in, 16)
                for e in range(2):
                    sp.wait_ge(taken[e], (r + 1) * MADE[e])
                    settle(sp)
                sp.dma_start(lay.table[bass.ds(r * CH * P, CH * P), :].rearrange("(w p) d -> p w d", p=P), stage[:, :, :]).then_inc(stored, 16)

            chunk(0, True)
            with sp.Fori(1, CHUNKS) as r:
                chunk(r)
            sp.wait_ge(stored, 16 * CHUNKS)

        def take(eng, copy, parity, r, first):
            if not first:
                eng.wait_ge(stored, 16 * r)
            for i, w in enumerate(range(parity, CH, 2)):
                eng.wait_ge(made[parity], r * MADE[parity] + i + 1)
                copy(stage[:, w, :], out[parity][:, 0:RW])
                copy(lay.dst_table[:, bass.ds((r * CH + w) * DW, DW)], out[parity][:, RW:BW]).then_inc(taken[parity], 1)

        @block.vector
        def _(dve):
            def chunk(r, first=False):
                k = [0]

                def step(ins, wait=True):
                    k[0] += 1
                    ins.then_inc(vec, 1)
                    if wait:
                        dve.wait_ge(vec, r * NV + k[0])

                def wide(a):
                    return bc(a[:, :].unsqueeze(2), P, CH, D)

                dve.wait_ge(x_in, 16 * (r + 1))
                step(dve.tensor_reduce(mean[:, :], x[:, :, :], AX, ALU.add))
                step(dve.tensor_scalar(mean[:, :], mean[:, :], 1.0 / D, None, ALU.mult))
                step(dve.tensor_tensor(xc[:, :, :], x[:, :, :], wide(mean), ALU.subtract), False)
                dve.wait_ge(squared, r + 1)
                step(dve.tensor_reduce(var[:, :], sq[:, :, :], AX, ALU.add))
                step(dve.tensor_scalar(var[:, :], var[:, :], 1.0 / D, EPS, ALU.mult, ALU.add), False)
                dve.wait_ge(rooted, r + 1)
                step(dve.reciprocal(std[:, :], std[:, :]))
                step(dve.tensor_tensor(xn[:, :, :], xc[:, :, :], wide(std), ALU.mult), False)
                take(dve, dve.tensor_copy, 1, r, first)

            chunk(0, True)
            with dve.Fori(1, CHUNKS) as r:
                chunk(r)

        @block.scalar
        def _(act):
            def chunk(r, first=False):
                act.wait_ge(vec, r * NV + CENTERED)
                act.activation(sq[:, :, :], xc[:, :, :], ACT.Square).then_inc(squared, 1)
                act.wait_ge(vec, r * NV + SPREAD)
                act.activation(std[:, :], var[:, :], ACT.Sqrt).then_inc(rooted, 1)
                for half in range(2):
                    act.wait_ge(h_turned, 2 * r + half + 1)
                    w = CH // 2 + 1 if half == 0 else CH // 2
                    at = half * (CH // 2 + 1)
                    act.activation(hT[:, at * P:(at + w) * P], turned[half][:, 0:w * P], ACT.Relu).then_inc(h_ready, 1)
                take(act, lambda o, i: act.activation(o, i, ACT.Copy), 0, r, first)

            chunk(0, True)
            with act.Fori(1, CHUNKS) as r:
                chunk(r)

        @block.tensor
        def _(pe):
            def chunk(r, first=False):
                pe.wait_ge(vec, r * NV + SCALED)
                for w in range(CH):
                    half, at = divmod(w, CH // 2 + 1)
                    ins = pe.transpose(turned[half][:, at * P:(at + 1) * P], xn[:, w, :], t.ident[:, :])
                    if w in (CH // 2, CH - 1):
                        ins.then_inc(h_turned, 1)
                for w in range(CH):
                    half, e = w // (CH // 2 + 1), w % 2
                    if w in (0, CH // 2 + 1):
                        pe.wait_ge(h_ready, 2 * r + half + 1)
                    if w >= 2:
                        pe.wait_ge(taken[e], r * MADE[e] + w // 2)
                    elif not first:
                        pe.wait_ge(taken[e], r * MADE[e])
                    lhs = hT[:, w * P:(w + 1) * P]
                    if lay.bias is not None:
                        pe.matmul(out[e][:, 0:BW], t.ones[0:1, :], lay.bias[0:1, :, :, :].rearrange("p a h c -> p (a h c)"),
                                  start=True, stop=False)
                    pe.matmul(out[e][:, 0:BW], lhs, lay.wcat[:, 0:BW], start=lay.bias is None, stop=True).then_inc(made[e], 1)

            chunk(0, True)
            with pe.Fori(1, CHUNKS) as r:
                chunk(r)
class Batch:

    def __init__(self, no, slot, turn):
        self.no, self.slot, self.turn = no, slot, turn
        self.reuses = not isinstance(no, int) or no >= RING
        self.some_before = not isinstance(no, int) or no > 0

    def before(self):
        if self.slot:
            return Batch(self.no - 1, self.slot - 1, self.turn)
        return Batch(self.no - 1, RING - 1, self.turn - 1)

    def after(self, n=1):
        return Batch(self.no + n, (self.slot + n) % RING, self.turn + (self.slot + n) // RING)

    def exists(self):
        return not isinstance(self.no, int) or self.no < BATCHES


def behind(b, n):
    if isinstance(b.no, int) and not 0 <= b.no - n < BATCHES:
        return None
    for _ in range(n):
        b = b.before()
    return b


def gap_to(i):
    return {0: 1, 1: 3}.get(i, 2)


def later(b, q, n, do, *more):
    at = b.after((q + n) // NG) if q + n >= NG else b
    if at.exists():
        do(at, (q + n) % NG, *more)


def edges(nc, kit, io, t, lay):
    H, C, R, RW, DW, VW = lay.H, lay.C, lay.R, lay.RW, lay.DW, lay.VW
    HG = H * G
    edge = lay.edge
    assert BATCHES % RING and NG % 2 == 1 and NG > RING and HG <= P and GS * RW <= 512 and 3 * G * HEADS <= 512
    with ExitStack() as ctx:
        def sb(name, shape, dt=F32):
            return kit.sb(f"{lay.n}_{name}", shape, dt, ctx)

        def ps(name):
            return kit.ps(f"{lay.n}_{name}", [P, 512], F32, ctx)

        def sem(name):
            return kit.sem(f"{lay.n}_{name}", ctx)

        idx = [sb(f"idx{i}", [P, G], I32) for i in range(RING)]
        place = [sb(f"place{i}", [P, G]) for i in range(RING)]
        rows = [sb(f"rows{i}", [P, G, RW]) for i in range(RING)]
        hot = [sb(f"hot{i}", [P, G, P]) for i in range(RING)]
        val = [sb(f"val{i}", [P, G, VW]) for i in range(RING)]
        res = [sb(f"res{i}", [P, P + 1]) for i in range(RING)]
        hot0 = [sb(f"hot0_{i}", [P, 1]) for i in range(RING)]
        score = [sb(f"score{i}", [P, H, G]) for i in range(RING)]
        hotT = [sb(f"hotT{i}", [P, GS * P], F32 if edge else BF16) for i in range(RING)]
        if edge:
            attrT = [sb(f"attrT{i}", [DE, G * P]) for i in range(RING)]
            mes = [sb(f"mes{i}", [P, GS * H, R]) for i in range(RING)]
        else:
            parts = sb("parts", [P, WINDOWS, 3, H], BF16)
            rest = sb("rest", [P, 2, WINDOWS, H])
            split = sem("split")
        raw = sb("raw", [P, G, H])
        fwd, bwd, top = sb("fwd", [P, P]), sb("bwd", [P, P]), sb("top", [P, P])
        chain_r = sb("chain_r", [1, 2, H, G + 1])
        chain_m = sb("chain_m", [1, 2, H, G + 1])
        chain = sb("chain", [1, 2, H, G + 1])
        before = sb("before", [1, 2, H, G])
        init = sb("init", [P, 2])
        gap = sb("gap", [1, 2, H])
        same = sb("same", [1, 1])
        fac_in, fac = sb("fac_in", [P, H]), sb("fac", [P, H])
        dif = sb("dif", [P, G, H])
        msg = [ps(f"msg{i}") for i in range(RING)]
        hotT_ps = ps("hotT_ps")
        agg = [ps("agg0"), ps("agg1")]
        mx = ps("mx")
        prob = ps("prob")
        ENDS, INITS, GAPS = P, 3 * P, 3 * P + 8

        gathered = [sem(f"gathered{i}") for i in range(RING)]
        attrs_in = [sem(f"attrs_in{i}") for i in range(RING)]
        vals_in = [sem(f"vals_in{i}") for i in range(RING)]
        resets_in = [sem(f"resets_in{i}") for i in range(RING)]
        prepared, staged = sem("prepared"), sem("staged")
        off_made, hot_made, hot_turned, hotT_made = sem("off_made"), sem("hot_made"), sem("hot_turned"), sem("hotT_made")
        msg_made, msg_added = sem("msg_made"), sem("msg_added")
        relu_made, weighted, scored, joined = sem("relu_made"), sem("weighted"), sem("scored"), sem("joined")
        turned, scanned, ends_made = sem("turned"), sem("scanned"), sem("ends_made")
        resets_kept = sem("resets_kept")
        chain_vec, chained, inits_made = sem("chain_vec"), sem("chained"), sem("inits_made")
        inits_taken, rescanned, top_made, top_turned = sem("inits_taken"), sem("rescanned"), sem("top_made"), sem("top_turned")
        dif_made, tops_kept, prob_made, prob_kept = sem("dif_made"), sem("tops_kept"), sem("prob_made"), sem("prob_kept")
        fac_made, rescaled = sem("fac_made"), sem("rescaled")
        val_made, agg_made, added = sem("val_made"), sem("agg_made"), sem("added")
        PREPARED = 4 + (RING if edge else 0)
        ATTR = RW + H
        block = ctx.enter_context(nc.Block())

        def run(eng, batch, extra=0):
            for u in range(RING):
                batch(Batch(u, u, 0))
            with eng.Fori(1, TURNS) as r:
                for u in range(RING):
                    batch(Batch(r * RING + u, u, r))
            for no in range(TURNS * RING, BATCHES + extra):
                batch(Batch(no, no % RING, no // RING))

        def step_slot(b, q):
            return (b.slot * NG + q) % RING

        FIRST = Batch(0, 0, 0)

        @block.gpsimd
        def _(pool):
            pool.memset(t.acc[:, :], 0.0).then_inc(prepared, 1)
            pool.memset(chain_r[:, :, :, :], -1e3 * BIG).then_inc(prepared, 1)
            pool.memset(chain_m[:, :, :, :], -BIG).then_inc(prepared, 1)
            pool.memset(chain[:, :, :, :], -BIG).then_inc(prepared, 1)
            if edge:
                for u in range(RING):
                    pool.memset(val[u][:, :, ATTR + DE:ATTR + DE + 1], 1.0).then_inc(prepared, 1)

            def gather(b):
                pool.wait_ge(staged, b.no + 1)
                settle(pool)
                for j in range(G):
                    if b.reuses and j % GS == 0:
                        pool.wait_ge(val_made, (b.no - RING) * NG + j // GS + 1)
                        settle(pool)
                    pool.indirect_dma_start(rows[b.slot][:, j, :], None, lay.table,
                                            bass.IndirectOffsetOnAxis(idx[b.slot][:, j:j + 1], 0)).then_inc(gathered[b.slot], 16)

            run(pool, gather)

        @block.sync
        def _(sp):
            def load(b):
                if b.reuses:
                    sp.wait_ge(top_made, b.no - RING + 1)
                sp.dma_start(res[b.slot][0:HG, :],
                             io.resets_h[bass.ds(b.no, 1), 0:H, :, :].rearrange("b h g e -> (b h g) e")).then_inc(resets_in[b.slot], 16)
                if edge:
                    groups = nc.values_load_multi_w_load_instructions(
                        t.groups[0:1, bass.ds(b.no * NG, NG)], engines=(SPE,), min_val=0, max_val=GROUPS,
                        skip_runtime_bounds_check_because="counts of groups")[1]
                    if b.reuses:
                        sp.wait_ge(msg_made, (b.no - RING + 1) * NG)
                        settle(sp)
                    for q in range(NG):
                        sp.dma_start(attrT[b.slot][:, q * GE:(q + 1) * GE],
                                     io.attrT[:, bass.ds(groups[q] * GE, GE)]).then_inc(attrs_in[b.slot], 16)
                    if b.reuses:
                        sp.wait_ge(agg_made, (b.no - RING + 1) * NG)
                        settle(sp)
                    for q in range(NG):
                        sp.dma_start(val[b.slot][:, q * GS:(q + 1) * GS, ATTR:ATTR + DE],
                                     io.attr[bass.ds(groups[q] * GE, GE), :].rearrange("(j p) d -> p j d", p=P)).then_inc(vals_in[b.slot], 16)

            run(sp, load)

        @block.scalar
        def _(act):
            def stage(b):
                if b.reuses:
                    act.wait_ge(gathered[b.slot], b.turn * G * 16)
                    act.wait_ge(hot_made, (b.no - RING + 1) * NG)
                act.activation(idx[b.slot][:, :], t.src_k[:, bass.ds(b.no * G, G)], ACT.Copy)
                act.activation(place[b.slot][:, :], t.rel_k[:, bass.ds(b.no * G, G)], ACT.Copy, scale=-1.0).then_inc(staged, 1)

            def chain_resets(c):
                if c.some_before:
                    act.wait_ge(chained, 2 * c.no)
                act.activation(chain_r[0:1, 0, :, 1:G + 1], bc(t.rsum_f[0:1, bass.ds(c.no * G, G)].unsqueeze(1), 1, H, G), ACT.Copy)
                act.activation(chain_r[0:1, 1, :, G:0:-1], bc(t.rsum_b[0:1, bass.ds(c.no * G, G)].unsqueeze(1), 1, H, G),
                               ACT.Copy).then_inc(resets_kept, 1)

            def off_nodes(b, q):
                if q == 0:
                    act.wait_ge(staged, b.no + 1)
                if b.reuses:
                    act.wait_ge(agg_made, (b.no - RING) * NG + q + 1)
                for j in range(GS):
                    s = q * GS + j
                    ins = act.activation(hot[b.slot][:, s, :], t.iota[:, :], ACT.Abs, bias=place[b.slot][:, s:s + 1])
                ins.then_inc(off_made, 1)

            def one_hot(b, q):
                act.wait_ge(off_made, b.no * NG + q + 1)
                part = hot[b.slot][:, q * GS:(q + 1) * GS, :]
                act.activation(part, part, ACT.Relu, scale=-1.0, bias=t.ones[:, 0:1]).then_inc(hot_made, 1)

            def keep_turned(b, q):
                g = b.no * NG + q
                act.wait_ge(hot_turned, g + 1)
                if b.some_before or q >= RING:
                    act.wait_ge(msg_made, g + 1 - RING)
                if q == 0:
                    if b.reuses:
                        act.wait_ge(fac_made, b.no - RING + 1)
                    act.activation(hot0[b.slot][:, :], hotT_ps[:, 0:1], ACT.Copy)
                act.activation(hotT[step_slot(b, q)][:, :], hotT_ps[:, 0:GS * P], ACT.Copy).then_inc(hotT_made, 1)

            def relu(b, q):
                act.wait_ge(msg_added, b.no * NG + q + 1)
                part = mes[step_slot(b, q)][:, :, 0:C]
                act.activation(part, part, ACT.Relu).then_inc(relu_made, 1)

            def probabilities(c):
                act.wait_ge(dif_made, c.no + 1)
                if c.some_before:
                    act.wait_ge(val_made, c.no * NG)
                act.activation(prob[:, 0:HG], dif[:, :, :].rearrange("p g h -> p (g h)"), ACT.Exp).then_inc(prob_made, 1)
                if c.reuses:
                    act.wait_ge(agg_made, (c.no - RING + 1) * NG)
                act.activation(val[c.slot][:, :, 0:RW].rearrange("p g (h r) -> p g h r", r=R)[:, :, :, C], dif[:, :, :],
                               ACT.Exp).then_inc(prob_kept, 1)

            def factor(c):
                act.wait_ge(inits_taken, c.no + 1)
                if c.some_before:
                    act.wait_ge(rescaled, c.no)
                act.activation(fac[:, :], fac_in[:, :], ACT.Exp, scale=hot0[c.slot][:, 0:1]).then_inc(fac_made, 1)

            def batch(b):
                c = behind(b, 1)
                if b.after(2).exists():
                    stage(b.after(2))
                if c:
                    chain_resets(c)
                for q in range(NG):
                    later(b, q, 4, off_nodes)
                    later(b, q, 3, keep_turned)
                    later(b, q, 4, one_hot)
                    if edge:
                        later(b, q, 1, relu)
                    if q == 3 and c:
                        probabilities(c)
                        factor(c)

            stage(Batch(0, 0, 0))
            stage(Batch(1, 1, 0))
            act.wait_ge(prepared, PREPARED)
            for q in range(4):
                off_nodes(FIRST, q)
                one_hot(FIRST, q)
                if q < 3:
                    keep_turned(FIRST, q)
            if edge:
                relu(FIRST, 0)
            run(act, batch, 1)

        @block.tensor
        def _(pe):
            def turn_hot(b, q):
                g = b.no * NG + q
                pe.wait_ge(hot_made, g + 1)
                if b.some_before or q:
                    pe.wait_ge(hotT_made, g)
                for j in range(GS):
                    ins = pe.transpose(hotT_ps[:, j * P:(j + 1) * P], hot[b.slot][:, q * GS + j, :], t.ident[:, :])
                ins.then_inc(hot_turned, 1)

            def messages(b, q, win):
                g = b.no * NG + q
                pe.wait_ge(hotT_made, g + 1)
                if edge:
                    if q == 0:
                        pe.wait_ge(attrs_in[b.slot], (b.turn + 1) * NG * 16)
                    if b.some_before or q >= RING:
                        pe.wait_ge(msg_added, g + 1 - RING)
                elif q == 0 and b.reuses:
                    pe.wait_ge(msg_added, b.no - RING + 1)
                if edge:
                    dst = lay.dst_table[:, bass.ds(win * DW, DW)]
                else:
                    dst = parts[:, :, :, :].rearrange("p w k h -> p (w k h)")[:, bass.ds(win * 3 * H, 3 * H)]
                turned_hot = hotT[step_slot(b, q)]
                for j in range(GS):
                    s = q * GS + j
                    if edge:
                        out = msg[step_slot(b, q)][:, j * RW:(j + 1) * RW]
                        pe.matmul(out, attrT[b.slot][:, s * P:(s + 1) * P], t.we[:, :, :].rearrange("k h r -> k (h r)"),
                                  start=True, stop=False)
                        ins = pe.matmul(out, turned_hot[:, j * P:(j + 1) * P], dst, start=False, stop=True)
                    else:
                        ins = pe.matmul(msg[b.slot][:, s * 3 * H:(s + 1) * 3 * H], turned_hot[:, j * P:(j + 1) * P], dst, start=True, stop=True)
                ins.then_inc(msg_made, 1)

            def turn_scores(c):
                pe.wait_ge(scored, (c.no + 1) * (NG if edge else 1))
                if c.some_before:
                    pe.wait_ge(tops_kept, c.no)
                settle(pe)
                pe.transpose(mx[0:HG, 0:P], score[c.slot][:, :, :].rearrange("p h g -> p (h g)"), t.ident[:, :]).then_inc(turned, 1)

            def turn_ends(c):
                pe.wait_ge(scanned, 2 * (c.no + 1))
                settle(pe)
                pe.transpose(mx[0:1, ENDS:ENDS + HG], fwd[0:HG, P - 1:P], t.ident[0:HG, 0:HG])
                pe.transpose(mx[0:1, ENDS + P:ENDS + P + HG], bwd[0:HG, 0:1], t.ident[0:HG, 0:HG]).then_inc(ends_made, 1)

            def turn_inits(c):
                pe.wait_ge(chained, 2 * (c.no + 1))
                pe.matmul(mx[0:HG, INITS:INITS + 1], before[0:1, 0, :, :].rearrange("p h g -> p (h g)"), t.ones[0:1, 0:1], start=True, stop=True)
                pe.matmul(mx[0:HG, INITS + 1:INITS + 2], before[0:1, 1, :, :].rearrange("p h g -> p (h g)"), t.ones[0:1, 0:1], start=True, stop=True)
                pe.matmul(mx[:, GAPS:GAPS + H], t.ones[0:1, :], gap[0:1, 1, :], start=True, stop=True).then_inc(inits_made, 1)

            def turn_tops(c):
                pe.wait_ge(top_made, c.no + 1)
                settle(pe)
                pe.transpose(mx[:, 0:HG], top[0:HG, :], t.ident[0:HG, 0:HG]).then_inc(top_turned, 1)

            def sums(c, q):
                if q == 0:
                    if edge:
                        pe.wait_ge(vals_in[c.slot], (c.turn + 1) * NG * 16)
                    pe.wait_ge(tops_kept, c.no + 1)
                    pe.wait_ge(prob_kept, c.no + 1)
                pe.wait_ge(val_made, c.no * NG + q + 1)
                if c.some_before or q >= 2:
                    pe.wait_ge(added, c.no * NG + q + 1 - gap_to(q))
                for j in range(GS):
                    s = q * GS + j
                    ins = pe.matmul(agg[q % 2][:, 0:VW], hot[c.slot][:, s, :], val[c.slot][:, s, :], start=j == 0, stop=j == GS - 1)
                ins.then_inc(agg_made, 1)

            def windows(step, n):
                return nc.values_load_multi_w_load_instructions(
                    t.wins[0:1, bass.ds(step, n)], engines=(PE,), min_val=0, max_val=WINDOWS - 1,
                    skip_runtime_bounds_check_because="clamped when made")[1]

            def batch(b):
                c, cc = behind(b, 1), behind(b, 2)
                wins = windows(b.no * NG + 2, NG) if b.exists() else [0] * NG
                for q in range(NG):
                    if c and q == 1:
                        turn_scores(c)
                    later(b, q, 2, messages, wins[q])
                    later(b, q, 3, turn_hot)
                    if cc:
                        sums(cc, q)
                    if c and q in (1, 2, 3):
                        (turn_ends, turn_inits, turn_tops)[q - 1](c)

            if not edge:
                pe.wait_ge(split, 5)
            first = windows(0, 2)
            turn_hot(FIRST, 0)
            turn_hot(FIRST, 1)
            messages(FIRST, 0, first[0])
            turn_hot(FIRST, 2)
            messages(FIRST, 1, first[1])
            run(pe, batch, 2)

        @block.vector
        def _(dve):
            dve.wait_ge(prepared, PREPARED)
            if not edge:
                table = lay.dst_table[:, :].rearrange("p (w h) -> p w h", h=H)
                for k in range(3):
                    dve.tensor_copy(parts[:, :, k, :], (table, rest[:, 0], rest[:, 1])[k]).then_inc(split, 1)
                    if k < 2:
                        dve.wait_ge(split, 2 * k + 1)
                        dve.tensor_tensor(rest[:, k], (table, rest[:, 0])[k], parts[:, :, k, :], ALU.subtract).then_inc(split, 1)
                        dve.wait_ge(split, 2 * k + 2)

            def add_rows(b, q):
                g = b.no * NG + q
                dve.wait_ge(msg_made, g + 1)
                if q == 0:
                    dve.wait_ge(gathered[b.slot], (b.turn + 1) * G * 16)
                if b.some_before or q >= RING:
                    dve.wait_ge(scored, g + 1 - RING)
                dve.tensor_tensor(mes[step_slot(b, q)][:, :, :].rearrange("p a r -> p (a r)"), msg[step_slot(b, q)][:, 0:GS * RW],
                                  rows[b.slot][:, q * GS:(q + 1) * GS, :].rearrange("p g r -> p (g r)"), ALU.add).then_inc(msg_added, 1)

            def weigh(b, q):
                dve.wait_ge(relu_made, b.no * NG + q + 1)
                part = mes[step_slot(b, q)][:, :, :].rearrange("p (g h) r -> p g (h r)", g=GS)
                dve.tensor_tensor(part, part, bc(t.att08[:, :, :].rearrange("p h r -> p (h r)").unsqueeze(1), P, GS, RW), ALU.mult).then_inc(weighted, 1)

            def reduce(b, q):
                dve.wait_ge(weighted, b.no * NG + q + 1)
                if b.reuses and q == 0:
                    dve.wait_ge(dif_made, b.no - RING + 1)
                dve.tensor_reduce(score[b.slot][:, :, q * GS:(q + 1) * GS].rearrange("p h g -> p g h"),
                                  mes[step_slot(b, q)][:, :, :].rearrange("p (g h) r -> p g h r", h=H), AX, ALU.add).then_inc(scored, 1)

            def scores_gat(b):
                if b.some_before:
                    dve.wait_ge(scored, b.no)
                dve.wait_ge(msg_made, (b.no + 1) * NG)
                dve.tensor_reduce(raw[:, :, :], msg[b.slot][:, 0:3 * HG].rearrange("p (g k h) -> p g h k", k=3, h=H), AX,
                                  ALU.add).then_inc(msg_added, 1)
                dve.wait_ge(gathered[b.slot], (b.turn + 1) * G * 16)
                dve.wait_ge(msg_added, b.no + 1)
                dve.tensor_tensor(raw[:, :, :], raw[:, :, :], rows[b.slot][:, :, :].rearrange("p g (h r) -> p g h r", r=R)[:, :, :, C],
                                  ALU.add).then_inc(joined, 1)
                if b.reuses:
                    dve.wait_ge(dif_made, b.no - RING + 1)
                dve.wait_ge(joined, b.no + 1)
                dve.scalar_tensor_tensor(score[b.slot][:, :, :].rearrange("p h g -> p g h"), raw[:, :, :], SLOPE, raw[:, :, :], ALU.mult, ALU.max).then_inc(scored, 1)

            def scan(c, out, which, initial, done):
                r = res[c.slot]
                s = mx[0:HG, 0:P]
                if which == 0:
                    dve.tensor_tensor_scan(out[0:HG, :], r[0:HG, 0:P], s, initial, ALU.add, ALU.max).then_inc(done, 1)
                else:
                    dve.tensor_tensor_scan(out[0:HG, ::-1], r[0:HG, P:0:-1], s[:, ::-1], initial, ALU.add, ALU.max).then_inc(done, 1)

            def scan_steps(c):
                dve.wait_ge(turned, c.no + 1)
                dve.wait_ge(resets_in[c.slot], (c.turn + 1) * 16)
                if c.some_before:
                    dve.wait_ge(top_made, c.no)
                scan(c, fwd, 0, -BIG, scanned)
                scan(c, bwd, 1, -BIG, scanned)

            def chain_step(c, k, ins, wait=True):
                ins.then_inc(chain_vec, 1)
                if wait:
                    dve.wait_ge(chain_vec, c.no * 7 + k)

            def chain_steps(c):
                if c.some_before:
                    dve.wait_ge(inits_made, c.no)
                chain_step(c, 1, dve.tensor_copy(chain_m[0:1, 0, :, 0], chain[0:1, 0, :, G]), False)
                dve.wait_ge(ends_made, c.no + 1)
                ends = mx[0:1, ENDS:ENDS + 2 * P].rearrange("p (a b) -> p a b", a=2)[:, :, 0:HG].rearrange("p a (h g) -> p a h g", g=G)
                chain_step(c, 2, dve.tensor_copy(chain_m[0:1, 0, :, 1:G + 1], ends[:, 0]), False)
                chain_step(c, 3, dve.tensor_copy(chain_m[0:1, 1, :, G:0:-1], ends[:, 1]), False)
                dve.wait_ge(resets_kept, c.no + 1)
                chain_step(c, 4, dve.tensor_scalar(same[:, :], res[c.slot][0:1, 0:1], 0.0, None, ALU.is_equal))
                dve.tensor_tensor_scan(chain[:, :, :, :].rearrange("p a h g -> p (a h g)"), chain_r[:, :, :, :].rearrange("p a h g -> p (a h g)"),
                                       chain_m[:, :, :, :].rearrange("p a h g -> p (a h g)"), -BIG, ALU.add, ALU.max).then_inc(chain_vec, 1)

            def chain_results(c):
                dve.wait_ge(chain_vec, c.no * 7 + 5)
                dve.tensor_tensor(gap[0:1, 0, :], chain_m[0:1, 0, :, 0], chain[0:1, 1, :, G], ALU.subtract).then_inc(chain_vec, 1)
                dve.tensor_copy(before[0:1, 0, :, :], chain[0:1, 0, :, 0:G]).then_inc(chained, 1)
                dve.tensor_copy(before[0:1, 1, :, :], chain[0:1, 1, :, G - 1::-1]).then_inc(chain_vec, 1)
                dve.wait_ge(chain_vec, c.no * 7 + 7)
                dve.tensor_scalar(gap[0:1, 1, :], gap[0:1, 0, :], 0.0, same[:, 0:1], ALU.min, ALU.mult).then_inc(chained, 1)

            def rescan_steps(c):
                dve.wait_ge(inits_made, c.no + 1)
                if c.some_before:
                    dve.wait_ge(fac_made, c.no)
                dve.tensor_copy(init[0:HG, :], mx[0:HG, INITS:INITS + 2]).then_inc(rescanned, 1)
                dve.tensor_copy(fac_in[:, :], mx[:, GAPS:GAPS + H]).then_inc(inits_taken, 1)
                dve.wait_ge(rescanned, 3 * c.no + 1)
                scan(c, fwd, 0, init[0:HG, 0:1], rescanned)
                scan(c, bwd, 1, init[0:HG, 1:2], rescanned)

            def join_scans(c):
                dve.wait_ge(rescanned, 3 * (c.no + 1))
                if c.some_before:
                    dve.wait_ge(top_turned, c.no)
                dve.tensor_tensor(top[0:HG, :], fwd[0:HG, :], bwd[0:HG, :], ALU.max).then_inc(top_made, 1)

            def subtract_tops(c):
                dve.wait_ge(top_turned, c.no + 1)
                if c.some_before:
                    dve.wait_ge(prob_kept, c.no)
                tops = mx[:, 0:HG].rearrange("p (h g) -> p g h", g=G)
                dve.tensor_tensor(dif[:, :, :], score[c.slot][:, :, :].rearrange("p h g -> p g h"), tops, ALU.subtract).then_inc(dif_made, 1)
                if c.reuses:
                    dve.wait_ge(agg_made, (c.no - RING + 1) * NG)
                dve.tensor_tensor(val[c.slot][:, :, RW:RW + H], tops, bc(t.last_k[:, bass.ds(c.no * G, G)].unsqueeze(2), P, G, H),
                                  ALU.mult).then_inc(tops_kept, 1)

            def acc_of(win, width):
                return t.acc[:, bass.ds(win * VW, width)]

            def rescale(c, win):
                dve.wait_ge(fac_made, c.no + 1)
                if c.some_before:
                    dve.wait_ge(added, c.no * NG)
                a = acc_of(win, RW).rearrange("p (h r) -> p h r", r=R)
                dve.tensor_tensor(a, a, bc(fac[:, :].unsqueeze(2), P, H, R), ALU.mult).then_inc(rescaled, 1)

            def weigh_rows(c, q):
                g = c.no * NG + q
                if q == 0:
                    dve.wait_ge(prob_made, c.no + 1)
                part = slice(q * GS, (q + 1) * GS)
                p = prob[:, q * GS * H:(q + 1) * GS * H]
                dve.tensor_tensor(val[c.slot][:, part, 0:RW].rearrange("p g (h r) -> p g h r", r=R)[:, :, :, 0:C],
                                  rows[c.slot][:, part, :].rearrange("p g (h r) -> p g h r", r=R)[:, :, :, 0:C],
                                  bc(p.rearrange("p (g h) -> p g h", h=H).unsqueeze(3), P, GS, H, C), ALU.mult).then_inc(val_made, 1)

            def add_sums(c, q, win):
                dve.wait_ge(agg_made, c.no * NG + q + 1)
                if q == 0:
                    dve.wait_ge(rescaled, c.no + 1)
                else:
                    dve.wait_ge(added, c.no * NG + q)
                a = acc_of(win, VW)
                dve.tensor_tensor(a, agg[q % 2][:, 0:VW], a, ALU.add).then_inc(added, 1)

            def windows(step, n):
                return nc.values_load_multi_w_load_instructions(
                    t.wins[0:1, bass.ds(step, n)], engines=(DVE,), min_val=0, max_val=WINDOWS - 1,
                    skip_runtime_bounds_check_because="clamped when made")[1]

            def before_weigh(c, cc, q, wins):
                if cc:
                    add_sums(cc, q, wins[q])
                if c and q == 1:
                    chain_steps(c)
                if c and q == 2:
                    rescan_steps(c)
                if c and q == 3:
                    subtract_tops(c)

            def before_reduce(c, q, win):
                if c and q == 0:
                    scan_steps(c)
                if c and q == 1:
                    chain_results(c)
                if c and q == 2:
                    join_scans(c)
                if c and q == 4:
                    weigh_rows(c, 1)
                    rescale(c, win)

            def after_reduce(c, cc, q):
                if cc and q < 2:
                    weigh_rows(cc, q + 3)
                if c and q == 3:
                    weigh_rows(c, 0)
                if c and q == 4:
                    weigh_rows(c, 2)

            def batch(b):
                c, cc = behind(b, 1), behind(b, 2)
                wins = windows(cc.no * NG, NG + bool(c)) if cc else windows(0, 1) if c else [0]
                for q in range(NG):
                    if edge:
                        later(b, q, 1, add_rows)
                    before_weigh(c, cc, q, wins)
                    if edge and b.exists():
                        weigh(b, q)
                    before_reduce(c, q, wins[-1])
                    if edge and b.exists():
                        reduce(b, q)
                    if not edge and b.exists() and q == 4:
                        scores_gat(b)
                    after_reduce(c, cc, q)

            if edge:
                add_rows(FIRST, 0)
            run(dve, batch, 2)
def merge(nc, kit, io, t, lay, out_of, last_step):
    H, C, R, RW, DW, VW = lay.H, lay.C, lay.R, lay.RW, lay.DW, lay.VW
    edge = lay.edge
    n = lay.n + "m_"
    ATTR = RW + H
    with ExitStack() as ctx:
        def sb(name, shape):
            return kit.sb(n + name, shape, F32, ctx)

        def sem(name):
            return kit.sem(n + name, ctx)

        own = sb("own", [P, CH, RW])
        num = sb("num", [P, CH, RW])
        loop = sb("loop", [P, CH, H, C])
        sl = sb("sl", [P, CH, H])
        seen = sb("seen", [P, CH, H])
        old = sb("old", [P, CH, H])
        new = sb("new", [P, CH, H])
        down = sb("down", [P, 2, CH, H])
        fac = sb("fac", [P, 2, CH, H])
        den = sb("den", [P, CH, H])
        res = sb("res", [P, CH, D])
        bias = sb("bias", [P, D])
        raw = sb("raw", [P, CH, H])
        if edge:
            count = sb("count", [P, CH, 1])
            mean = sb("mean", [P, CH, DE])
            meanT = sb("meanT", [DE, CH * P])
            mes = sb("mes", [P, CH, RW])
            pos = sb("pos", [P, CH * H, C])
            turned = [kit.ps(n + f"turned{i}", [P, 512], F32, ctx) for i in range(2)]
            ee = [kit.ps(n + f"ee{i}", [P, 512], F32, ctx) for i in range(3)]
        else:
            x = sb("x", [P, CH, D])
        loaded, own_in, vec, act_done = sem("loaded"), sem("own_in"), sem("vec"), sem("act_done")
        turned_ready, meanT_ready, ee_ready, stored = sem("turned_ready"), sem("meanT_ready"), sem("ee_ready"), sem("stored")
        MEAN, MES, SCORE = (3, 7, 10) if edge else (0, 0, 2)
        DOWN = SCORE + 5
        OWN_USED = DOWN + 2
        DONE = DOWN + 8 - (0 if edge else -1)
        NA = 3 if edge else 2
        block = ctx.enter_context(nc.Block())

        @block.sync
        def _(sp):
            sp.dma_start(bias[:, :], bc(lay.bias_out, P, D)).then_inc(loaded, 16)

            def chunk(r, first, last=False):
                if not first:
                    sp.wait_ge(vec, (r - 1) * DONE + OWN_USED)
                    settle(sp)
                rows = bass.ds(r * CH * P, CH * P)
                sp.dma_start(own[:, :, :], lay.table[rows, :].rearrange("(w p) d -> p w d", p=P)).then_inc(own_in, 16)
                if not edge:
                    if not first:
                        sp.wait_ge(vec, r * DONE)
                        settle(sp)
                    sp.dma_start(x[:, :, :], lay.x_in[rows, :].rearrange("(w p) d -> p w d", p=P)).then_inc(own_in, 16)
                    sp.wait_ge(vec, (r + 1) * DONE)
                    settle(sp)
                    if not last:
                        sp.dma_start(io.out[rows, :].rearrange("(w p) d -> p w d", p=P), res[:, :, :]).then_inc(stored, 16)
                    else:
                        at = r * CH * P
                        full = (CH - 1) * P
                        sp.dma_start(io.out[at:at + full, :].rearrange("(w p) d -> p w d", p=P), res[:, 0:CH - 1, :]).then_inc(stored, 16)
                        sp.dma_start(io.out[at + full:NODES, :], res[0:LASTW, CH - 1, :]).then_inc(stored, 16)

            chunk(0, True)
            with sp.Fori(1, CHUNKS - 1) as r:
                chunk(r, False)
            chunk(CHUNKS - 1, False, True)
            if not edge:
                sp.wait_ge(stored, 16 * (CHUNKS + 1))

        @block.scalar
        def _(act):
            def chunk(r):
                if edge:
                    for half in range(2):
                        act.wait_ge(turned_ready, 2 * r + half + 1)
                        at, w = half * 4, 4 - half
                        act.activation(meanT[:, at * P:(at + w) * P], turned[half][0:DE, 0:w * P], ACT.Copy).then_inc(meanT_ready, 1)
                    act.wait_ge(vec, r * DONE + MES)
                    act.activation(pos[:, :, :], mes[:, :, :].rearrange("p w (h r) -> p (w h) r", r=R)[:, :, 0:C], ACT.Relu).then_inc(act_done, 1)
                act.wait_ge(vec, r * DONE + DOWN)
                act.activation(fac[:, :, :, :], down[:, :, :, :], ACT.Exp).then_inc(act_done, 1)

            chunk(0)
            with act.Fori(1, CHUNKS) as r:
                chunk(r)

        @block.tensor
        def _(pe):
            def chunk(r):
                pe.wait_ge(vec, r * DONE + MEAN)
                settle(pe)
                for w in range(CH):
                    half, at = divmod(w, 4)
                    ins = pe.transpose(turned[half][0:DE, at * P:(at + 1) * P], mean[:, w, :], t.ident[:, :])
                    if w in (3, CH - 1):
                        ins.then_inc(turned_ready, 1)
                pe.wait_ge(meanT_ready, 2 * (r + 1))
                for w in range(CH):
                    ins = pe.matmul(ee[w // 3][:, (w % 3) * RW:(w % 3 + 1) * RW], meanT[:, w * P:(w + 1) * P],
                                    t.we[:, :, :].rearrange("k h r -> k (h r)"), start=True, stop=True)
                ins.then_inc(ee_ready, 1)

            if edge:
                chunk(0)
                with pe.Fori(1, CHUNKS) as r:
                    chunk(r)

        @block.vector
        def _(dve):
            dve.wait_ge(loaded, 16)

            def chunk(r):
                k = [0]

                def step(ins, wait=True):
                    k[0] += 1
                    ins.then_inc(vec, 1)
                    if wait:
                        dve.wait_ge(vec, r * DONE + k[0])

                a = t.acc[:, bass.ds(r * CH * VW, CH * VW)].rearrange("p (w v) -> p w v", v=VW)
                dst = lay.dst_table[:, bass.ds(r * CH * DW, CH * DW)].rearrange("p (w v) -> p w v", v=DW)
                sums = a[:, :, 0:RW].rearrange("p w (h r) -> p w h r", r=R)
                own4 = own[:, :, :].rearrange("p w (h r) -> p w h r", r=R)
                if edge:
                    step(dve.tensor_scalar(count[:, :, :], a[:, :, ATTR + DE:ATTR + DE + 1], 1.0, None, ALU.max))
                    step(dve.reciprocal(count[:, :, :], count[:, :, :]))
                    step(dve.tensor_tensor(mean[:, :, :], a[:, :, ATTR:ATTR + DE], bc(count[:, :, :], P, CH, DE), ALU.mult), False)
                    assert k[0] == MEAN
                    dve.wait_ge(own_in, 16 * (r + 1))
                    dve.wait_ge(ee_ready, r + 1)
                    for i in range(3):
                        w = slice(3 * i, min(3 * i + 3, CH))
                        c = (w.stop - w.start) * RW
                        step(dve.tensor_tensor(mes[:, w, :].rearrange("p w v -> p (w v)"), ee[i][:, 0:c],
                                               own[:, w, :].rearrange("p w v -> p (w v)"), ALU.add), i == 2)
                    step(dve.tensor_tensor(mes[:, :, :], mes[:, :, :], dst, ALU.add), False)
                    assert k[0] == MES
                    dve.wait_ge(act_done, r * 2 + 1)
                    pos4 = pos[:, :, :].rearrange("p (w h) c -> p w h c", h=H)
                    step(dve.tensor_tensor(pos4, pos4, bc(t.att08[:, :, 0:C].unsqueeze(1), P, CH, H, C), ALU.mult))
                    step(dve.tensor_reduce(raw[:, :, :].rearrange("p w h -> p (w h)"), pos[:, :, :], AX, ALU.add))
                    step(dve.tensor_tensor(sl[:, :, :], raw[:, :, :], mes[:, :, :].rearrange("p w (h r) -> p w h r", r=R)[:, :, :, C], ALU.add))
                else:
                    dve.wait_ge(own_in, 32 * (r + 1))
                    step(dve.tensor_tensor(raw[:, :, :], own4[:, :, :, C], dst, ALU.add))
                    step(dve.scalar_tensor_tensor(sl[:, :, :], raw[:, :, :], SLOPE, raw[:, :, :], ALU.mult, ALU.max))
                assert k[0] == SCORE
                step(dve.tensor_scalar(seen[:, :, :], sums[:, :, :, C], 0.5, BIG, ALU.is_gt, ALU.mult))
                step(dve.scalar_tensor_tensor(old[:, :, :], seen[:, :, :], -BIG, a[:, :, RW:RW + H], ALU.add, ALU.add))
                step(dve.tensor_tensor(new[:, :, :], old[:, :, :], sl[:, :, :], ALU.max))
                step(dve.tensor_tensor(down[:, 0], old[:, :, :], new[:, :, :], ALU.subtract), False)
                step(dve.tensor_tensor(down[:, 1], sl[:, :, :], new[:, :, :], ALU.subtract), False)
                assert k[0] == DOWN
                dve.wait_ge(act_done, (r + 1) * (2 if edge else 1))
                num4 = num[:, :, :].rearrange("p w (h r) -> p w h r", r=R)
                step(dve.tensor_tensor(num4, sums, bc(fac[:, 0].unsqueeze(3), P, CH, H, R), ALU.mult), False)
                step(dve.tensor_tensor(loop[:, :, :, :], own4[:, :, :, 0:C], bc(fac[:, 1].unsqueeze(3), P, CH, H, C), ALU.mult))
                assert k[0] == OWN_USED
                step(dve.tensor_tensor(num4[:, :, :, 0:C], num4[:, :, :, 0:C], loop[:, :, :, :], ALU.add), False)
                step(dve.tensor_tensor(den[:, :, :], num4[:, :, :, C], fac[:, 1], ALU.add))
                step(dve.tensor_scalar(den[:, :, :], den[:, :, :], 1e-16, None, ALU.add))
                step(dve.reciprocal(den[:, :, :], den[:, :, :]))
                wide = bc(bias[:, :].unsqueeze(1), P, CH, D)
                step(dve.tensor_tensor(loop[:, :, :, :], num4[:, :, :, 0:C], bc(den[:, :, :].unsqueeze(3), P, CH, H, C), ALU.mult))
                flat = loop[:, :, :, :].rearrange("p w h c -> p w (h c)")
                if edge:
                    step(dve.tensor_tensor(t.gn[:, bass.ds(r * CH * D, CH * D)].rearrange("p (w d) -> p w d", d=D), flat, wide, ALU.add))
                else:
                    step(dve.tensor_tensor(flat, flat, wide, ALU.add))
                    dve.wait_ge(stored, 16 * r) if not isinstance(r, int) else None
                    step(dve.scalar_tensor_tensor(res[:, :, :], flat, 0.0, x[:, :, :], ALU.max, ALU.add))
                assert k[0] == DONE, (k[0], DONE)

            chunk(0)
            with dve.Fori(1, CHUNKS) as r:
                chunk(r)


def graph_norm(nc, kit, io, t, lay):
    with ExitStack() as ctx:
        def sb(name, shape):
            return kit.sb("g_" + name, shape, F32, ctx)

        def sem(name):
            return kit.sem("g_" + name, ctx)

        x = sb("x", [P, WINDOWS, D])
        sq = sb("sq", [P, WINDOWS * D])
        par = sb("par", [P, 3, D])
        valid = sb("valid", [P, P])
        col = sb("col", [P, 2, D])
        std = sb("std", [P, D])
        bank = [kit.ps(f"g_bank{i}", [P, 512], F32, ctx) for i in range(4)]
        loaded, x_in, masked, vec = sem("loaded"), sem("x_in"), sem("masked"), sem("vec")
        summed, squared, rooted, stored = sem("summed"), sem("squared"), sem("rooted"), sem("stored")
        block = ctx.enter_context(nc.Block())
        CENTERED, VAR, OUT = 5, 9, 14

        @block.gpsimd
        def _(pool):
            pool.memset(valid[:, :], 0.0).then_inc(masked, 1)
            pool.wait_ge(masked, 1)
            pool.memset(valid[0:LASTW, :], 1.0).then_inc(masked, 1)

        @block.sync
        def _(sp):
            for i, a in enumerate((io.gn_weight, io.gn_bias, io.gn_mean_scale)):
                sp.dma_start(par[:, i, :], bc(a, P, D)).then_inc(loaded, 16)
            sp.dma_start(x[:, :, :], io.x.rearrange("(w p) d -> p w d", p=P)).then_inc(x_in, 16)
            sp.wait_ge(vec, OUT)
            sp.dma_start(io.x1.rearrange("(w p) d -> p w d", p=P), x[:, :, :]).then_inc(stored, 16)
            sp.wait_ge(stored, 16)

        @block.tensor
        def _(pe):
            for i, src in enumerate((t.gn, sq)):
                if i == 0:
                    pe.wait_ge(masked, 2)
                else:
                    pe.wait_ge(squared, 1)
                for w in range(0, WINDOWS - 1, 4):
                    pe.matmul(bank[2 * i][:, :], t.ones[:, :], src[:, w * D:(w + 4) * D], start=w == 0, stop=w == WINDOWS - 5)
                pe.matmul(bank[2 * i + 1][:, 0:D], valid[:, :], src[:, (WINDOWS - 1) * D:WINDOWS * D], start=True, stop=True).then_inc(summed, 1)

        @block.scalar
        def _(act):
            act.wait_ge(vec, CENTERED)
            act.activation(sq[:, :], t.gn[:, :], ACT.Square).then_inc(squared, 1)
            act.wait_ge(vec, VAR)
            act.activation(std[:, :], col[:, 1, :], ACT.Sqrt).then_inc(rooted, 1)

        @block.vector
        def _(dve):
            n = [0]

            def step(ins, wait=True):
                n[0] += 1
                ins.then_inc(vec, 1)
                if wait:
                    dve.wait_ge(vec, n[0])

            def mean_of(i):
                dve.wait_ge(summed, i + 1)
                step(dve.tensor_reduce(col[:, i, :], bank[2 * i][:, :].rearrange("p (w d) -> p d w", d=D), AX, ALU.add))
                step(dve.tensor_tensor(col[:, i, :], col[:, i, :], bank[2 * i + 1][:, 0:D], ALU.add))

            g3 = t.gn[:, :].rearrange("p (w d) -> p w d", d=D)

            def wide(a):
                return bc(a.unsqueeze(1), P, WINDOWS, D)

            dve.wait_ge(loaded, 48)
            mean_of(0)
            step(dve.tensor_scalar(col[:, 0, :], col[:, 0, :], 1.0 / NODES, None, ALU.mult))
            step(dve.tensor_tensor(col[:, 0, :], col[:, 0, :], par[:, 2, :], ALU.mult))
            step(dve.tensor_tensor(g3, g3, wide(col[:, 0, :]), ALU.subtract), False)
            assert n[0] == CENTERED
            dve.wait_ge(vec, CENTERED)
            mean_of(1)
            step(dve.tensor_scalar(col[:, 1, :], col[:, 1, :], 1.0 / NODES, None, ALU.mult))
            step(dve.tensor_scalar(col[:, 1, :], col[:, 1, :], EPS, None, ALU.add))
            assert n[0] == VAR
            dve.wait_ge(rooted, 1)
            step(dve.reciprocal(std[:, :], std[:, :]))
            step(dve.tensor_tensor(std[:, :], std[:, :], par[:, 0, :], ALU.mult))
            step(dve.tensor_tensor(g3, g3, wide(std[:, :]), ALU.mult))
            step(dve.tensor_tensor(g3, g3, wide(par[:, 1, :]), ALU.add))
            dve.wait_ge(x_in, 16)
            step(dve.scalar_tensor_tensor(x[:, :, :], g3, 0.0, x[:, :, :], ALU.max, ALU.add), False)
            assert n[0] == OUT


def layer(kit, n, H, table, x_in, edge, ctx):
    lay = Names()
    lay.n, lay.H, lay.C, lay.R = n, H, D // H, D // H + 1
    lay.RW = H * lay.R
    lay.DW = lay.RW if edge else H
    lay.VW = lay.RW + H + (DE + 1 if edge else 0)
    lay.table, lay.x_in, lay.edge = table, x_in, edge
    lay.lin = SLOPE if edge else 1.0
    return lay


def program(nc, io):
    with ExitStack() as ctx:
        kit, t = Kit(nc, ctx), Names()
        io.tab_i, io.tab_f = kit.dram("tab_i", (2, KP), I32), kit.dram("tab_f", (2, KT))
        io.keys, io.resets = kit.dram("keys", (1 + KP * GE,)), kit.dram("resets", (KP * GE + P,))
        io.resets_r, io.resets_h = kit.dram("resets_r", (KT, P + 1)), kit.dram("resets_h", (BATCHES, HEADS, G, P + 1))
        io.x1 = kit.dram("x1", (NP, D))
        l0 = layer(kit, "gatv2", 4, kit.dram("table0", (NP, 4 * 33)), io.x, True, ctx)
        l1 = layer(kit, "gat", 8, kit.dram("table1", (NP, 8 * 17)), io.x1, False, ctx)
        t.ident, t.ones = kit.sb("ident", [P, P]), kit.sb("ones", [P, P])
        t.iota_i, t.iota = kit.sb("iota_i", [P, P], I32), kit.sb("iota", [P, P])
        rows = kit.sb("step_rows", [97, KT], I32)
        t.groups, t.wins = rows[0:1, 0:KP], rows[32:33, 0:KP]
        t.rsum_f, t.rsum_b = rows[64:65, :].bitcast(F32), rows[96:97, :].bitcast(F32)
        t.src_k, t.rel_k = kit.sb("src_k", [P, KT], mybir.dt.int16), kit.sb("rel_k", [P, KT], BF16)
        t.last_k = kit.sb("last_k", [P, KT], BF16)
        constants(nc, kit, t)
        step_tables(nc, kit, io, t)
        with ExitStack() as part:
            t.gn = None
            with ExitStack() as low:
                l0.dst_table = kit.sb("xr", [P, WINDOWS * l0.DW], F32, low)
                t.we, t.att08 = kit.sb("we", [DE, 4, 33], F32, low), kit.sb("att08", [P, 4, 33], F32, low)
                with ExitStack() as w:
                    both = kit.sb("w0", [P, 8, 33], F32, w)
                    l0.bias = kit.sb("b0", [1, 2, 4, 33], F32, w)
                    l0.wcat = both[:, :, :].rearrange("p h r -> p (h r)")
                    l0.mats = [(io.wl, io.bl, P, io.att, both[:, 0:4, :], True), (io.wr, io.br, P, io.att, both[:, 4:8, :], True),
                               (io.we, None, DE, io.att, t.we, True)]
                    load_weights(nc, kit, io, t, l0)
                    project(nc, kit, io, t, l0)
                t.acc = kit.sb("acc0", [P, WINDOWS * l0.VW], F32, low)
                edges(nc, kit, io, t, l0)
                t.gn = kit.sb("gn", [P, WINDOWS * D], F32, low)
                l0.bias_out = io.bias_out0
                merge(nc, kit, io, t, l0, None, None)
                graph_norm(nc, kit, io, t, l0)
        l1.dst_table = kit.sb("a_dst", [P, WINDOWS * l1.DW])
        with ExitStack() as w:
            cat = kit.sb("w1", [P, l1.RW + l1.DW], F32, w)
            l1.bias, l1.wcat = None, cat[:, :]
            to = cat[:, 0:l1.RW].rearrange("p (h r) -> p h r", r=l1.R)
            l1.mats = [(io.w1, None, P, io.att_src, to, True),
                       (io.w1, None, P, io.att_dst, cat[:, l1.RW:l1.RW + l1.DW].rearrange("p (h r) -> p h r", r=1), False)]
            load_weights(nc, kit, io, t, l1)
            project(nc, kit, io, t, l1)
        t.acc = kit.sb("acc1", [P, WINDOWS * l1.VW])
        edges(nc, kit, io, t, l1)
        l1.bias_out = io.bias1
        merge(nc, kit, io, t, l1, None, None)


def kernel(**inputs):
    import numpy as np
    import concourse.bacc as bacc
    from concourse.bass_utils import run_bass_kernel_spmd as run

    def arr(name):
        return np.asarray(inputs[name])

    x = np.zeros((NP, D), np.float32)
    x[:NODES] = arr("x")
    src, dst = np.zeros(GP * GE, np.int32), np.full(GP * GE, NOWHERE, np.int32)
    src[:EDGES], dst[:EDGES] = arr("src"), arr("dst")
    attr = np.zeros((GP * GE, DE), np.float32)
    attr[:EDGES] = arr("edge_attr_64")
    dst = dst.reshape(GP, GE)

    def row(name):
        return np.ascontiguousarray(arr(name).reshape(1, D))

    data = {
        "x": x, "src_rows": src.reshape(GP, GE), "dst_rows": dst, "dst_lasts": np.ascontiguousarray(dst[:GROUPS, -1])[None],
        "attr": attr, "attrT": np.ascontiguousarray(attr.T),
        "wl": arr("L0_gnn_Wl"), "bl": row("L0_gnn_bl"), "wr": arr("L0_gnn_Wr"), "br": row("L0_gnn_br"), "we": arr("L0_gnn_We"),
        "att": row("L0_gnn_att"), "bias_out0": row("L0_gnn_bias_out"), "gn_weight": row("L0_gnn_gn_weight"),
        "gn_bias": row("L0_gnn_gn_bias"), "gn_mean_scale": row("L0_gnn_gn_mean_scale"),
        "w1": arr("L1_gnn_W"), "att_src": row("L1_gnn_att_src"), "att_dst": row("L1_gnn_att_dst"), "bias1": row("L1_gnn_bias"),
    }
    nc = bacc.Bacc("TRN2", target_bir_lowering=False, num_devices=1)

    def given(name):
        a = data[name]
        return nc.dram_tensor("in_" + name, a.shape, mybir.dt.from_np(a.dtype), kind="ExternalInput").ap()

    io = Names()
    io.x = given("x")
    io.src_rows = given("src_rows")
    io.dst_rows = given("dst_rows")
    io.dst_lasts = given("dst_lasts")
    io.attr = given("attr")
    io.attrT = given("attrT")
    io.wl = given("wl")
    io.bl = given("bl")
    io.wr = given("wr")
    io.br = given("br")
    io.we = given("we")
    io.att = given("att")
    io.bias_out0 = given("bias_out0")
    io.gn_weight = given("gn_weight")
    io.gn_bias = given("gn_bias")
    io.gn_mean_scale = given("gn_mean_scale")
    io.w1 = given("w1")
    io.att_src = given("att_src")
    io.att_dst = given("att_dst")
    io.bias1 = given("bias1")
    io.out = nc.dram_tensor("out", (NODES, D), F32, kind="ExternalOutput").ap()
    program(nc, io)
    r = run(nc, [{"in_" + name: a for name, a in data.items()}], core_ids=[0])
    return r.results[0]["out"]
```

```python
from contextlib import ExitStack

import concourse.bass as bass
from concourse import mybir

F32 = mybir.dt.float32
I32 = mybir.dt.int32
BF16 = mybir.dt.bfloat16
ALU = mybir.AluOpType
ACT = mybir.ActivationFunctionType
AX = mybir.AxisListType.X
DVE, PE, SPE = mybir.EngineType.DVE, mybir.EngineType.PE, mybir.EngineType.SP

P = 128
NODES = 6250
EDGES = 206250
D = 128
DE = 64
WINDOWS = -(-NODES // P)
NP = WINDOWS * P
LASTW = NODES - (WINDOWS - 1) * P
GS = 3
GE = GS * P
GROUPS = -(-EDGES // GE)
GP = GROUPS + 1
NG = 5
G = NG * GS
RING = 3
BATCHES = -(-(GROUPS + WINDOWS - 1) // NG)
TURNS = BATCHES // RING
KC = -(-(BATCHES + 2) * NG // P)
KP = KC * P
KT = KP * GS
NOWHERE = 1 << 14
BIG = 1e30
HEADS = 8
SLOPE = 0.2
EPS = 1e-5
CH = 7
CHUNKS = WINDOWS // CH
assert CHUNKS * CH == WINDOWS


class Names:
    pass


def bc(ap, *shape):
    return ap.to_broadcast(list(shape))


def settle(eng):
    eng.nop(nofuse=True)


class Kit:

    def __init__(self, nc, ctx):
        self.nc, self.ctx, self.used = nc, ctx, {}

    def own(self, name):
        self.used[name] = self.used.get(name, 0) + 1
        return name if self.used[name] == 1 else f"{name}_{self.used[name]}"

    def sb(self, name, shape, dt=F32, ctx=None):
        return (ctx or self.ctx).enter_context(self.nc.sbuf_tensor(self.own(name), shape, dt))

    def ps(self, name, shape, dt=F32, ctx=None):
        return (ctx or self.ctx).enter_context(self.nc.psum_tensor(self.own(name), shape, dt))

    def sem(self, name, ctx=None):
        return self.ctx.enter_context(self.nc.semaphore(self.own(name)))

    def dram(self, name, shape, dt=F32):
        return self.nc.dram_tensor(name, shape, dt).ap()


def constants(nc, kit, t):
    made = kit.sem("c_made")
    sel = kit.sem("c_sel")
    with nc.Block() as block:
        @block.gpsimd
        def _(pool):
            pool.memset(t.ident[:, :], 0.0).then_inc(made, 1)
            pool.memset(t.ones[:, :], 1.0).then_inc(made, 1)
            pool.iota(t.iota_i[:, :], [[1, P]], base=0, channel_multiplier=0).then_inc(made, 1)
            pool.memset(t.valid[:, :], 0.0).then_inc(made, 1)
            pool.wait_ge(made, 4)
            pool.memset(t.valid[0:LASTW, :], 1.0).then_inc(sel, 1)
            pool.affine_select(out=t.ident[:, :], in_=t.ident[:, :], compare_op=ALU.not_equal, fill=1.0,
                               base=0, pattern=[[-1, P]], channel_multiplier=1).then_inc(sel, 1)
            pool.tensor_copy(t.iota[:, :], t.iota_i[:, :]).then_inc(sel, 1)
            pool.wait_ge(sel, 3)


def step_tables(nc, kit, io, t):
    with ExitStack() as ctx:
        def sb(name, shape, dt=F32):
            return kit.sb(name, shape, dt, ctx)

        lasts_i = sb("lasts_i", [P, GROUPS], I32)
        lastw = sb("lastw", [P, GROUPS], I32)
        group_no = sb("group_no", [P, GROUPS], I32)
        ends_at = sb("ends_at", [P, GROUPS])
        before = sb("before", [P, GROUPS])
        step_no_i = sb("step_no_i", [P, KC], I32)
        step_no = sb("step_no", [P, KC])
        group_f = sb("group_f", [P, KC])
        group_i = sb("group_i", [P, KC], I32)
        win_f = sb("win_f", [P, KC])
        win_i = sb("win_i", [P, KC], I32)
        srcr = sb("srcr", [P, KC, GE], I32)
        dstr = sb("dstr", [P, KC, GE], I32)
        srcf = sb("srcf", [P, KC, GE])
        dstf = sb("dstf", [P, KC, GE])
        rel = sb("rel", [P, KC, GE])
        inw = sb("inw", [P, KC, GE])
        key = sb("key", [P, KC, GE])
        prev = sb("prev", [P, KC, GE])
        reset = sb("reset", [P, KC, GE])
        after = sb("after", [P, KC, GE])
        last = sb("last", [P, KC, GE])
        tail = sb("tail", [1, P])
        sums = sb("sums", [P, 2, KC * GS])
        turned = [kit.ps(f"turned{i}", [P, 512], F32, ctx) for i in range(2)]
        loaded, numbered, vec = kit.sem("t_loaded"), kit.sem("t_numbered"), kit.sem("t_vec")
        rows_src, rows_dst = kit.sem("t_rows_src"), kit.sem("t_rows_dst")
        keys_out, keys_in = kit.sem("t_keys_out"), kit.sem("t_keys_in")
        resets_out, resets_in = kit.sem("t_resets_out"), kit.sem("t_resets_in")
        rows_out = kit.sem("t_rows_out")
        tabs_out, tabs_in = kit.sem("t_tabs_out"), kit.sem("t_tabs_in")
        turned_ready, turned_used = kit.sem("t_turned_ready"), kit.sem("t_turned_used")
        FOUND = KC + 9
        KEYED, RESET, SUMMED, FLAGGED = FOUND + 10, FOUND + 12, FOUND + 14, FOUND + 15
        block = ctx.enter_context(nc.Block())

        def by_tile(a):
            return a[:, :, :].rearrange("p c (j e) -> p (c j) e", e=P)

        @block.gpsimd
        def _(pool):
            pool.iota(group_no[:, :], [[1, GROUPS]], base=0, channel_multiplier=0).then_inc(numbered, 1)
            pool.iota(step_no_i[:, :], [[P, KC]], base=0, channel_multiplier=1).then_inc(numbered, 1)
            pool.wait_ge(vec, FOUND)
            for rows, table, done in ((dstr, io.dst_rows, rows_dst), (srcr, io.src_rows, rows_src)):
                for c in range(KC):
                    pool.indirect_dma_start(rows[:, c, :], None, table,
                                            bass.IndirectOffsetOnAxis(group_i[:, c:c + 1], 0)).then_inc(done, 16)

        @block.sync
        def _(sp):
            def steps_of(flat, at=0):
                return flat[at:at + KP * GE].rearrange("(c p e) -> p c e", p=P, e=GE)

            sp.dma_start(lasts_i[:, :], bc(io.dst_lasts, P, GROUPS)).then_inc(loaded, 16)
            with nc.allow_non_contiguous_dma(reason="small tables"):
                sp.wait_ge(vec, FOUND)
                sp.dma_start(io.tab_i[0, :].rearrange("(c p) -> p c", p=P), group_i[:, :]).then_inc(tabs_out, 16)
                sp.dma_start(io.tab_i[1, :].rearrange("(c p) -> p c", p=P), win_i[:, :]).then_inc(tabs_out, 16)
                sp.wait_ge(vec, KEYED)
                sp.dma_start(steps_of(io.keys, 1), key[:, :, :]).then_inc(keys_out, 16)
                sp.dma_start(io.keys[0:1].rearrange("(a b) -> a b", a=1), tail[0:1, 0:1]).then_inc(keys_out, 16)
                sp.wait_ge(keys_out, 32)
                sp.dma_start(prev[:, :, :], steps_of(io.keys)).then_inc(keys_in, 16)
                sp.wait_ge(vec, RESET)
                sp.dma_start(steps_of(io.resets), reset[:, :, :]).then_inc(resets_out, 16)
                sp.dma_start(io.resets[KP * GE:KP * GE + P].rearrange("(a b) -> a b", a=1), tail[0:1, :]).then_inc(resets_out, 16)
                sp.wait_ge(resets_out, 32)
                sp.dma_start(after[:, :, :], steps_of(io.resets, 1)).then_inc(resets_in, 16)
                sp.wait_ge(resets_in, 16)
                rows = io.resets_r.rearrange("(c p j) e -> p c j e", p=P, j=GS)
                for c in range(KC):
                    sp.dma_start(rows[:, c, :, 0:P], reset[:, c, :].rearrange("p (j e) -> p j e", e=P)).then_inc(rows_out, 16)
                    sp.dma_start(rows[:, c, :, P:P + 1], after[:, c, :].rearrange("p (j e) -> p j e", e=P)[:, :, P - 1:P]).then_inc(rows_out, 16)
                sp.wait_ge(vec, SUMMED)
                for i in range(2):
                    sp.dma_start(io.tab_f[i, :].rearrange("(c p j) -> p c j", p=P, j=GS),
                                 sums[:, i, :].rearrange("p (c j) -> p c j", j=GS)).then_inc(tabs_out, 16)
            sp.wait_ge(tabs_out, 64)
            for row, table in ((t.groups, io.tab_i[0:1, :]), (t.wins, io.tab_i[1:2, :]),
                               (t.rsum_f, io.tab_f[0:1, :]), (t.rsum_b, io.tab_f[1:2, :])):
                sp.dma_start(row, table).then_inc(tabs_in, 16)
            sp.wait_ge(rows_out, 32 * KC)
            sp.wait_ge(tabs_in, 64)

        @block.vector
        def _(dve):
            n = [0]

            def step(ins, wait=True):
                n[0] += 1
                ins.then_inc(vec, 1)
                if wait:
                    dve.wait_ge(vec, n[0])

            dve.wait_ge(loaded, 16)
            dve.wait_ge(numbered, 2)
            step(dve.tensor_scalar(lastw[:, :], lasts_i[:, :], 7, None, ALU.arith_shift_right), False)
            step(dve.tensor_copy(step_no[:, :], step_no_i[:, :]))
            step(dve.tensor_scalar(ends_at[:, :], lastw[:, :], float(WINDOWS - 1), 0.0, ALU.min, ALU.max))
            step(dve.tensor_tensor(ends_at[:, :], ends_at[:, :], group_no[:, :], ALU.add))
            for c in range(KC):
                step(dve.tensor_scalar(before[:, :], ends_at[:, :], step_no[:, c:c + 1], 0.0, ALU.is_lt, ALU.add,
                                       accum_out=group_f[:, c:c + 1]))
            step(dve.tensor_tensor(win_f[:, :], step_no[:, :], group_f[:, :], ALU.subtract))
            step(dve.tensor_scalar(win_f[:, :], win_f[:, :], float(WINDOWS - 1), 0.0, ALU.min, ALU.max))
            step(dve.tensor_copy(group_i[:, :], group_f[:, :]), False)
            step(dve.tensor_copy(win_i[:, :], win_f[:, :]), False)
            step(dve.memset(tail[:, :], -BIG))
            assert n[0] == FOUND
            dve.wait_ge(rows_dst, 16 * KC)
            step(dve.tensor_copy(dstf[:, :, :], dstr[:, :, :]))
            step(dve.scalar_tensor_tensor(rel[:, :, :], bc(win_f[:, :].unsqueeze(2), P, KC, GE), -float(P), dstf[:, :, :],
                                          ALU.mult, ALU.add))
            step(dve.tensor_scalar(inw[:, :, :], rel[:, :, :], 0.0, None, ALU.is_ge), False)
            step(dve.tensor_scalar(prev[:, :, :], rel[:, :, :], float(P), None, ALU.is_lt))
            step(dve.tensor_tensor(inw[:, :, :], inw[:, :, :], prev[:, :, :], ALU.mult))
            one_more = bc(step_no[:, :].unsqueeze(2), P, KC, GE)
            step(dve.scalar_tensor_tensor(key[:, :, :], one_more, 1.0, dstf[:, :, :], ALU.add, ALU.add))
            step(dve.tensor_tensor(key[:, :, :], key[:, :, :], inw[:, :, :], ALU.mult))
            step(dve.scalar_tensor_tensor(reset[:, :, :], one_more, 1.0, key[:, :, :], ALU.add, ALU.subtract))
            step(dve.tensor_scalar(key[:, :, :], reset[:, :, :], -1.0, None, ALU.mult), False)
            dve.wait_ge(rows_src, 16 * KC)
            step(dve.tensor_copy(srcf[:, :, :], srcr[:, :, :]))
            assert n[0] == KEYED
            dve.wait_ge(keys_in, 16)
            step(dve.tensor_tensor(reset[:, :, :], key[:, :, :], prev[:, :, :], ALU.not_equal))
            step(dve.tensor_scalar(reset[:, :, :], reset[:, :, :], -BIG, None, ALU.mult))
            assert n[0] == RESET
            dve.wait_ge(resets_in, 16)
            step(dve.tensor_reduce(sums[:, 0, :], by_tile(reset), AX, ALU.add), False)
            step(dve.tensor_reduce(sums[:, 1, :], by_tile(after), AX, ALU.add))
            assert n[0] == SUMMED
            step(dve.tensor_scalar(last[:, :, :], after[:, :, :], 0.0, None, ALU.is_lt))
            assert n[0] == FLAGGED

        @block.scalar
        def _(act):
            for i in range(3 * KC):
                what, c = divmod(i, KC)
                act.wait_ge(turned_ready, i + 1)
                out = (t.rel_k, t.src_k, t.last_k)[what][:, c * GE:(c + 1) * GE].rearrange("p (k j) -> p j k", j=GS)
                act.activation(out, turned[i % 2][:, 0:GE].rearrange("p (j k) -> p j k", j=GS), ACT.Copy).then_inc(turned_used, 1)

        @block.tensor
        def _(pe):
            for i in range(3 * KC):
                what, c = divmod(i, KC)
                if c == 0:
                    pe.wait_ge(vec, (KEYED, KEYED, FLAGGED)[what])
                if i >= 2:
                    pe.wait_ge(turned_used, i - 1)
                for j in range(GS):
                    ins = pe.transpose(turned[i % 2][:, j * P:(j + 1) * P], (rel, srcf, last)[what][:, c, j * P:(j + 1) * P], t.ident[:, :])
                ins.then_inc(turned_ready, 1)
def load_weights(nc, kit, io, t, lay):
    H, C, R = lay.H, lay.C, lay.R
    with ExitStack() as ctx:
        def sb(name, shape):
            return kit.sb(f"{lay.n}_{name}", shape, F32, ctx)

        mats = lay.mats
        prod = sb("prod", [P, D])
        raw = sb("raw", [P, D])
        att = sb("att", [P, len(mats), D])
        loaded, vec = kit.sem(f"{lay.n}w_loaded"), kit.sem(f"{lay.n}w_vec")
        loads = sum(3 if b is not None else 2 for _, b, _, _, _, _ in mats)
        block = ctx.enter_context(nc.Block())

        @block.sync
        def _(sp):
            for i, (w, b, rows, a, to, keep) in enumerate(mats):
                dst = to[0:rows, :, 0:C] if keep else raw[0:rows, :].rearrange("p (h c) -> p h c", h=H)
                with nc.allow_non_contiguous_dma(reason="weights, once"):
                    sp.dma_start(dst, w.rearrange("k (h c) -> k h c", h=H)).then_inc(loaded, 16)
                    sp.dma_start(att[:, i, :], bc(a, P, D)).then_inc(loaded, 16)
                    if b is not None:
                        sp.dma_start(lay.bias[0:1, i, :, 0:C], b.rearrange("o (h c) -> o h c", h=H)).then_inc(loaded, 16)

        @block.vector
        def _(dve):
            n = [0]

            def step(ins):
                n[0] += 1
                ins.then_inc(vec, 1)
                dve.wait_ge(vec, n[0])

            dve.wait_ge(loaded, 16 * loads)
            for i, (w, b, rows, a, to, keep) in enumerate(mats):
                src = to[0:rows, :, 0:C] if keep else raw[0:rows, :].rearrange("p (h c) -> p h c", h=H)
                col = to[0:rows, :, C] if keep else to[0:rows, :, 0]
                last = bc(col.unsqueeze(2), rows, H, 1)
                for src, rows, last in [(src, rows, last)] + (
                        [(lay.bias[0:1, i, :, 0:C], 1, lay.bias[0:1, i, :, C:C + 1])] if b is not None else []):
                    pr = prod[0:rows, :].rearrange("p (h c) -> p h c", h=H)
                    step(dve.tensor_tensor(pr, src, att[0:rows, i, :].rearrange("p (h c) -> p h c", h=H), ALU.mult))
                    step(dve.tensor_reduce(last, pr, AX, ALU.add))
                    if lay.lin != 1.0:
                        step(dve.tensor_scalar(last, last, lay.lin, None, ALU.mult))
            if lay.edge:
                step(dve.memset(t.att08[:, :, C:C + 1], 1.0))
                step(dve.tensor_scalar(t.att08[:, :, 0:C], att[:, 0, :].rearrange("p (h c) -> p h c", h=H), 1.0 - SLOPE, None, ALU.mult))


def project(nc, kit, io, t, lay):
    RW, DW = lay.RW, lay.DW
    BW = RW + DW
    n = lay.n + "p_"
    with ExitStack() as ctx:
        def sb(name, shape):
            return kit.sb(n + name, shape, F32, ctx)

        def sem(name):
            return kit.sem(n + name, ctx)

        x = sb("x", [P, CH, D])
        xc = sb("xc", [P, CH, D])
        sq = sb("sq", [P, CH, D])
        xn = sb("xn", [P, CH, D])
        hT = sb("hT", [P, CH * P])
        mean = sb("mean", [P, CH])
        var = sb("var", [P, CH])
        std = sb("std", [P, CH])
        stage = sb("stage", [P, CH, RW])
        bias = sb("bias", [P, BW])
        turned = [kit.ps(n + f"turned{i}", [P, 512], F32, ctx) for i in range(2)]
        out = [kit.ps(n + f"out{i}", [P, 512], F32, ctx) for i in range(2)]
        x_in, stored = sem("x_in"), sem("stored")
        vec, squared, rooted = sem("vec"), sem("squared"), sem("rooted")
        h_turned, h_ready = sem("h_turned"), sem("h_ready")
        made = [sem("made_even"), sem("made_odd")]
        taken = [sem("taken_even"), sem("taken_odd")]
        if lay.bias is not None:
            spread = sem("spread")
        MADE = [(CH + 1) // 2, CH // 2]
        DVE_TAKES, ACT_TAKES = ((1,), (0,)) if lay.bias is None else ((0, 1), ())
        CENTERED, SPREAD, SCALED, NV = 3, 5, 7, 7
        block = ctx.enter_context(nc.Block())

        @block.gpsimd
        def _(pool):
            def load(r, first=False):
                if not first:
                    pool.wait_ge(vec, (r - 1) * NV + CENTERED)
                    settle(pool)
                pool.dma_start(x[:, :, :], lay.x_in[bass.ds(r * CH * P, CH * P), :].rearrange("(w p) d -> p w d", p=P)).then_inc(x_in, 16)

            load(0, True)
            with pool.Fori(1, CHUNKS) as r:
                load(r)

        @block.sync
        def _(sp):
            def store(r):
                for e in range(2):
                    sp.wait_ge(taken[e], (r + 1) * MADE[e])
                    settle(sp)
                sp.dma_start(lay.table[bass.ds(r * CH * P, CH * P), :].rearrange("(w p) d -> p w d", p=P), stage[:, :, :]).then_inc(stored, 16)

            store(0)
            with sp.Fori(1, CHUNKS) as r:
                store(r)
            sp.wait_ge(stored, 16 * CHUNKS)

        def take(eng, copy, parities, r, first):
            if parities and not first:
                eng.wait_ge(stored, 16 * r)
            for w in range(CH):
                e = w % 2
                if e in parities:
                    eng.wait_ge(made[e], r * MADE[e] + w // 2 + 1)
                    copy(stage[:, w, :], out[e][:, 0:RW], bias[:, 0:RW])
                    copy(lay.dst_table[:, bass.ds((r * CH + w) * DW, DW)], out[e][:, RW:BW], bias[:, RW:BW]).then_inc(taken[e], 1)

        @block.vector
        def _(dve):
            def normalise(r, first=False):
                k = [0]

                def step(ins, wait=True):
                    k[0] += 1
                    ins.then_inc(vec, 1)
                    if wait:
                        dve.wait_ge(vec, r * NV + k[0])

                def wide(a):
                    return bc(a[:, :].unsqueeze(2), P, CH, D)

                dve.wait_ge(x_in, 16 * (r + 1))
                step(dve.tensor_reduce(mean[:, :], x[:, :, :], AX, ALU.add))
                step(dve.tensor_scalar(mean[:, :], mean[:, :], 1.0 / D, None, ALU.mult))
                step(dve.tensor_tensor(xc[:, :, :], x[:, :, :], wide(mean), ALU.subtract), False)
                dve.wait_ge(squared, r + 1)
                step(dve.tensor_reduce(var[:, :], sq[:, :, :], AX, ALU.add))
                step(dve.tensor_scalar(var[:, :], var[:, :], 1.0 / D, EPS, ALU.mult, ALU.add), False)
                dve.wait_ge(rooted, r + 1)
                step(dve.reciprocal(std[:, :], std[:, :]))
                if not first:
                    dve.wait_ge(h_turned, 2 * r)
                step(dve.tensor_tensor(xn[:, :, :], xc[:, :, :], wide(std), ALU.mult), False)

            def copy(out, rows, bias):
                if lay.bias is None:
                    return dve.tensor_copy(out, rows)
                return dve.tensor_tensor(out, rows, bias, ALU.add)

            if lay.bias is not None:
                dve.wait_ge(spread, 1)
                dve.tensor_copy(bias[:, :], out[0][:, 0:BW]).then_inc(spread, 1)
                dve.wait_ge(spread, 2)
            normalise(0, True)
            normalise(1)
            take(dve, copy, DVE_TAKES, 0, True)
            with dve.Fori(2, CHUNKS) as r:
                normalise(r)
                take(dve, copy, DVE_TAKES, r - 1, False)
            take(dve, copy, DVE_TAKES, CHUNKS - 1, False)

        @block.scalar
        def _(act):
            def spreads(r):
                act.wait_ge(vec, r * NV + CENTERED)
                act.activation(sq[:, :, :], xc[:, :, :], ACT.Square).then_inc(squared, 1)
                act.wait_ge(vec, r * NV + SPREAD)
                act.activation(std[:, :], var[:, :], ACT.Sqrt).then_inc(rooted, 1)

            def relu(r, first=False):
                if not first:
                    for e in range(2):
                        act.wait_ge(made[e], r * MADE[e])
                for half in range(2):
                    act.wait_ge(h_turned, 2 * r + half + 1)
                    w = CH // 2 + 1 if half == 0 else CH // 2
                    at = half * (CH // 2 + 1)
                    act.activation(hT[:, at * P:(at + w) * P], turned[half][:, 0:w * P], ACT.Relu).then_inc(h_ready, 1)

            def copy(out, rows, bias):
                return act.activation(out, rows, ACT.Copy)

            spreads(0)
            relu(0, True)
            spreads(1)
            take(act, copy, ACT_TAKES, 0, True)
            with act.Fori(2, CHUNKS) as r:
                relu(r - 1)
                spreads(r)
                take(act, copy, ACT_TAKES, r - 1, False)
            relu(CHUNKS - 1)
            take(act, copy, ACT_TAKES, CHUNKS - 1, False)

        @block.tensor
        def _(pe):
            def chunk(r, first=False):
                pe.wait_ge(vec, r * NV + SCALED)
                if not first:
                    pe.wait_ge(h_ready, 2 * r)
                for w in range(CH):
                    half, at = divmod(w, CH // 2 + 1)
                    ins = pe.transpose(turned[half][:, at * P:(at + 1) * P], xn[:, w, :], t.ident[:, :])
                    if w in (CH // 2, CH - 1):
                        ins.then_inc(h_turned, 1)
                for w in range(CH):
                    half, e = w // (CH // 2 + 1), w % 2
                    if w in (0, CH // 2 + 1):
                        pe.wait_ge(h_ready, 2 * r + half + 1)
                    if w >= 2:
                        pe.wait_ge(taken[e], r * MADE[e] + w // 2)
                    elif not first:
                        pe.wait_ge(taken[e], r * MADE[e])
                    lhs = hT[:, w * P:(w + 1) * P]
                    pe.matmul(out[e][:, 0:BW], lhs, lay.wcat[:, 0:BW], start=True, stop=True).then_inc(made[e], 1)

            if lay.bias is not None:
                pe.matmul(out[0][:, 0:BW], t.ones[0:1, :], lay.bias[0:1, :, :, :].rearrange("p a h c -> p (a h c)"),
                          start=True, stop=True).then_inc(spread, 1)
                pe.wait_ge(spread, 2)
            chunk(0, True)
            with pe.Fori(1, CHUNKS) as r:
                chunk(r)
class Batch:

    def __init__(self, no, slot, turn):
        self.no, self.slot, self.turn = no, slot, turn
        self.reuses = not isinstance(no, int) or no >= RING
        self.some_before = not isinstance(no, int) or no > 0

    def before(self):
        if self.slot:
            return Batch(self.no - 1, self.slot - 1, self.turn)
        return Batch(self.no - 1, RING - 1, self.turn - 1)

    def after(self, n=1):
        return Batch(self.no + n, (self.slot + n) % RING, self.turn + (self.slot + n) // RING)

    def exists(self):
        return not isinstance(self.no, int) or self.no < BATCHES


def behind(b, n):
    if isinstance(b.no, int) and not 0 <= b.no - n < BATCHES:
        return None
    for _ in range(n):
        b = b.before()
    return b


def gap_to(i):
    return {0: 1, 1: 3}.get(i, 2)


def later(b, q, n, do, *more):
    at = b.after((q + n) // NG) if q + n >= NG else b
    if at.exists():
        do(at, (q + n) % NG, *more)


def edges(nc, kit, io, t, lay):
    H, C, R, RW, DW, VW = lay.H, lay.C, lay.R, lay.RW, lay.DW, lay.VW
    HG = H * G
    edge = lay.edge
    assert BATCHES % RING and NG % 2 == 1 and NG > RING and HG <= P and GS * RW <= 512 and 3 * G * HEADS <= 512
    with ExitStack() as ctx:
        def sb(name, shape, dt=F32):
            return kit.sb(f"{lay.n}_{name}", shape, dt, ctx)

        def ps(name):
            return kit.ps(f"{lay.n}_{name}", [P, 512], F32, ctx)

        def sem(name):
            return kit.sem(f"{lay.n}_{name}", ctx)

        idx = [sb(f"idx{i}", [P, G], I32) for i in range(RING)]
        place = [sb(f"place{i}", [P, G]) for i in range(RING)]
        rows = [sb(f"rows{i}", [P, G, RW]) for i in range(RING)]
        hot = [sb(f"hot{i}", [P, G, P]) for i in range(RING)]
        val = [sb(f"val{i}", [P, G, VW]) for i in range(RING)]
        res = [sb(f"res{i}", [P, P + 1]) for i in range(RING)]
        hot0 = [sb(f"hot0_{i}", [P, 1]) for i in range(RING)]
        score = [sb(f"score{i}", [P, H, G]) for i in range(RING)]
        hotT = [sb(f"hotT{i}", [P, GS * P], F32 if edge else BF16) for i in range(RING)]
        if edge:
            attrT = [sb(f"attrT{i}", [DE, G * P]) for i in range(RING)]
            mes = [sb(f"mes{i}", [P, GS * H, R]) for i in range(RING)]
        else:
            parts = sb("parts", [P, WINDOWS, 3, H], BF16)
            rest = sb("rest", [P, 2, WINDOWS, H])
            split = sem("split")
        raw = sb("raw", [P, G, H])
        fwd, bwd, top = sb("fwd", [P, P]), sb("bwd", [P, P]), sb("top", [P, P])
        chain_r = sb("chain_r", [1, 2, H, G + 1])
        chain_m = sb("chain_m", [1, 2, H, G + 1])
        chain = sb("chain", [1, 2, H, G + 1])
        before = sb("before", [1, 2, H, G])
        init = sb("init", [P, 2])
        gap = sb("gap", [1, 2, H])
        same = sb("same", [1, 1])
        fac_in, fac = sb("fac_in", [P, H]), sb("fac", [P, H])
        dif = sb("dif", [P, G, H])
        msg = [ps(f"msg{i}") for i in range(RING)]
        hotT_ps = ps("hotT_ps")
        agg = [ps("agg0"), ps("agg1")]
        mx = ps("mx")
        prob = ps("prob")
        ENDS, INITS, GAPS = P, 3 * P, 3 * P + 8

        gathered = [sem(f"gathered{i}") for i in range(RING)]
        resets_in = [sem(f"resets_in{i}") for i in range(RING)]
        prepared, staged = sem("prepared"), sem("staged")
        off_made, hot_made, hot_turned, hotT_made = sem("off_made"), sem("hot_made"), sem("hot_turned"), sem("hotT_made")
        msg_made, msg_added = sem("msg_made"), sem("msg_added")
        scored = sem("scored")
        if edge:
            attrs_in = [sem(f"attrs_in{i}") for i in range(RING)]
            vals_in = [sem(f"vals_in{i}") for i in range(RING)]
            relu_made, weighted = sem("relu_made"), sem("weighted")
        else:
            joined = sem("joined")
        turned, scanned, ends_made = sem("turned"), sem("scanned"), sem("ends_made")
        resets_kept = sem("resets_kept")
        chain_vec, chained, inits_made = sem("chain_vec"), sem("chained"), sem("inits_made")
        inits_taken, rescanned, top_made, top_turned = sem("inits_taken"), sem("rescanned"), sem("top_made"), sem("top_turned")
        dif_made, tops_kept, prob_made, prob_kept = sem("dif_made"), sem("tops_kept"), sem("prob_made"), sem("prob_kept")
        fac_made, rescaled = sem("fac_made"), sem("rescaled")
        val_made, agg_made, added = sem("val_made"), sem("agg_made"), sem("added")
        PREPARED = 4 + (RING if edge else 0)
        ATTR = RW + H
        block = ctx.enter_context(nc.Block())

        def run(eng, batch, extra=0):
            for u in range(RING):
                batch(Batch(u, u, 0))
            with eng.Fori(1, TURNS) as r:
                for u in range(RING):
                    batch(Batch(r * RING + u, u, r))
            for no in range(TURNS * RING, BATCHES + extra):
                batch(Batch(no, no % RING, no // RING))

        def step_slot(b, q):
            return (b.slot * NG + q) % RING

        FIRST = Batch(0, 0, 0)

        @block.gpsimd
        def _(pool):
            pool.memset(chain_r[:, :, :, :], -1e3 * BIG).then_inc(prepared, 1)
            pool.memset(chain_m[:, :, :, :], -BIG).then_inc(prepared, 1)
            pool.memset(chain[:, :, :, :], -BIG).then_inc(prepared, 1)
            if edge:
                for u in range(RING):
                    pool.memset(val[u][:, :, ATTR + DE:ATTR + DE + 1], 1.0).then_inc(prepared, 1)

            def gather(b):
                pool.wait_ge(staged, b.no + 1)
                settle(pool)
                for j in range(G):
                    if b.reuses and j % GS == 0:
                        pool.wait_ge(val_made, (b.no - RING) * NG + j // GS + 1)
                        settle(pool)
                    pool.indirect_dma_start(rows[b.slot][:, j, :], None, lay.table,
                                            bass.IndirectOffsetOnAxis(idx[b.slot][:, j:j + 1], 0)).then_inc(gathered[b.slot], 16)

            run(pool, gather)

        @block.sync
        def _(sp):
            def load(b):
                if b.reuses:
                    sp.wait_ge(top_made, b.no - RING + 1)
                sp.dma_start(res[b.slot][0:HG, :],
                             bc(io.resets_r[bass.ds(b.no * G, G), :].unsqueeze(0), H, G, P + 1)).then_inc(resets_in[b.slot], 16)
                if edge:
                    groups = nc.values_load_multi_w_load_instructions(
                        t.groups[0:1, bass.ds(b.no * NG, NG)], engines=(SPE,), min_val=0, max_val=GROUPS,
                        skip_runtime_bounds_check_because="counts of groups")[1]
                    if b.reuses:
                        sp.wait_ge(msg_made, (b.no - RING + 1) * NG)
                        settle(sp)
                    for q in range(NG):
                        sp.dma_start(attrT[b.slot][:, q * GE:(q + 1) * GE],
                                     io.attrT[:, bass.ds(groups[q] * GE, GE)]).then_inc(attrs_in[b.slot], 16)
                    if b.reuses:
                        sp.wait_ge(agg_made, (b.no - RING + 1) * NG)
                        settle(sp)
                    for q in range(NG):
                        sp.dma_start(val[b.slot][:, q * GS:(q + 1) * GS, ATTR:ATTR + DE],
                                     io.attr[bass.ds(groups[q] * GE, GE), :].rearrange("(j p) d -> p j d", p=P)).then_inc(vals_in[b.slot], 16)

            run(sp, load)

        @block.scalar
        def _(act):
            def stage(b):
                if b.reuses:
                    act.wait_ge(gathered[b.slot], b.turn * G * 16)
                    act.wait_ge(hot_made, (b.no - RING + 1) * NG)
                act.activation(idx[b.slot][:, :], t.src_k[:, bass.ds(b.no * G, G)], ACT.Copy)
                act.activation(place[b.slot][:, :], t.rel_k[:, bass.ds(b.no * G, G)], ACT.Copy, scale=-1.0).then_inc(staged, 1)

            def chain_resets(c):
                if c.some_before:
                    act.wait_ge(chained, 2 * c.no)
                act.activation(chain_r[0:1, 0, :, 1:G + 1], bc(t.rsum_f[0:1, bass.ds(c.no * G, G)].unsqueeze(1), 1, H, G), ACT.Copy)
                act.activation(chain_r[0:1, 1, :, G:0:-1], bc(t.rsum_b[0:1, bass.ds(c.no * G, G)].unsqueeze(1), 1, H, G),
                               ACT.Copy).then_inc(resets_kept, 1)

            def off_nodes(b, q):
                if q == 0:
                    act.wait_ge(staged, b.no + 1)
                if b.reuses:
                    act.wait_ge(agg_made, (b.no - RING) * NG + q + 1)
                for j in range(GS):
                    s = q * GS + j
                    ins = act.activation(hot[b.slot][:, s, :], t.iota[:, :], ACT.Abs, bias=place[b.slot][:, s:s + 1])
                ins.then_inc(off_made, 1)

            def one_hot(b, q):
                act.wait_ge(off_made, b.no * NG + q + 1)
                part = hot[b.slot][:, q * GS:(q + 1) * GS, :]
                act.activation(part, part, ACT.Relu, scale=-1.0, bias=t.ones[:, 0:1]).then_inc(hot_made, 1)

            def keep_turned(b, q):
                g = b.no * NG + q
                act.wait_ge(hot_turned, g + 1)
                if b.some_before or q >= RING:
                    act.wait_ge(msg_made, g + 1 - RING)
                if q == 0:
                    if b.reuses:
                        act.wait_ge(fac_made, b.no - RING + 1)
                    act.activation(hot0[b.slot][:, :], hotT_ps[:, 0:1], ACT.Copy)
                act.activation(hotT[step_slot(b, q)][:, :], hotT_ps[:, 0:GS * P], ACT.Copy).then_inc(hotT_made, 1)

            def relu(b, q):
                act.wait_ge(msg_added, b.no * NG + q + 1)
                part = mes[step_slot(b, q)][:, :, 0:C]
                act.activation(part, part, ACT.Relu).then_inc(relu_made, 1)

            def probabilities(c):
                act.wait_ge(dif_made, c.no + 1)
                if c.some_before:
                    act.wait_ge(val_made, c.no * NG)
                act.activation(prob[:, 0:HG], dif[:, :, :].rearrange("p g h -> p (g h)"), ACT.Exp).then_inc(prob_made, 1)
                act.activation(val[c.slot][:, :, 0:RW].rearrange("p g (h r) -> p g h r", r=R)[:, :, :, C], dif[:, :, :],
                               ACT.Exp).then_inc(prob_kept, 1)

            def factor(c):
                act.wait_ge(inits_taken, c.no + 1)
                if c.some_before:
                    act.wait_ge(rescaled, c.no)
                act.activation(fac[:, :], fac_in[:, :], ACT.Exp, scale=hot0[c.slot][:, 0:1]).then_inc(fac_made, 1)

            def batch(b):
                c = behind(b, 1)
                if b.after(2).exists():
                    stage(b.after(2))
                if c:
                    chain_resets(c)
                for q in range(NG):
                    later(b, q, 4, off_nodes)
                    later(b, q, 3, keep_turned)
                    later(b, q, 4, one_hot)
                    if edge:
                        later(b, q, 1, relu)
                    if q == 3 and c:
                        probabilities(c)
                        factor(c)

            stage(Batch(0, 0, 0))
            stage(Batch(1, 1, 0))
            act.wait_ge(prepared, PREPARED)
            for q in range(4):
                off_nodes(FIRST, q)
                one_hot(FIRST, q)
                if q < 3:
                    keep_turned(FIRST, q)
            if edge:
                relu(FIRST, 0)
            run(act, batch, 1)

        @block.tensor
        def _(pe):
            def turn_hot(b, q):
                g = b.no * NG + q
                pe.wait_ge(hot_made, g + 1)
                if b.some_before or q:
                    pe.wait_ge(hotT_made, g)
                for j in range(GS):
                    ins = pe.transpose(hotT_ps[:, j * P:(j + 1) * P], hot[b.slot][:, q * GS + j, :], t.ident[:, :])
                ins.then_inc(hot_turned, 1)

            def messages(b, q, win):
                g = b.no * NG + q
                pe.wait_ge(hotT_made, g + 1)
                if edge:
                    if q == 0:
                        pe.wait_ge(attrs_in[b.slot], (b.turn + 1) * NG * 16)
                    if b.some_before or q >= RING:
                        pe.wait_ge(msg_added, g + 1 - RING)
                elif q == 0 and b.reuses:
                    pe.wait_ge(msg_added, b.no - RING + 1)
                if edge:
                    dst = lay.dst_table[:, bass.ds(win * DW, DW)]
                else:
                    dst = parts[:, :, :, :].rearrange("p w k h -> p (w k h)")[:, bass.ds(win * 3 * H, 3 * H)]
                turned_hot = hotT[step_slot(b, q)]
                for j in range(GS):
                    s = q * GS + j
                    if edge:
                        out = msg[step_slot(b, q)][:, j * RW:(j + 1) * RW]
                        pe.matmul(out, attrT[b.slot][:, s * P:(s + 1) * P], t.we[:, :, :].rearrange("k h r -> k (h r)"),
                                  start=True, stop=False)
                        ins = pe.matmul(out, turned_hot[:, j * P:(j + 1) * P], dst, start=False, stop=True)
                    else:
                        ins = pe.matmul(msg[b.slot][:, s * 3 * H:(s + 1) * 3 * H], turned_hot[:, j * P:(j + 1) * P], dst, start=True, stop=True)
                ins.then_inc(msg_made, 1)

            def turn_scores(c):
                pe.wait_ge(scored, (c.no + 1) * (NG if edge else 1))
                if c.some_before:
                    pe.wait_ge(tops_kept, c.no)
                settle(pe)
                pe.transpose(mx[0:HG, 0:P], score[c.slot][:, :, :].rearrange("p h g -> p (h g)"), t.ident[:, :]).then_inc(turned, 1)

            def turn_ends(c):
                pe.wait_ge(scanned, 2 * (c.no + 1))
                settle(pe)
                pe.transpose(mx[0:1, ENDS:ENDS + HG], fwd[0:HG, P - 1:P], t.ident[0:HG, 0:HG])
                pe.transpose(mx[0:1, ENDS + P:ENDS + P + HG], bwd[0:HG, 0:1], t.ident[0:HG, 0:HG]).then_inc(ends_made, 1)

            def turn_inits(c):
                pe.wait_ge(chained, 2 * (c.no + 1))
                pe.matmul(mx[0:HG, INITS:INITS + 1], before[0:1, 0, :, :].rearrange("p h g -> p (h g)"), t.ones[0:1, 0:1], start=True, stop=True)
                pe.matmul(mx[0:HG, INITS + 1:INITS + 2], before[0:1, 1, :, :].rearrange("p h g -> p (h g)"), t.ones[0:1, 0:1], start=True, stop=True)
                pe.matmul(mx[:, GAPS:GAPS + H], t.ones[0:1, :], gap[0:1, 1, :], start=True, stop=True).then_inc(inits_made, 1)

            def turn_tops(c):
                pe.wait_ge(top_made, c.no + 1)
                settle(pe)
                pe.transpose(mx[:, 0:HG], top[0:HG, :], t.ident[0:HG, 0:HG]).then_inc(top_turned, 1)

            def sums(c, q):
                if q == 0:
                    if edge:
                        pe.wait_ge(vals_in[c.slot], (c.turn + 1) * NG * 16)
                    pe.wait_ge(tops_kept, c.no + 1)
                    pe.wait_ge(prob_kept, c.no + 1)
                pe.wait_ge(val_made, c.no * NG + q + 1)
                if c.some_before or q >= 2:
                    pe.wait_ge(added, c.no * NG + q + 1 - gap_to(q))
                for j in range(GS):
                    s = q * GS + j
                    ins = pe.matmul(agg[q % 2][:, 0:VW], hot[c.slot][:, s, :], val[c.slot][:, s, :], start=j == 0, stop=j == GS - 1)
                ins.then_inc(agg_made, 1)

            def windows(step, n):
                return nc.values_load_multi_w_load_instructions(
                    t.wins[0:1, bass.ds(step, n)], engines=(PE,), min_val=0, max_val=WINDOWS - 1,
                    skip_runtime_bounds_check_because="clamped when made")[1]

            def batch(b):
                c, cc = behind(b, 1), behind(b, 2)
                wins = windows(b.no * NG + 2, NG) if b.exists() else [0] * NG
                for q in range(NG):
                    if c and q == 1:
                        turn_scores(c)
                    later(b, q, 2, messages, wins[q])
                    later(b, q, 3, turn_hot)
                    if cc:
                        sums(cc, q)
                    if c and q in (1, 2, 3):
                        (turn_ends, turn_inits, turn_tops)[q - 1](c)

            if not edge:
                pe.wait_ge(split, 5)
            first = windows(0, 2)
            turn_hot(FIRST, 0)
            turn_hot(FIRST, 1)
            messages(FIRST, 0, first[0])
            turn_hot(FIRST, 2)
            messages(FIRST, 1, first[1])
            run(pe, batch, 2)

        @block.vector
        def _(dve):
            dve.memset(t.acc[:, :], 0.0).then_inc(prepared, 1)
            dve.wait_ge(prepared, PREPARED)
            if not edge:
                table = lay.dst_table[:, :].rearrange("p (w h) -> p w h", h=H)
                for k in range(3):
                    dve.tensor_copy(parts[:, :, k, :], (table, rest[:, 0], rest[:, 1])[k]).then_inc(split, 1)
                    if k < 2:
                        dve.wait_ge(split, 2 * k + 1)
                        dve.tensor_tensor(rest[:, k], (table, rest[:, 0])[k], parts[:, :, k, :], ALU.subtract).then_inc(split, 1)
                        dve.wait_ge(split, 2 * k + 2)

            def add_rows(b, q):
                g = b.no * NG + q
                dve.wait_ge(msg_made, g + 1)
                if q == 0:
                    dve.wait_ge(gathered[b.slot], (b.turn + 1) * G * 16)
                if b.some_before or q >= RING:
                    dve.wait_ge(scored, g + 1 - RING)
                dve.tensor_tensor(mes[step_slot(b, q)][:, :, :].rearrange("p a r -> p (a r)"), msg[step_slot(b, q)][:, 0:GS * RW],
                                  rows[b.slot][:, q * GS:(q + 1) * GS, :].rearrange("p g r -> p (g r)"), ALU.add).then_inc(msg_added, 1)

            def weigh(b, q):
                dve.wait_ge(relu_made, b.no * NG + q + 1)
                part = mes[step_slot(b, q)][:, :, :].rearrange("p (g h) r -> p g (h r)", g=GS)
                dve.tensor_tensor(part, part, bc(t.att08[:, :, :].rearrange("p h r -> p (h r)").unsqueeze(1), P, GS, RW), ALU.mult).then_inc(weighted, 1)

            def reduce(b, q):
                dve.wait_ge(weighted, b.no * NG + q + 1)
                if b.reuses and q == 0:
                    dve.wait_ge(dif_made, b.no - RING + 1)
                dve.tensor_reduce(score[b.slot][:, :, q * GS:(q + 1) * GS].rearrange("p h g -> p g h"),
                                  mes[step_slot(b, q)][:, :, :].rearrange("p (g h) r -> p g h r", h=H), AX, ALU.add).then_inc(scored, 1)

            def scores_gat(b):
                if b.some_before:
                    dve.wait_ge(scored, b.no)
                dve.wait_ge(msg_made, (b.no + 1) * NG)
                dve.tensor_reduce(raw[:, :, :], msg[b.slot][:, 0:3 * HG].rearrange("p (g k h) -> p g h k", k=3, h=H), AX,
                                  ALU.add).then_inc(msg_added, 1)
                dve.wait_ge(gathered[b.slot], (b.turn + 1) * G * 16)
                dve.wait_ge(msg_added, b.no + 1)
                dve.tensor_tensor(raw[:, :, :], raw[:, :, :], rows[b.slot][:, :, :].rearrange("p g (h r) -> p g h r", r=R)[:, :, :, C],
                                  ALU.add).then_inc(joined, 1)
                if b.reuses:
                    dve.wait_ge(dif_made, b.no - RING + 1)
                dve.wait_ge(joined, b.no + 1)
                dve.scalar_tensor_tensor(score[b.slot][:, :, :].rearrange("p h g -> p g h"), raw[:, :, :], SLOPE, raw[:, :, :], ALU.mult, ALU.max).then_inc(scored, 1)

            def scan(c, out, which, initial, done):
                r = res[c.slot]
                s = mx[0:HG, 0:P]
                if which == 0:
                    dve.tensor_tensor_scan(out[0:HG, :], r[0:HG, 0:P], s, initial, ALU.add, ALU.max).then_inc(done, 1)
                else:
                    dve.tensor_tensor_scan(out[0:HG, ::-1], r[0:HG, P:0:-1], s[:, ::-1], initial, ALU.add, ALU.max).then_inc(done, 1)

            def scan_tiles(c):
                dve.wait_ge(turned, c.no + 1)
                dve.wait_ge(resets_in[c.slot], (c.turn + 1) * 16)
                if c.some_before:
                    dve.wait_ge(top_made, c.no)
                scan(c, fwd, 0, -BIG, scanned)
                scan(c, bwd, 1, -BIG, scanned)

            def chain_op(c, k, ins, wait=True):
                ins.then_inc(chain_vec, 1)
                if wait:
                    dve.wait_ge(chain_vec, c.no * 7 + k)

            def chain_tiles(c):
                if c.some_before:
                    dve.wait_ge(inits_made, c.no)
                chain_op(c, 1, dve.tensor_copy(chain_m[0:1, 0, :, 0], chain[0:1, 0, :, G]), False)
                dve.wait_ge(ends_made, c.no + 1)
                ends = mx[0:1, ENDS:ENDS + 2 * P].rearrange("p (a b) -> p a b", a=2)[:, :, 0:HG].rearrange("p a (h g) -> p a h g", g=G)
                chain_op(c, 2, dve.tensor_copy(chain_m[0:1, 0, :, 1:G + 1], ends[:, 0]), False)
                chain_op(c, 3, dve.tensor_copy(chain_m[0:1, 1, :, G:0:-1], ends[:, 1]), False)
                dve.wait_ge(resets_kept, c.no + 1)
                chain_op(c, 4, dve.tensor_scalar(same[:, :], res[c.slot][0:1, 0:1], 0.0, None, ALU.is_equal))
                dve.tensor_tensor_scan(chain[:, :, :, :].rearrange("p a h g -> p (a h g)"), chain_r[:, :, :, :].rearrange("p a h g -> p (a h g)"),
                                       chain_m[:, :, :, :].rearrange("p a h g -> p (a h g)"), -BIG, ALU.add, ALU.max).then_inc(chain_vec, 1)

            def chain_results(c):
                dve.wait_ge(chain_vec, c.no * 7 + 5)
                dve.tensor_tensor(gap[0:1, 0, :], chain_m[0:1, 0, :, 0], chain[0:1, 1, :, G], ALU.subtract).then_inc(chain_vec, 1)
                dve.tensor_copy(before[0:1, 0, :, :], chain[0:1, 0, :, 0:G]).then_inc(chained, 1)
                dve.tensor_copy(before[0:1, 1, :, :], chain[0:1, 1, :, G - 1::-1]).then_inc(chain_vec, 1)
                dve.wait_ge(chain_vec, c.no * 7 + 7)
                dve.tensor_scalar(gap[0:1, 1, :], gap[0:1, 0, :], 0.0, same[:, 0:1], ALU.min, ALU.mult).then_inc(chained, 1)

            def rescan_tiles(c):
                dve.wait_ge(inits_made, c.no + 1)
                if c.some_before:
                    dve.wait_ge(fac_made, c.no)
                dve.tensor_copy(init[0:HG, :], mx[0:HG, INITS:INITS + 2]).then_inc(rescanned, 1)
                dve.tensor_copy(fac_in[:, :], mx[:, GAPS:GAPS + H]).then_inc(inits_taken, 1)
                dve.wait_ge(rescanned, 3 * c.no + 1)
                scan(c, fwd, 0, init[0:HG, 0:1], rescanned)
                scan(c, bwd, 1, init[0:HG, 1:2], rescanned)

            def join_scans(c):
                dve.wait_ge(rescanned, 3 * (c.no + 1))
                if c.some_before:
                    dve.wait_ge(top_turned, c.no)
                dve.tensor_tensor(top[0:HG, :], fwd[0:HG, :], bwd[0:HG, :], ALU.max).then_inc(top_made, 1)

            def subtract_tops(c):
                dve.wait_ge(top_turned, c.no + 1)
                if c.some_before:
                    dve.wait_ge(prob_kept, c.no)
                tops = mx[:, 0:HG].rearrange("p (h g) -> p g h", g=G)
                dve.tensor_tensor(dif[:, :, :], score[c.slot][:, :, :].rearrange("p h g -> p g h"), tops, ALU.subtract).then_inc(dif_made, 1)
                dve.tensor_tensor(val[c.slot][:, :, RW:RW + H], tops, bc(t.last_k[:, bass.ds(c.no * G, G)].unsqueeze(2), P, G, H),
                                  ALU.mult).then_inc(tops_kept, 1)

            def acc_of(win, width):
                return t.acc[:, bass.ds(win * VW, width)]

            def rescale(c, win):
                dve.wait_ge(fac_made, c.no + 1)
                if c.some_before:
                    dve.wait_ge(added, c.no * NG)
                a = acc_of(win, RW).rearrange("p (h r) -> p h r", r=R)
                dve.tensor_tensor(a, a, bc(fac[:, :].unsqueeze(2), P, H, R), ALU.mult).then_inc(rescaled, 1)

            def weigh_rows(c, q):
                g = c.no * NG + q
                if q == 0:
                    dve.wait_ge(prob_made, c.no + 1)
                part = slice(q * GS, (q + 1) * GS)
                p = prob[:, q * GS * H:(q + 1) * GS * H]
                dve.tensor_tensor(val[c.slot][:, part, 0:RW].rearrange("p g (h r) -> p g h r", r=R)[:, :, :, 0:C],
                                  rows[c.slot][:, part, :].rearrange("p g (h r) -> p g h r", r=R)[:, :, :, 0:C],
                                  bc(p.rearrange("p (g h) -> p g h", h=H).unsqueeze(3), P, GS, H, C), ALU.mult).then_inc(val_made, 1)

            def add_sums(c, q, win):
                dve.wait_ge(agg_made, c.no * NG + q + 1)
                if q == 0:
                    dve.wait_ge(rescaled, c.no + 1)
                else:
                    dve.wait_ge(added, c.no * NG + q)
                a = acc_of(win, VW)
                dve.tensor_tensor(a, agg[q % 2][:, 0:VW], a, ALU.add).then_inc(added, 1)

            def windows(step, n):
                return nc.values_load_multi_w_load_instructions(
                    t.wins[0:1, bass.ds(step, n)], engines=(DVE,), min_val=0, max_val=WINDOWS - 1,
                    skip_runtime_bounds_check_because="clamped when made")[1]

            def before_weigh(c, cc, q, wins):
                if cc:
                    add_sums(cc, q, wins[q])
                if c and q == 1:
                    chain_tiles(c)
                if c and q == 2:
                    rescan_tiles(c)
                if c and q == 3:
                    subtract_tops(c)

            def before_reduce(c, q, win):
                if c and q == 0:
                    scan_tiles(c)
                if c and q == 1:
                    chain_results(c)
                if c and q == 2:
                    join_scans(c)
                if c and q == 4:
                    weigh_rows(c, 1)
                    rescale(c, win)

            def after_reduce(c, cc, q):
                if cc and q < 2:
                    weigh_rows(cc, q + 3)
                if c and q == 3:
                    weigh_rows(c, 0)
                if c and q == 4:
                    weigh_rows(c, 2)

            def batch(b):
                c, cc = behind(b, 1), behind(b, 2)
                wins = windows(cc.no * NG, NG + bool(c)) if cc else windows(0, 1) if c else [0]
                for q in range(NG):
                    if edge:
                        later(b, q, 1, add_rows)
                    before_weigh(c, cc, q, wins)
                    if edge and b.exists():
                        weigh(b, q)
                    before_reduce(c, q, wins[-1])
                    if edge and b.exists():
                        reduce(b, q)
                    if not edge and b.exists() and q == 4:
                        scores_gat(b)
                    after_reduce(c, cc, q)

            if edge:
                add_rows(FIRST, 0)
            run(dve, batch, 2)
def add_nodes(pe, t, banks, src, r, first=False):
    last = isinstance(r, int) and r == CHUNKS - 1
    at, full = r * CH * D, 4 * D
    pe.matmul(banks[0][:, 0:full], t.ones[:, :], src[:, bass.ds(at, full)], start=first, stop=last)
    part = (CH - 4 - last) * D
    if last:
        pe.matmul(banks[1][:, part:part + D], t.valid[:, :], src[:, bass.ds(at + full + part, D)], start=False, stop=False)
    return pe.matmul(banks[1][:, 0:part], t.ones[:, :], src[:, bass.ds(at + full, part)], start=first, stop=last)


def merge(nc, kit, io, t, lay):
    H, C, R, RW, DW, VW = lay.H, lay.C, lay.R, lay.RW, lay.DW, lay.VW
    edge = lay.edge
    n = lay.n + "m_"
    ATTR = RW + H
    with ExitStack() as ctx:
        def sb(name, shape):
            return kit.sb(n + name, shape, F32, ctx)

        def sem(name):
            return kit.sem(n + name, ctx)

        own2 = [sb(f"own{i}", [P, CH, RW]) for i in range(2)]
        num = sb("num", [P, CH, RW])
        loop = sb("loop", [P, CH, H, C])
        sl = sb("sl", [P, CH, H])
        seen = sb("seen", [P, CH, H])
        old = sb("old", [P, CH, H])
        new = sb("new", [P, CH, H])
        down = sb("down", [P, 2, CH, H])
        fac = sb("fac", [P, 2, CH, H])
        den = sb("den", [P, CH, H])
        res = sb("res", [P, CH, D])
        bias = sb("bias", [P, D])
        raw = sb("raw", [P, CH, H])
        if edge:
            count = sb("count", [P, CH, 1])
            mean = sb("mean", [P, CH, DE])
            meanT = sb("meanT", [DE, CH * P])
            mes = sb("mes", [P, CH, RW])
            pos = sb("pos", [P, CH * H, C])
            turned = [kit.ps(n + f"turned{i}", [P, 512], F32, ctx) for i in range(2)]
            ee = [kit.ps(n + f"ee{i}", [P, 512], F32, ctx) for i in range(3)]
        else:
            x2 = [sb(f"x{i}", [P, CH, D]) for i in range(2)]
        loaded, vec, act_done = sem("loaded"), sem("vec"), sem("act_done")
        own_in = [sem("own_in0"), sem("own_in1")]
        if edge:
            means, turned_ready, meanT_ready, ee_ready = sem("means"), sem("turned_ready"), sem("meanT_ready"), sem("ee_ready")
        else:
            stored = sem("stored")
        EE_USED, MES, SCORE = (3, 4, 7) if edge else (0, 0, 2)
        DOWN = SCORE + 5
        OWN_USED = DOWN + 2
        DONE = DOWN + 8 - (0 if edge else -1)
        block = ctx.enter_context(nc.Block())

        @block.sync
        def _(sp):
            sp.dma_start(bias[:, :], bc(lay.bias_out, P, D)).then_inc(loaded, 16)

            def store(r, last=False):
                sp.wait_ge(vec, (r + 1) * DONE)
                settle(sp)
                at = r * CH * P
                if not last:
                    sp.dma_start(io.out[bass.ds(at, CH * P), :].rearrange("(w p) d -> p w d", p=P), res[:, :, :]).then_inc(stored, 16)
                else:
                    full = (CH - 1) * P
                    sp.dma_start(io.out[at:at + full, :].rearrange("(w p) d -> p w d", p=P), res[:, 0:CH - 1, :]).then_inc(stored, 16)
                    sp.dma_start(io.out[at + full:NODES, :], res[0:LASTW, CH - 1, :]).then_inc(stored, 16)

            if not edge:
                store(0)
                with sp.Fori(1, CHUNKS - 1) as r:
                    store(r)
                store(CHUNKS - 1, True)
                sp.wait_ge(stored, 16 * (CHUNKS + 1))

        @block.gpsimd
        def _(pool):
            def load(r, slot):
                rows = bass.ds(r * CH * P, CH * P)
                if not isinstance(r, int) or r >= 2:
                    pool.wait_ge(vec, (r - 2) * DONE + OWN_USED)
                    settle(pool)
                pool.dma_start(own2[slot][:, :, :], lay.table[rows, :].rearrange("(w p) d -> p w d", p=P)).then_inc(own_in[slot], 16)
                if not edge:
                    if not isinstance(r, int) or r >= 2:
                        pool.wait_ge(vec, (r - 1) * DONE)
                        settle(pool)
                    pool.dma_start(x2[slot][:, :, :], lay.x_in[rows, :].rearrange("(w p) d -> p w d", p=P)).then_inc(own_in[slot], 16)

            load(0, 0)
            load(1, 1)
            with pool.Fori(1, (CHUNKS - 1) // 2) as i:
                load(2 * i, 0)
                load(2 * i + 1, 1)
            load(CHUNKS - 1, 0)

        @block.scalar
        def _(act):
            def chunk(r):
                if edge:
                    for half in range(2):
                        act.wait_ge(turned_ready, 2 * r + half + 1)
                        at, w = half * 4, 4 - half
                        act.activation(meanT[:, at * P:(at + w) * P], turned[half][0:DE, 0:w * P], ACT.Copy).then_inc(meanT_ready, 1)
                    act.wait_ge(vec, r * DONE + MES)
                    act.activation(pos[:, :, :], mes[:, :, :].rearrange("p w (h r) -> p (w h) r", r=R)[:, :, 0:C], ACT.Relu).then_inc(act_done, 1)
                act.wait_ge(vec, r * DONE + DOWN)
                act.activation(fac[:, :, :, :], down[:, :, :, :], ACT.Exp).then_inc(act_done, 1)

            chunk(0)
            with act.Fori(1, CHUNKS) as r:
                chunk(r)

        @block.tensor
        def _(pe):
            def chunk(r, first=False):
                pe.wait_ge(means, 3 * (r + 1))
                settle(pe)
                for w in range(CH):
                    half, at = divmod(w, 4)
                    ins = pe.transpose(turned[half][0:DE, at * P:(at + 1) * P], mean[:, w, :], t.ident[:, :])
                    if w in (3, CH - 1):
                        ins.then_inc(turned_ready, 1)
                pe.wait_ge(meanT_ready, 2 * (r + 1))
                if not first:
                    pe.wait_ge(vec, (r - 1) * DONE + EE_USED)
                for w in range(CH):
                    ins = pe.matmul(ee[w // 3][:, (w % 3) * RW:(w % 3 + 1) * RW], meanT[:, w * P:(w + 1) * P],
                                    t.we[:, :, :].rearrange("k h r -> k (h r)"), start=True, stop=True)
                ins.then_inc(ee_ready, 1)

            if edge:
                def add_results(r, first=False):
                    pe.wait_ge(vec, (r + 1) * DONE)
                    settle(pe)
                    add_nodes(pe, t, t.node_sums, t.gn, r, first)

                chunk(0, True)
                chunk(1)
                add_results(0, True)
                with pe.Fori(2, CHUNKS) as r:
                    chunk(r)
                    add_results(r - 1)
                add_results(CHUNKS - 1)

        @block.vector
        def _(dve):
            dve.wait_ge(loaded, 16)

            def sums_of(r):
                return t.acc[:, bass.ds(r * CH * VW, CH * VW)].rearrange("p (w v) -> p w v", v=VW)

            def mean_attributes(r):
                a = sums_of(r)
                dve.tensor_scalar(count[:, :, :], a[:, :, ATTR + DE:ATTR + DE + 1], 1.0, None, ALU.max).then_inc(means, 1)
                dve.wait_ge(means, 3 * r + 1)
                dve.reciprocal(count[:, :, :], count[:, :, :]).then_inc(means, 1)
                dve.wait_ge(means, 3 * r + 2)
                dve.tensor_tensor(mean[:, :, :], a[:, :, ATTR:ATTR + DE], bc(count[:, :, :], P, CH, DE), ALU.mult).then_inc(means, 1)

            def chunk(r, slot, turn, last=False):
                k = [0]
                own = own2[slot]

                def step(ins, wait=True):
                    k[0] += 1
                    ins.then_inc(vec, 1)
                    if wait:
                        dve.wait_ge(vec, r * DONE + k[0])

                a = sums_of(r)
                dst = lay.dst_table[:, bass.ds(r * CH * DW, CH * DW)].rearrange("p (w v) -> p w v", v=DW)
                sums = a[:, :, 0:RW].rearrange("p w (h r) -> p w h r", r=R)
                own4 = own[:, :, :].rearrange("p w (h r) -> p w h r", r=R)
                if edge:
                    dve.wait_ge(own_in[slot], 16 * (turn + 1))
                    dve.wait_ge(ee_ready, r + 1)
                    for i in range(3):
                        w = slice(3 * i, min(3 * i + 3, CH))
                        c = (w.stop - w.start) * RW
                        step(dve.tensor_tensor(mes[:, w, :].rearrange("p w v -> p (w v)"), ee[i][:, 0:c],
                                               own[:, w, :].rearrange("p w v -> p (w v)"), ALU.add), i == 2)
                    step(dve.tensor_tensor(mes[:, :, :], mes[:, :, :], dst, ALU.add), False)
                    assert k[0] == MES
                    if not last:
                        mean_attributes(r + 1)
                    dve.wait_ge(act_done, r * 2 + 1)
                    pos4 = pos[:, :, :].rearrange("p (w h) c -> p w h c", h=H)
                    step(dve.tensor_tensor(pos4, pos4, bc(t.att08[:, :, 0:C].unsqueeze(1), P, CH, H, C), ALU.mult))
                    step(dve.tensor_reduce(raw[:, :, :].rearrange("p w h -> p (w h)"), pos[:, :, :], AX, ALU.add))
                    step(dve.tensor_tensor(sl[:, :, :], raw[:, :, :], mes[:, :, :].rearrange("p w (h r) -> p w h r", r=R)[:, :, :, C], ALU.add))
                else:
                    dve.wait_ge(own_in[slot], 32 * (turn + 1))
                    step(dve.tensor_tensor(raw[:, :, :], own4[:, :, :, C], dst, ALU.add))
                    step(dve.scalar_tensor_tensor(sl[:, :, :], raw[:, :, :], SLOPE, raw[:, :, :], ALU.mult, ALU.max))
                assert k[0] == SCORE
                step(dve.tensor_scalar(seen[:, :, :], sums[:, :, :, C], 0.5, BIG, ALU.is_gt, ALU.mult))
                step(dve.scalar_tensor_tensor(old[:, :, :], seen[:, :, :], -BIG, a[:, :, RW:RW + H], ALU.add, ALU.add))
                step(dve.tensor_tensor(new[:, :, :], old[:, :, :], sl[:, :, :], ALU.max))
                step(dve.tensor_tensor(down[:, 0], old[:, :, :], new[:, :, :], ALU.subtract), False)
                step(dve.tensor_tensor(down[:, 1], sl[:, :, :], new[:, :, :], ALU.subtract), False)
                assert k[0] == DOWN
                dve.wait_ge(act_done, (r + 1) * (2 if edge else 1))
                num4 = num[:, :, :].rearrange("p w (h r) -> p w h r", r=R)
                step(dve.tensor_tensor(num4, sums, bc(fac[:, 0].unsqueeze(3), P, CH, H, R), ALU.mult), False)
                step(dve.tensor_tensor(loop[:, :, :, :], own4[:, :, :, 0:C], bc(fac[:, 1].unsqueeze(3), P, CH, H, C), ALU.mult))
                assert k[0] == OWN_USED
                step(dve.tensor_tensor(num4[:, :, :, 0:C], num4[:, :, :, 0:C], loop[:, :, :, :], ALU.add), False)
                step(dve.tensor_tensor(den[:, :, :], num4[:, :, :, C], fac[:, 1], ALU.add))
                step(dve.tensor_scalar(den[:, :, :], den[:, :, :], 1e-16, None, ALU.add))
                step(dve.reciprocal(den[:, :, :], den[:, :, :]))
                wide = bc(bias[:, :].unsqueeze(1), P, CH, D)
                step(dve.tensor_tensor(loop[:, :, :, :], num4[:, :, :, 0:C], bc(den[:, :, :].unsqueeze(3), P, CH, H, C), ALU.mult))
                flat = loop[:, :, :, :].rearrange("p w h c -> p w (h c)")
                if edge:
                    step(dve.tensor_tensor(t.gn[:, bass.ds(r * CH * D, CH * D)].rearrange("p (w d) -> p w d", d=D), flat, wide, ALU.add))
                else:
                    step(dve.tensor_tensor(flat, flat, wide, ALU.add))
                    if not isinstance(r, int) or r:
                        dve.wait_ge(stored, 16 * r)
                    step(dve.scalar_tensor_tensor(res[:, :, :], flat, 0.0, x2[slot][:, :, :], ALU.max, ALU.add))
                assert k[0] == DONE, (k[0], DONE)

            if edge:
                mean_attributes(0)
            chunk(0, 0, 0)
            with dve.Fori(1, (CHUNKS - 1) // 2) as i:
                chunk(2 * i - 1, 1, i - 1)
                chunk(2 * i, 0, i)
            chunk(CHUNKS - 2, 1, (CHUNKS - 2) // 2)
            chunk(CHUNKS - 1, 0, (CHUNKS - 1) // 2, True)


def graph_norm(nc, kit, io, t, lay):
    with ExitStack() as ctx:
        def sb(name, shape):
            return kit.sb("g_" + name, shape, F32, ctx)

        def sem(name):
            return kit.sem("g_" + name, ctx)

        x = sb("x", [P, WINDOWS * D])
        sq = sb("sq", [P, WINDOWS * D])
        par = sb("par", [P, 3, D])
        col = sb("col", [P, 2, D])
        std = sb("std", [P, D])
        squares = [kit.ps(f"g_squares{i}", [P, 512], F32, ctx) for i in range(2)]
        loaded, x_in, vec = sem("loaded"), sem("x_in"), sem("vec")
        summed, squared, rooted, stored = sem("summed"), sem("squared"), sem("rooted"), sem("stored")
        centred, made = sem("centred"), sem("made")
        block = ctx.enter_context(nc.Block())
        MEAN, VAR = 5, 10

        def scaled_at(r):
            return VAR + 2 + (1 if r == 0 else 2 * r)

        def shifted_at(r):
            return VAR + 2 + min(2 * r + 3, 2 * CHUNKS)

        def chunk_of(a, r):
            return a[:, r * CH * D:(r + 1) * CH * D]

        @block.sync
        def _(sp):
            for i, a in enumerate((io.gn_weight, io.gn_bias, io.gn_mean_scale)):
                sp.dma_start(par[:, i, :], bc(a, P, D)).then_inc(loaded, 16)
            sp.dma_start(x[:, :].rearrange("p (w d) -> p w d", d=D), io.x.rearrange("(w p) d -> p w d", p=P)).then_inc(x_in, 16)
            for r in range(CHUNKS):
                sp.wait_ge(made, r + 1)
                sp.dma_start(io.x1[r * CH * P:(r + 1) * CH * P, :].rearrange("(w p) d -> p w d", p=P),
                             chunk_of(x, r).rearrange("p (w d) -> p w d", d=D)).then_inc(stored, 16)
            sp.wait_ge(stored, 16 * CHUNKS)

        @block.tensor
        def _(pe):
            for r in range(CHUNKS):
                pe.wait_ge(squared, r + 1)
                add_nodes(pe, t, squares, sq, r, r == 0).then_inc(summed, 1)

        @block.scalar
        def _(act):
            for r in range(CHUNKS):
                act.wait_ge(centred, r + 1)
                act.activation(chunk_of(sq, r), chunk_of(t.gn, r), ACT.Square).then_inc(squared, 1)
            act.wait_ge(vec, VAR)
            act.activation(std[:, :], col[:, 1, :], ACT.Sqrt).then_inc(rooted, 1)

        @block.vector
        def _(dve):
            n = [0]

            def step(ins, wait=True):
                n[0] += 1
                ins.then_inc(vec, 1)
                if wait:
                    dve.wait_ge(vec, n[0])

            def mean_of(i, banks):
                step(dve.tensor_reduce(col[:, i, :], banks[0][:, 0:4 * D].rearrange("p (w d) -> p d w", d=D), AX, ALU.add), False)
                step(dve.tensor_reduce(std[:, :], banks[1][:, 0:(CH - 4) * D].rearrange("p (w d) -> p d w", d=D), AX, ALU.add))
                step(dve.tensor_tensor(col[:, i, :], col[:, i, :], std[:, :], ALU.add))
                step(dve.tensor_scalar(col[:, i, :], col[:, i, :], 1.0 / NODES, None, ALU.mult))

            def by_window(a, r):
                return chunk_of(a, r).rearrange("p (w d) -> p w d", d=D)

            def wide(a):
                return bc(a.unsqueeze(1), P, CH, D)

            dve.wait_ge(loaded, 48)
            mean_of(0, t.node_sums)
            step(dve.tensor_tensor(col[:, 0, :], col[:, 0, :], par[:, 2, :], ALU.mult))
            assert n[0] == MEAN
            for r in range(CHUNKS):
                g = by_window(t.gn, r)
                dve.tensor_tensor(g, g, wide(col[:, 0, :]), ALU.subtract).then_inc(centred, 1)
            dve.wait_ge(summed, CHUNKS)
            mean_of(1, squares)
            step(dve.tensor_scalar(col[:, 1, :], col[:, 1, :], EPS, None, ALU.add))
            assert n[0] == VAR
            dve.wait_ge(rooted, 1)
            step(dve.reciprocal(std[:, :], std[:, :]))
            step(dve.tensor_tensor(std[:, :], std[:, :], par[:, 0, :], ALU.mult))
            dve.wait_ge(centred, CHUNKS)
            dve.wait_ge(x_in, 16)
            for r in range(CHUNKS + 2):
                if r < CHUNKS:
                    g = by_window(t.gn, r)
                    step(dve.tensor_tensor(g, g, wide(std[:, :]), ALU.mult), False)
                if 0 <= r - 1 < CHUNKS:
                    g = by_window(t.gn, r - 1)
                    dve.wait_ge(vec, scaled_at(r - 1))
                    step(dve.tensor_tensor(g, g, wide(par[:, 1, :]), ALU.add), False)
                if 0 <= r - 2:
                    dve.wait_ge(vec, shifted_at(r - 2))
                    dve.scalar_tensor_tensor(chunk_of(x, r - 2), chunk_of(t.gn, r - 2), 0.0, chunk_of(x, r - 2), ALU.max, ALU.add).then_inc(made, 1)


def layer(kit, n, H, table, x_in, edge, ctx):
    lay = Names()
    lay.n, lay.H, lay.C, lay.R = n, H, D // H, D // H + 1
    lay.RW = H * lay.R
    lay.DW = lay.RW if edge else H
    lay.VW = lay.RW + H + (DE + 1 if edge else 0)
    lay.table, lay.x_in, lay.edge = table, x_in, edge
    lay.lin = SLOPE if edge else 1.0
    return lay


def program(nc, io):
    with ExitStack() as ctx:
        kit, t = Kit(nc, ctx), Names()
        io.tab_i, io.tab_f = kit.dram("tab_i", (2, KP), I32), kit.dram("tab_f", (2, KT))
        io.keys, io.resets = kit.dram("keys", (1 + KP * GE,)), kit.dram("resets", (KP * GE + P,))
        io.resets_r = kit.dram("resets_r", (KT, P + 1))
        io.x1 = kit.dram("x1", (NP, D))
        l0 = layer(kit, "gatv2", 4, kit.dram("table0", (NP, 4 * 33)), io.x, True, ctx)
        l1 = layer(kit, "gat", 8, kit.dram("table1", (NP, 8 * 17)), io.x1, False, ctx)
        t.ident, t.ones = kit.sb("ident", [P, P]), kit.sb("ones", [P, P])
        t.iota_i, t.iota = kit.sb("iota_i", [P, P], I32), kit.sb("iota", [P, P])
        t.valid = kit.sb("valid", [P, P])
        rows = kit.sb("step_rows", [97, KT], I32)
        t.groups, t.wins = rows[0:1, 0:KP], rows[32:33, 0:KP]
        t.rsum_f, t.rsum_b = rows[64:65, :].bitcast(F32), rows[96:97, :].bitcast(F32)
        t.src_k, t.rel_k = kit.sb("src_k", [P, KT], mybir.dt.int16), kit.sb("rel_k", [P, KT], BF16)
        t.last_k = kit.sb("last_k", [P, KT], BF16)
        constants(nc, kit, t)
        step_tables(nc, kit, io, t)
        with ExitStack() as low:
            l0.dst_table = kit.sb("xr", [P, WINDOWS * l0.DW], F32, low)
            t.we, t.att08 = kit.sb("we", [DE, 4, 33], F32, low), kit.sb("att08", [P, 4, 33], F32, low)
            with ExitStack() as w:
                both = kit.sb("w0", [P, 8, 33], F32, w)
                l0.bias = kit.sb("b0", [1, 2, 4, 33], F32, w)
                l0.wcat = both[:, :, :].rearrange("p h r -> p (h r)")
                l0.mats = [(io.wl, io.bl, P, io.att, both[:, 0:4, :], True), (io.wr, io.br, P, io.att, both[:, 4:8, :], True),
                           (io.we, None, DE, io.att, t.we, True)]
                load_weights(nc, kit, io, t, l0)
                project(nc, kit, io, t, l0)
            t.acc = kit.sb("acc0", [P, WINDOWS * l0.VW], F32, low)
            edges(nc, kit, io, t, l0)
            t.gn = kit.sb("gn", [P, WINDOWS * D], F32, low)
            t.node_sums = [kit.ps(f"node_sums{i}", [P, 512], F32, low) for i in range(2)]
            l0.bias_out = io.bias_out0
            merge(nc, kit, io, t, l0)
            graph_norm(nc, kit, io, t, l0)
        l1.dst_table = kit.sb("a_dst", [P, WINDOWS * l1.DW])
        with ExitStack() as w:
            cat = kit.sb("w1", [P, l1.RW + l1.DW], F32, w)
            l1.bias, l1.wcat = None, cat[:, :]
            to = cat[:, 0:l1.RW].rearrange("p (h r) -> p h r", r=l1.R)
            l1.mats = [(io.w1, None, P, io.att_src, to, True),
                       (io.w1, None, P, io.att_dst, cat[:, l1.RW:l1.RW + l1.DW].rearrange("p (h r) -> p h r", r=1), False)]
            load_weights(nc, kit, io, t, l1)
            project(nc, kit, io, t, l1)
        t.acc = kit.sb("acc1", [P, WINDOWS * l1.VW])
        edges(nc, kit, io, t, l1)
        l1.bias_out = io.bias1
        merge(nc, kit, io, t, l1)


def kernel(**inputs):
    import numpy as np
    import concourse.bacc as bacc
    from concourse.bass_utils import run_bass_kernel_spmd as run

    def arr(name):
        return np.asarray(inputs[name])

    x = np.zeros((NP, D), np.float32)
    x[:NODES] = arr("x")
    src, dst = np.zeros(GP * GE, np.int32), np.full(GP * GE, NOWHERE, np.int32)
    src[:EDGES], dst[:EDGES] = arr("src"), arr("dst")
    attr = np.zeros((GP * GE, DE), np.float32)
    attr[:EDGES] = arr("edge_attr_64")
    dst = dst.reshape(GP, GE)

    def row(name):
        return np.ascontiguousarray(arr(name).reshape(1, D))

    data = {
        "x": x, "src_rows": src.reshape(GP, GE), "dst_rows": dst, "dst_lasts": np.ascontiguousarray(dst[:GROUPS, -1])[None],
        "attr": attr, "attrT": np.ascontiguousarray(attr.T),
        "wl": arr("L0_gnn_Wl"), "bl": row("L0_gnn_bl"), "wr": arr("L0_gnn_Wr"), "br": row("L0_gnn_br"), "we": arr("L0_gnn_We"),
        "att": row("L0_gnn_att"), "bias_out0": row("L0_gnn_bias_out"), "gn_weight": row("L0_gnn_gn_weight"),
        "gn_bias": row("L0_gnn_gn_bias"), "gn_mean_scale": row("L0_gnn_gn_mean_scale"),
        "w1": arr("L1_gnn_W"), "att_src": row("L1_gnn_att_src"), "att_dst": row("L1_gnn_att_dst"), "bias1": row("L1_gnn_bias"),
    }
    nc = bacc.Bacc("TRN2", target_bir_lowering=False, num_devices=1)

    def given(name):
        a = data[name]
        return nc.dram_tensor("in_" + name, a.shape, mybir.dt.from_np(a.dtype), kind="ExternalInput").ap()

    io = Names()
    io.x = given("x")
    io.src_rows = given("src_rows")
    io.dst_rows = given("dst_rows")
    io.dst_lasts = given("dst_lasts")
    io.attr = given("attr")
    io.attrT = given("attrT")
    io.wl = given("wl")
    io.bl = given("bl")
    io.wr = given("wr")
    io.br = given("br")
    io.we = given("we")
    io.att = given("att")
    io.bias_out0 = given("bias_out0")
    io.gn_weight = given("gn_weight")
    io.gn_bias = given("gn_bias")
    io.gn_mean_scale = given("gn_mean_scale")
    io.w1 = given("w1")
    io.att_src = given("att_src")
    io.att_dst = given("att_dst")
    io.bias1 = given("bias1")
    io.out = nc.dram_tensor("out", (NODES, D), F32, kind="ExternalOutput").ap()
    program(nc, io)
    r = run(nc, [{"in_" + name: a for name, a in data.items()}], core_ids=[0])
    return r.results[0]["out"]
```
